# Optimizing a Trainium2 kernel written in Bass

```python
import numpy as np
import jax
import jax.numpy as jnp

def _softmax(x, axis=-1):
    return jax.nn.softmax(x, axis=axis)

def _gelu(x):
    return jax.nn.gelu(x, approximate=True)

def _silu(x):
    return jax.nn.silu(x)

def _sigmoid(x):
    return jax.nn.sigmoid(x)

def _layernorm(x, axis=-1, eps=1e-05):
    m = jnp.mean(x, axis=axis, keepdims=True)
    v = jnp.var(x, axis=axis, keepdims=True)
    return (x - m) / jnp.sqrt(v + eps)

def _scatter_add(tgt, idx, src, axis=0):
    return tgt.at[idx].add(src)

def _segment_sum(src, seg, n):
    return jax.ops.segment_sum(src, seg, n)
kernel_name = 'mk_flamingo_gated_d2_seqx_r8_798c54'

def setup_inputs(seed: int=0):
    np.random.seed(seed)
    _w = jnp.asarray

    def _rec_inputs():
        import jax
        import jax.numpy as jnp
        _rk = jax.random.key(seed)
        x = 2.818e-05 + 1 * jax.random.normal(jax.random.fold_in(_rk, 1), (4, 256, 256), jnp.float32)
        _lenS = 256 - jax.random.randint(jax.random.fold_in(_rk, 7), (4,), 0, max(1, 256 // 4) + 1, jnp.int32)
        _lenS2 = 256 - jax.random.randint(jax.random.fold_in(_rk, 8), (4,), 0, max(1, 256 // 4) + 1, jnp.int32)
        _ctx_1024P = jax.random.normal(jax.random.fold_in(_rk, 11), (4, 16, 128), jnp.float32)
        _ctx_1024c = jax.random.dirichlet(jax.random.fold_in(_rk, 511), 0.3 * jnp.ones((16,), jnp.float32), (4, 256))
        _ctx_1024t = jnp.einsum('bsk,bkd->bsd', _ctx_1024c, _ctx_1024P)
        _ctx_1024t = _ctx_1024t * jax.lax.rsqrt(jnp.mean(jnp.square(_ctx_1024t)) + 1e-12) * 0.953939
        ctx_1024 = 7.22013e-05 + 1.00017 * (_ctx_1024t + 0.3 * jax.random.normal(jax.random.fold_in(_rk, 611), (4, 256, 128), jnp.float32))
        _g = jax.random.normal(jax.random.fold_in(_rk, 9001), (2, 2), jnp.float32)
        _g = jnp.sign(_g) * jnp.maximum(jnp.abs(_g), 1.0) + (_g == 0) * 1.0
        g_xattn = _g[0]
        g_ffn = _g[1]
        return (x, ctx_1024, g_xattn, g_ffn)
    x, ctx_1024, g_xattn, g_ffn = _rec_inputs()

    def _L0_xattn_setup():
        import jax, jax.numpy as jnp
        import numpy as np
        B_, L_, D_MODEL = (4, 256, 128)
        D_STATE, D_CONV, EXPAND = (16, 4, 2)
        D_INNER = EXPAND * D_MODEL
        DT_RANK = (D_MODEL + 15) // 16

        def silu(x):
            return x * jax.nn.sigmoid(x)
        key = jax.random.key(seed)
        ks = jax.random.split(key, 10)
        f32 = jnp.float32
        hidden_states = jax.random.normal(ks[0], (B_, L_, D_MODEL), dtype=f32)
        z = jax.random.normal(ks[1], (B_, D_INNER, L_), dtype=f32)
        in_proj_w = jax.random.normal(ks[2], (D_INNER, D_MODEL), dtype=f32) * 0.02
        conv_w = jax.random.normal(ks[3], (D_INNER, 1, D_CONV), dtype=f32) * 0.1
        conv_b = jax.random.normal(ks[4], (D_INNER,), dtype=f32) * 0.02
        x_proj_w = jax.random.normal(ks[5], (DT_RANK + 2 * D_STATE, D_INNER), dtype=f32) * 0.02
        dt_proj_w = jax.random.uniform(ks[6], (D_INNER, DT_RANK), dtype=f32, minval=-DT_RANK ** (-0.5), maxval=DT_RANK ** (-0.5))
        dt = jnp.exp(jax.random.uniform(ks[7], (D_INNER,), dtype=f32, minval=np.log(0.001), maxval=np.log(0.1)))
        dt_proj_b = jnp.log(jnp.expm1(dt))
        A_log = jnp.log(jnp.broadcast_to(jnp.arange(1, D_STATE + 1, dtype=f32), (D_INNER, D_STATE)))
        D = jnp.ones((D_INNER,), f32)
        return {'hidden_states': hidden_states, 'z': z, 'in_proj_w': in_proj_w, 'conv_w': conv_w, 'conv_b': conv_b, 'x_proj_w': x_proj_w, 'dt_proj_w': dt_proj_w, 'dt_proj_b': dt_proj_b, 'A_log': A_log, 'D': D}
    _L0_xattn_all = _L0_xattn_setup()
    _L0_xattn_in = {k: v for k, v in _L0_xattn_all.items() if k in ('in_proj_w', 'conv_w', 'conv_b', 'x_proj_w', 'dt_proj_w', 'dt_proj_b', 'A_log', 'D')}
    del _L0_xattn_all

    def _L0_ffn_setup():
        import jax, jax.numpy as jnp
        import numpy as np
        B, S, H, I = (1, 64, 256, 768)

        def _quantized_matmul(x, w, scale):
            wq = w.astype(jnp.float8_e4m3fn).astype(x.dtype)
            y = jnp.einsum('bsi,io->bso', x, wq)
            return y * scale
        key = jax.random.key(seed)
        ks = jax.random.split(key, 7)
        return {'x': jax.random.normal(ks[0], (B, S, H), dtype=jnp.float32), 'gate_w': jax.random.normal(ks[1], (H, I), dtype=jnp.float32) * 0.02, 'up_w': jax.random.normal(ks[2], (H, I), dtype=jnp.float32) * 0.02, 'down_w': jax.random.normal(ks[3], (I, H), dtype=jnp.float32) * 0.02, 'gate_scale': jax.random.uniform(ks[4], (I,), dtype=jnp.float32, minval=0.5, maxval=1.5), 'up_scale': jax.random.uniform(ks[5], (I,), dtype=jnp.float32, minval=0.5, maxval=1.5), 'down_scale': jax.random.uniform(ks[6], (H,), dtype=jnp.float32, minval=0.5, maxval=1.5)}
    _L0_ffn_all = _L0_ffn_setup()
    _L0_ffn_in = {k: v for k, v in _L0_ffn_all.items() if k in ('gate_w', 'up_w', 'down_w', 'gate_scale', 'up_scale', 'down_scale')}
    del _L0_ffn_all

    def _L1_xattn_setup():
        import jax, jax.numpy as jnp
        import numpy as np
        B, S1, S2, DCA = (2, 256, 128, 16)
        QDIM, KDIM, H = (256, 128, 16)
        HD = QDIM // H
        SCALE = HD ** (-0.5)
        EPS = 1e-06
        DCA_WEIGHT = 1.0

        def _ln(t, w, b):
            m = jnp.mean(t, axis=-1, keepdims=True)
            v = jnp.var(t, axis=-1, keepdims=True)
            return (t - m) * jax.lax.rsqrt(v + EPS) * w + b

        def _attn(q, k, v):
            s = jnp.einsum('bhqd,bhkd->bhqk', q, k) * SCALE
            p = jax.nn.softmax(s, axis=-1)
            return jnp.einsum('bhqk,bhkd->bhqd', p, v)
        key = jax.random.key(seed)
        ks = jax.random.split(key, 8)
        w = lambda k, shape: jax.random.normal(k, shape, jnp.float32) * 0.02
        return {'x': jax.random.normal(ks[0], (B, S1, QDIM), jnp.float32), 'y': jax.random.normal(ks[1], (B, S2 + DCA, KDIM), jnp.float32), 'Wq': w(ks[2], (QDIM, QDIM)), 'bq': jnp.zeros((QDIM,), jnp.float32), 'Wk': w(ks[3], (KDIM, QDIM)), 'bk': jnp.zeros((QDIM,), jnp.float32), 'Wv': w(ks[4], (KDIM, QDIM)), 'bv': jnp.zeros((QDIM,), jnp.float32), 'Wkv_dca': w(ks[5], (KDIM, 2 * QDIM)), 'bkv_dca': jnp.zeros((2 * QDIM,), jnp.float32), 'qn_w': jnp.ones((HD,), jnp.float32), 'qn_b': jnp.zeros((HD,), jnp.float32), 'kn_w': jnp.ones((HD,), jnp.float32), 'kn_b': jnp.zeros((HD,), jnp.float32), 'kn_dca_w': jnp.ones((HD,), jnp.float32), 'kn_dca_b': jnp.zeros((HD,), jnp.float32), 'Wo': w(ks[6], (QDIM, QDIM)), 'bo': jnp.zeros((QDIM,), jnp.float32)}
    _L1_xattn_all = _L1_xattn_setup()
    _L1_xattn_in = {k: v for k, v in _L1_xattn_all.items() if k in ('Wq', 'bq', 'Wk', 'bk', 'Wv', 'bv', 'Wkv_dca', 'bkv_dca', 'qn_w', 'qn_b', 'kn_w', 'kn_b', 'kn_dca_w', 'kn_dca_b', 'Wo', 'bo')}
    del _L1_xattn_all

    def _L1_ffn_setup():
        import jax, jax.numpy as jnp
        import numpy as np
        E = 8
        K = 2
        DIM = 256
        INTER = 176
        N_SHARED = 2
        STD = 0.02
        key = jax.random.key(seed)
        ks = jax.random.split(key, 9)
        B, S = (2, 256)
        return {'x': jax.random.normal(ks[0], (B, S, DIM), dtype=jnp.float32), 'gate_w': jax.random.normal(ks[1], (E, DIM), dtype=jnp.float32) * STD, 'router_bias': jnp.zeros((E,), dtype=jnp.float32), 'W1': jax.random.normal(ks[2], (E, DIM, INTER), dtype=jnp.float32) * STD, 'W3': jax.random.normal(ks[3], (E, DIM, INTER), dtype=jnp.float32) * STD, 'W2': jax.random.normal(ks[4], (E, INTER, DIM), dtype=jnp.float32) * STD, 'sw1': jax.random.normal(ks[5], (N_SHARED * INTER, DIM), dtype=jnp.float32) * STD, 'sw3': jax.random.normal(ks[6], (N_SHARED * INTER, DIM), dtype=jnp.float32) * STD, 'sw2': jax.random.normal(ks[7], (DIM, N_SHARED * INTER), dtype=jnp.float32) * STD}
    _L1_ffn_all = _L1_ffn_setup()
    _L1_ffn_in = {k: v for k, v in _L1_ffn_all.items() if k in ('gate_w', 'router_bias', 'W1', 'W3', 'W2', 'sw1', 'sw3', 'sw2')}
    del _L1_ffn_all
    return {'x': x, 'ctx_1024': ctx_1024, 'g_xattn': g_xattn, 'g_ffn': g_ffn, 'L0_xattn_in_proj_w': _L0_xattn_in['in_proj_w'], 'L0_xattn_conv_w': _L0_xattn_in['conv_w'], 'L0_xattn_conv_b': _L0_xattn_in['conv_b'], 'L0_xattn_x_proj_w': _L0_xattn_in['x_proj_w'], 'L0_xattn_dt_proj_w': _L0_xattn_in['dt_proj_w'], 'L0_xattn_dt_proj_b': _L0_xattn_in['dt_proj_b'], 'L0_xattn_A_log': _L0_xattn_in['A_log'], 'L0_xattn_D': _L0_xattn_in['D'], 'L0_ffn_gate_w': _L0_ffn_in['gate_w'], 'L0_ffn_up_w': _L0_ffn_in['up_w'], 'L0_ffn_down_w': _L0_ffn_in['down_w'], 'L0_ffn_gate_scale': _L0_ffn_in['gate_scale'], 'L0_ffn_up_scale': _L0_ffn_in['up_scale'], 'L0_ffn_down_scale': _L0_ffn_in['down_scale'], 'L1_xattn_Wq': _L1_xattn_in['Wq'], 'L1_xattn_bq': _L1_xattn_in['bq'], 'L1_xattn_Wk': _L1_xattn_in['Wk'], 'L1_xattn_bk': _L1_xattn_in['bk'], 'L1_xattn_Wv': _L1_xattn_in['Wv'], 'L1_xattn_bv': _L1_xattn_in['bv'], 'L1_xattn_Wkv_dca': _L1_xattn_in['Wkv_dca'], 'L1_xattn_bkv_dca': _L1_xattn_in['bkv_dca'], 'L1_xattn_qn_w': _L1_xattn_in['qn_w'], 'L1_xattn_qn_b': _L1_xattn_in['qn_b'], 'L1_xattn_kn_w': _L1_xattn_in['kn_w'], 'L1_xattn_kn_b': _L1_xattn_in['kn_b'], 'L1_xattn_kn_dca_w': _L1_xattn_in['kn_dca_w'], 'L1_xattn_kn_dca_b': _L1_xattn_in['kn_dca_b'], 'L1_xattn_Wo': _L1_xattn_in['Wo'], 'L1_xattn_bo': _L1_xattn_in['bo'], 'L1_ffn_gate_w': _L1_ffn_in['gate_w'], 'L1_ffn_router_bias': _L1_ffn_in['router_bias'], 'L1_ffn_W1': _L1_ffn_in['W1'], 'L1_ffn_W3': _L1_ffn_in['W3'], 'L1_ffn_W2': _L1_ffn_in['W2'], 'L1_ffn_sw1': _L1_ffn_in['sw1'], 'L1_ffn_sw3': _L1_ffn_in['sw3'], 'L1_ffn_sw2': _L1_ffn_in['sw2']}

def reference(x, ctx_1024, g_xattn, g_ffn, L0_xattn_in_proj_w, L0_xattn_conv_w, L0_xattn_conv_b, L0_xattn_x_proj_w, L0_xattn_dt_proj_w, L0_xattn_dt_proj_b, L0_xattn_A_log, L0_xattn_D, L0_ffn_gate_w, L0_ffn_up_w, L0_ffn_down_w, L0_ffn_gate_scale, L0_ffn_up_scale, L0_ffn_down_scale, L1_xattn_Wq, L1_xattn_bq, L1_xattn_Wk, L1_xattn_bk, L1_xattn_Wv, L1_xattn_bv, L1_xattn_Wkv_dca, L1_xattn_bkv_dca, L1_xattn_qn_w, L1_xattn_qn_b, L1_xattn_kn_w, L1_xattn_kn_b, L1_xattn_kn_dca_w, L1_xattn_kn_dca_b, L1_xattn_Wo, L1_xattn_bo, L1_ffn_gate_w, L1_ffn_router_bias, L1_ffn_W1, L1_ffn_W3, L1_ffn_W2, L1_ffn_sw1, L1_ffn_sw3, L1_ffn_sw2):
    import jax
    import jax.numpy as jnp

    def _L0_xattn_ref(hidden_states, z, in_proj_w, conv_w, conv_b, x_proj_w, dt_proj_w, dt_proj_b, A_log, D):
        import jax, jax.numpy as jnp
        import numpy as np
        B_, L_, D_MODEL = (4, 256, 128)
        D_STATE, D_CONV, EXPAND = (16, 4, 2)
        D_INNER = EXPAND * D_MODEL
        DT_RANK = (D_MODEL + 15) // 16

        def silu(x):
            return x * jax.nn.sigmoid(x)
        Bsz, L, _ = hidden_states.shape
        d_inner, _, d_conv = conv_w.shape
        dt_rank = dt_proj_w.shape[1]
        d_state = A_log.shape[1]
        x = jnp.einsum('bld,ed->bel', hidden_states, in_proj_w)
        xc = jax.lax.conv_general_dilated(x, conv_w, window_strides=(1,), padding=[(d_conv - 1, 0)], feature_group_count=d_inner, dimension_numbers=('NCH', 'OIH', 'NCH'))
        x = silu(xc + conv_b[None, :, None])
        x_dbl = jnp.einsum('bdl,ed->bel', x, x_proj_w)
        dt_low, Bm, Cm = jnp.split(x_dbl, [dt_rank, dt_rank + d_state], axis=1)
        dt = jnp.einsum('brl,dr->bdl', dt_low, dt_proj_w)
        dt = jax.nn.softplus(dt + dt_proj_b[None, :, None])
        A = -jnp.exp(A_log)
        dt_t = jnp.moveaxis(dt, -1, 0)
        B_t = jnp.moveaxis(Bm, -1, 0)
        C_t = jnp.moveaxis(Cm, -1, 0)
        u_t = jnp.moveaxis(x, -1, 0)

        def step(state, inp):
            d, b, c, u = inp
            dA = jnp.exp(d[..., None] * A)
            state = state * dA + (d * u)[..., None] * b[:, None, :]
            y = jnp.einsum('bdn,bn->bd', state, c)
            return (state, y)
        state0 = jnp.zeros((Bsz, d_inner, d_state), x.dtype)
        _, ys = jax.lax.scan(step, state0, (dt_t, B_t, C_t, u_t))
        y = jnp.moveaxis(ys, 0, 2)
        y = y + D[None, :, None] * x
        y = y * silu(z)
        return jnp.swapaxes(y, 1, 2)

    def _L0_ffn_ref(x, gate_w, up_w, down_w, gate_scale, up_scale, down_scale):
        import jax, jax.numpy as jnp
        import numpy as np
        B, S, H, I = (1, 64, 256, 768)

        def _quantized_matmul(x, w, scale):
            wq = w.astype(jnp.float8_e4m3fn).astype(x.dtype)
            y = jnp.einsum('bsi,io->bso', x, wq)
            return y * scale
        gate = jax.nn.silu(_quantized_matmul(x, gate_w, gate_scale))
        up = _quantized_matmul(x, up_w, up_scale)
        fuse = gate * up
        return _quantized_matmul(fuse, down_w, down_scale)

    def _L1_xattn_ref(x, y, Wq, bq, Wk, bk, Wv, bv, Wkv_dca, bkv_dca, qn_w, qn_b, kn_w, kn_b, kn_dca_w, kn_dca_b, Wo, bo):
        import jax, jax.numpy as jnp
        import numpy as np
        B, S1, S2, DCA = (2, 256, 128, 16)
        QDIM, KDIM, H = (256, 128, 16)
        HD = QDIM // H
        SCALE = HD ** (-0.5)
        EPS = 1e-06
        DCA_WEIGHT = 1.0

        def _ln(t, w, b):
            m = jnp.mean(t, axis=-1, keepdims=True)
            v = jnp.var(t, axis=-1, keepdims=True)
            return (t - m) * jax.lax.rsqrt(v + EPS) * w + b

        def _attn(q, k, v):
            s = jnp.einsum('bhqd,bhkd->bhqk', q, k) * SCALE
            p = jax.nn.softmax(s, axis=-1)
            return jnp.einsum('bhqk,bhkd->bhqd', p, v)
        b, s1, _ = x.shape
        y_dca = y[:, -DCA:, :]
        y_main = y[:, :-DCA, :]
        kv_dca = (y_dca @ Wkv_dca + bkv_dca).reshape(b, DCA, 2, H, HD)
        k_dca = _ln(kv_dca[:, :, 0], kn_dca_w, kn_dca_b)
        v_dca = kv_dca[:, :, 1]
        s2 = y_main.shape[1]
        q = _ln((x @ Wq + bq).reshape(b, s1, H, HD), qn_w, qn_b)
        kv = jnp.concatenate([y_main @ Wk + bk, y_main @ Wv + bv], axis=-1)
        kv = kv.reshape(b, s2, H, 2 * HD)
        k = _ln(kv[..., :HD], kn_w, kn_b)
        v = kv[..., HD:]
        qT = q.transpose(0, 2, 1, 3)
        ctx = _attn(qT, k.transpose(0, 2, 1, 3), v.transpose(0, 2, 1, 3))
        ctx = ctx.transpose(0, 2, 1, 3).reshape(b, s1, QDIM)
        ctx_dca = _attn(qT, k_dca.transpose(0, 2, 1, 3), v_dca.transpose(0, 2, 1, 3))
        ctx_dca = ctx_dca.transpose(0, 2, 1, 3).reshape(b, s1, QDIM)
        ctx = ctx + DCA_WEIGHT * ctx_dca
        return ctx @ Wo + bo

    def _L1_ffn_ref(x, gate_w, router_bias, W1, W3, W2, sw1, sw3, sw2):
        import jax, jax.numpy as jnp
        import numpy as np
        E = 8
        K = 2
        DIM = 256
        INTER = 176
        N_SHARED = 2
        STD = 0.02
        B, S, D = x.shape
        X = x.reshape(-1, D)
        T = X.shape[0]
        logits = jnp.einsum('td,ed->te', X, gate_w)
        scores = jax.nn.sigmoid(logits)
        sel = scores + router_bias[None, :]
        _, idx = jax.lax.top_k(sel, K)
        w = jnp.take_along_axis(scores, idx, axis=1)
        w = w / jnp.clip(jnp.sum(w, axis=-1, keepdims=True), 1e-12)
        gate_full = jnp.zeros((T, E), dtype=w.dtype).at[jnp.arange(T)[:, None], idx].set(w)
        h1 = jnp.einsum('td,edh->eth', X, W1)
        h3 = jnp.einsum('td,edh->eth', X, W3)
        y = jnp.einsum('eth,ehd->etd', jax.nn.silu(h1) * h3, W2)
        out = jnp.einsum('etd,te->td', y, gate_full)
        shared = jnp.einsum('th,dh->td', jax.nn.silu(jnp.einsum('td,hd->th', X, sw1)) * jnp.einsum('td,hd->th', X, sw3), sw2)
        out = out + shared
        return out.reshape(B, S, D)
    x = x + jnp.tanh(g_xattn[0]) * _L0_xattn_ref(ctx_1024, _layernorm(x, axis=-1), L0_xattn_in_proj_w, L0_xattn_conv_w, L0_xattn_conv_b, L0_xattn_x_proj_w, L0_xattn_dt_proj_w, L0_xattn_dt_proj_b, L0_xattn_A_log, L0_xattn_D)
    x = x + jnp.tanh(g_ffn[0]) * _L0_ffn_ref(_layernorm(x, axis=-1), L0_ffn_gate_w, L0_ffn_up_w, L0_ffn_down_w, L0_ffn_gate_scale, L0_ffn_up_scale, L0_ffn_down_scale)
    x = x + jnp.tanh(g_xattn[1]) * _L1_xattn_ref(_layernorm(x, axis=-1), ctx_1024, L1_xattn_Wq, L1_xattn_bq, L1_xattn_Wk, L1_xattn_bk, L1_xattn_Wv, L1_xattn_bv, L1_xattn_Wkv_dca, L1_xattn_bkv_dca, L1_xattn_qn_w, L1_xattn_qn_b, L1_xattn_kn_w, L1_xattn_kn_b, L1_xattn_kn_dca_w, L1_xattn_kn_dca_b, L1_xattn_Wo, L1_xattn_bo)
    x = x + jnp.tanh(g_ffn[1]) * _L1_ffn_ref(_layernorm(x, axis=-1), L1_ffn_gate_w, L1_ffn_router_bias, L1_ffn_W1, L1_ffn_W3, L1_ffn_W2, L1_ffn_sw1, L1_ffn_sw3, L1_ffn_sw2)
    return x

_drawn_inputs = setup_inputs


def setup_inputs(seed=0):
    import zlib

    import numpy as np

    out = dict(_drawn_inputs(seed))
    spreads = {'g_ffn': (-1.0, 0.6),
     'L0_xattn_D': (1.0, 0.6),
     'L1_xattn_bq': (0.0, 2.0),
     'L1_xattn_bk': (0.0, 1.42),
     'L1_xattn_bv': (0.0, 1.501),
     'L1_xattn_bkv_dca': (0.0, 0.8),
     'L1_xattn_qn_w': (1.0, 0.6),
     'L1_xattn_qn_b': (0.0, 2.0),
     'L1_xattn_kn_w': (1.0, 0.6),
     'L1_xattn_kn_b': (0.0, 2.0),
     'L1_xattn_kn_dca_w': (1.0, 0.6),
     'L1_xattn_kn_dca_b': (0.0, 2.0),
     'L1_xattn_bo': (0.0, 0.639),
     'L1_ffn_router_bias': (0.0, 0.8)}
    factors = {'L0_xattn_in_proj_w': 5.649,
     'L0_xattn_conv_w': 5.894,
     'L0_xattn_conv_b': 8.0,
     'L0_xattn_x_proj_w': 8.0,
     'L0_xattn_dt_proj_w': 8.0,
     'L0_xattn_dt_proj_b': 8.0,
     'L0_xattn_A_log': 8.0,
     'L0_ffn_gate_scale': 7.023,
     'L0_ffn_up_scale': 8.0,
     'L0_ffn_down_scale': 7.89,
     'L1_ffn_gate_w': 8.0,
     'L1_ffn_W1': 7.037,
     'L1_ffn_W3': 6.969,
     'L1_ffn_W2': 6.95,
     'L1_ffn_sw1': 3.512,
     'L1_ffn_sw3': 3.482,
     'L1_ffn_sw2': 3.491,
     'L1_xattn_Wq': 7.723,
     'L1_xattn_Wk': 7.422,
     'L1_xattn_Wv': 5.175,
     'L1_xattn_Wkv_dca': 5.233,
     'L1_xattn_Wo': 3.857}
    for name, (base, spread) in spreads.items():
        noise = np.random.default_rng([zlib.crc32(name.encode()), seed]).standard_normal(out[name].shape)
        drawn = base * np.exp(spread * noise) if base else spread * noise
        out[name] = jnp.asarray(drawn.astype(out[name].dtype))
    for name, factor in factors.items():
        out[name] = (out[name] * factor).astype(out[name].dtype)
    return out
```

```python
from contextlib import ExitStack

import concourse.bass as bass
from concourse import mybir

P = 128
ALU = mybir.AluOpType
ACT = mybir.ActivationFunctionType
F32 = mybir.dt.float32
F32R = mybir.dt.float32r
F8 = mybir.dt.float8e4
U32 = mybir.dt.uint32
AX_X = mybir.AxisListType.X

B, L, D, DC = 4, 256, 256, 128
T2 = L // P
K2 = D // P
NS, DTR, TAPS = 16, 8, 4
FF = 768
MF = FF // P
H, HD = 16, 16
DCA = 16
MAIN = L - DCA
E, INTER, SHARED = 8, 176, 352
HID = E * INTER + SHARED
MM = -(-HID // P)
MG = E * INTER // P
HP = H // 2
LN_EPS, QK_EPS = 1e-5, 1e-6
BCR = 2 * NS
XR = 104

V_CW, V_CB, V_DTB, V_AL, V_D, V_GS, V_US = 0, 8, 10, 12, 44, 46, 52
V_MM, V_N = 58, 60
R_DS, R_BQ, R_BO, R_QW, R_QB, R_RB, R_KW, R_KB, R_G, R_KM, R_TR = 0, 256, 512, 768, 784, 800, 808, 840, 872, 876, 884
R_N = R_TR + E * E

PER = dict(
    zstat=4, zvar=1, zrstd=1, zhat=2, ztanh=1, zg=1,
    xi=1, xpad=1, conv_step=6, conv=2, conv_tanh=1, u=1, xdbl=1, bc_hi=1, bc_lo=2,
    dt_pre=1, sp_abs=2, sp_t=1, sp_ln=1, sp_relu=2, sp_step=6, dt=1, du=1,
    bc=NS, c_sb=NS, dA=2 * NS, dbu=NS, h=NS, p=NS, y_red=NS, ys=2, yT=1, yz=1, x1=1,
    kv_ps=1, kv=2, vst=3, kstep=6, kvar=1, krstd=1, kstack=5, kT_ps=2, kT=2,
    lstat=12, lvar=3, lrstd=3, xh=6, xT_ps=3, xT=2, x_hi=2, x_lo=2,
    gu=MF, g_tanh=MF, g_a=MF, h_ff=MF, down=1, dsc=1, x2=1,
    q_ps=1, q=1, qstep=6, qvar=1, qrstd=1, qstack=4, qT_ps=4, qT=4, s_ps=8, mx=16, mstack=2,
    st_ps=H, prob=H, pv=HP, o_sb=HP, oT_ps=HP, o_step=2 * HP, ctok=HP,
    cT_ps=1, cT=1, wo_ps=1, xbo=1, x3=1,
    lg=1, lg_tanh=1, r_step=12, gates=2, gT_ps=1, gT=1,
    h13=MM, y2_part=MM - 1, k_m=1, q_hi2=1, m_tanh=MM, m_a=MM, m_b=MG, hg=MM, y2=1, xo=1,
)
ONCE = ["early", "later", "ident_r", "ones_set", "zeros_set", "act_step", "pool_step", "setup", "wdt_part", "raw_hi", "raw_lo", "q_clip", "q_big", "q_sum", "q_out"]


def build(nc, x, ctxT, w_in, w_xp, w_dt, w_gu, w_dn, w_q, w_kv, w_kvd, w_o, w_gate, w13, w2, kvb, vecs, rows, gsel, cst, out):
    with ExitStack() as es:
        def sb(name, shape, dt=F32):
            return es.enter_context(nc.sbuf_tensor(name, shape, dt))

        cident = sb("cident", [P, P + BCR])
        ident = cident[:, 0:P]
        identR = sb("identR", [P, P], F32R)
        vec = sb("vec", [P, V_N])
        row = sb("row", [P, R_N])
        kv_bias = sb("kv_bias", [P, T2, 2 * D])
        win = sb("win", [DC, 2 * P])
        wxp = sb("wxp", [P, 2, XR])
        small = sb("small", [P, MG * P + BCR], F32R)
        gselR = small[0:2 * E, 0:MG * P].rearrange("p (m c) -> p m c", m=MG)
        wdt_hi = small[:, 0:2 * P]
        wdt_lo = small[:, 2 * P:4 * P]
        selBC = small[0:2 * BCR, MG * P:MG * P + BCR]
        wgu = sb("wgu", [P, MF, K2, 2, P], F32R)
        wdn = sb("wdn", [P, MF, D])
        wq = sb("wq", [P, K2, D])
        wkv = sb("wkv", [DC, 2 * D])
        wkvd = sb("wkvd", [DC, 2 * D])
        wo = sb("wo", [P, K2, D])
        wgate = sb("wgate", [P, K2, E])
        w13_hi = sb("w13_hi", [P, MM, K2, 2, P], F32R)
        w13_lo = sb("w13_lo", [P, MM, K2, 2, P], F32R)
        w2s = sb("w2s", [P, MM, D])
        negA = sb("negA", [P, 2, NS])
        halfD = sb("halfD", [P, 2])
        gsu = sb("gsu", [P, MF])
        halfgs = sb("halfgs", [P, MF])
        tg = sb("tg", [P, 4])
        tgh = sb("tgh", [P, 1])
        dsb = row[:, R_DS:R_DS + D]
        gbo = row[:, R_BO:R_BO + D]
        qwb = row[:, R_QW:R_QW + 2 * HD].rearrange("p (a c) -> p a c", a=2)
        mhalf = sb("mhalf", [P, 2 * H])

        xin = sb("xin", [P, T2, D])
        ctx = sb("ctx", [DC, L])
        zst = sb("zst", [P, T2, 6])
        zmv = sb("zmv", [P, T2, 2])
        zv = sb("zv", [P, T2])
        zr = sb("zr", [P, T2])
        zg = sb("zg", [P, T2, D])
        xpad = sb("xpad", [P, 2, TAPS - 1 + L])
        cv = sb("cv", [P, 2, L])
        u2 = sb("u2", [P, 2, L])
        stack = sb("stack", [P, L], F32R)
        dt_sb = sb("dt_sb", [P, 2, L])
        du = sb("du", [P, 2, L])
        zh, zt = dt_sb, du
        dA = sb("dA", [P, 2, 2, L])
        hb = sb("hb", [P, 3, 2, L])
        cs = sb("cs", [P, 2, L])
        sp_x = hb[:, 0]
        sp_l = hb[:, 1]
        sp_q = hb[:, 2]
        sp_r = zt
        sp_m = zh[:, :, :].bitcast(U32)
        xa = sb("xa", [P, T2, D])

        ctxR = sb("ctxR", [DC, 3, P])
        xb = sb("xb", [P, T2, D])
        work = sb("work", [P, 10, L])
        xh = sb("xh", [P, T2, D])
        lst = sb("lst", [P, T2, 6])
        lmv = sb("lmv", [P, T2, 2])
        lv = sb("lv", [P, T2])
        lr = sb("lr", [P, T2])
        xT = sb("xT", [P, K2, L])
        xhi = sb("xhi", [P, K2, L], F32R)
        xlo = sb("xlo", [P, K2, L], F32R)
        kvs = sb("kvs", [P, T2, 2 * D])
        VW = 2 * (HD + 1)
        vst = sb("vst", [P, T2, H * VW + 64 - VW])
        vsth = [vst[:, t, 0:H * VW].rearrange("p (h c) -> p h c", h=H) for t in range(T2)]
        qk = sb("qk", [P, T2, H, HD])
        sq = xh[:, :, :].rearrange("p t (h c) -> p t h c", h=H)
        hs = sb("hs", [P, 4, T2 * H])
        st = sb("st", [P, T2, H, 64], F32R)
        kT = sb("kT", [P, HP, L], F32R)
        qT = sb("qT", [P, HP, L], F32R)
        mx = sb("mx", [P, T2, H, 2])

        ctok = qk
        rec = sb("rec", [P, 4, 2])
        opr = sb("opr", [P, 4, 2, HD])
        rt = sb("rt", [P, 6, T2, E])
        rk = work[:, 9, :].rearrange("p (a t f) -> p a t f", a=2, t=T2)
        rs = sb("rs", [P, T2])
        gst = sb("gst", [P, T2, 2 * E], F32R)
        gT = sb("gT", [2 * E, L], F32R)
        xo = xT
        RAW = 2
        raw = sb("raw", [P, RAW, 512])
        f8 = sb("f8", [P, 3, 512], F8)

        ps = es.enter_context(nc.psum_tensor("ps", [P, 8, 512], F32))
        psR = ps[:, :, :].bitcast(F32R)

        sem = {name: es.enter_context(nc.semaphore(name)) for name in PER}
        once = {name: es.enter_context(nc.semaphore(name)) for name in ONCE}
        raw_in = [es.enter_context(nc.semaphore(f"raw_in{i}")) for i in range(RAW)]
        ctx_in = es.enter_context(nc.semaphore("ctx_in"))
        ctxR_in = es.enter_context(nc.semaphore("ctxR_in"))
        x_in = es.enter_context(nc.semaphore("x_in"))
        stored = es.enter_context(nc.semaphore("stored"))

        def at(name, b, n):
            return sem[name], b * PER[name] + n + 1

        def bank(i, w=512, n=1):
            return ps[:, i:i + n, :].rearrange("p a b -> p (a b)")[:, 0:w]

        chunks = [("gu", m) for m in range(MF)] + [("dn", c) for c in range(3)] + [("w13", m) for m in range(MM)]
        block = es.enter_context(nc.Block())

        QUANT = MF + 3

        def chunk_in(eng, i):
            eng.wait_ge(raw_in[i % RAW], 16 * (i // RAW + 1))

        EARLY = [(vec[:, :], vecs), (row[:, :], rows), (win[:, :], w_in), (wxp[:, :, :], w_xp), (cident[:, :], cst),
                 (work[:, 9, :], w_dt), (work[0:2 * E, 0:6, :].rearrange("p a b -> p (a b)")[:, 0:MG * P], gsel)]
        LATER = [(kv_bias[:, :, :], kvb), (wkv[:, :], w_kv), (wkvd[:, :], w_kvd), (wgate[:, :, :], w_gate),
                 (wq[:, :, :], w_q), (wo[:, :, :], w_o), (w2s[:, :, :], w2)]
        ZEROED = 5
        qtmp = work[:, 0:2, :].rearrange("p a b -> p (a b)")
        b7x = ps[:, 7, :].rearrange("p (k c) -> p k c", k=2)

        def bankR(i, w, n):
            return psR[:, i:i + n, :].rearrange("p a b -> p (a b)")[:, 0:w]

        T = dict(kv=0, kstack=12, kT=13, ln0=14, xT0=18, ffn=20, down=29, x2=31, q=35, qT=45, scores=48, m=57, heads=60,
                 wo=78, ln2=80, xT2=83, router=85, moe=94, out=127, quant=1, raw=30)
        T.update({"in": 0, "xproj": 8, "dt": 11, "scan": 22, "y": 124})
        DT = dict(ffn=1.5, scores=1, heads=0.8, moe=2.3, scan=5.2, quant=3, raw=1.5)

        def together(*parts):
            steps = [[next(p), i, p] for i, p in enumerate(parts)]
            while steps:
                step = min(steps, key=lambda s: s[:2])
                step[0] = next(step[2], None)
                if step[0] is None:
                    steps.remove(step)

        def schedule(mamba, rest, *weights):
            together(mamba(0), *(w() for w in weights))
            for b in range(1, B):
                together(rest(b - 1), mamba(b))
            together(rest(B - 1))

        @block.sync
        def _(sp):
            def load_ctx(b):
                sp.dma_start(ctx[:, :], ctxT[b]).then_inc(ctx_in, 16)

            def load_x(b):
                sp.dma_start(xin[:, :, :], x[b].rearrange("(t p) d -> p t d", p=P)).then_inc(x_in, 16)

            def load_ctxR(b):
                sp.dma_start(ctxR[:, 0, :], ctxT[b, :, 0:P]).then_inc(ctxR_in, 16)
                sp.dma_start(ctxR[:, 1, 0:MAIN - P], ctxT[b, :, P:MAIN]).then_inc(ctxR_in, 16)
                sp.dma_start(ctxR[:, 2, MAIN - P:P], ctxT[b, :, MAIN:L]).then_inc(ctxR_in, 16)

            def store(b):
                sp.wait_ge(*at("xo", b, 1))
                sp.dma_start(out[b].rearrange("(t p) d -> p t d", p=P), xo[:, :, :]).then_inc(stored, 16)

            load_ctx(0)
            for dst, src in EARLY:
                sp.dma_start(dst, src).then_inc(once["early"], 16)
            load_x(0)
            sp.wait_ge(once["zeros_set"], ZEROED)
            load_ctxR(0)
            for i, (kind, c) in enumerate(chunks):
                if i == QUANT:
                    for dst, src in LATER:
                        sp.dma_start(dst, src).then_inc(once["later"], 16)
                if RAW <= i:
                    if i - RAW < QUANT:
                        sp.wait_ge(once["q_clip"], i - RAW + 1)
                        sp.wait_ge(once["q_big"], 2 * (i - RAW + 1))
                    else:
                        sp.wait_ge(once["raw_lo"], i - RAW - QUANT + 1)
                src = w_gu[:, c] if kind == "gu" else w_dn[:, 512 * c:512 * c + 512] if kind == "dn" else w13[:, c]
                sp.dma_start(raw[:, i % RAW, :], src).then_inc(raw_in[i % RAW], 16)
            for b in range(B):
                if b + 1 < B:
                    sp.wait_ge(*at("xi", b, 1))
                    load_ctx(b + 1)
                    sp.wait_ge(*at("x1", b, 1))
                    load_x(b + 1)
                    sp.wait_ge(*at("kv_ps", b, 1))
                    load_ctxR(b + 1)
                store(b)
            sp.wait_ge(stored, 16 * B)

        @block.gpsimd
        def _(g):
            for name in PER:
                g.sem_inc(sem[name], 1)
            g.memset(ctxR[:, :, :], 0.0).then_inc(once["zeros_set"], 1)
            g.memset(xpad[:, :, :], 0.0).then_inc(once["zeros_set"], 1)
            g.memset(dA[:, :, :, :], 0.0).then_inc(once["zeros_set"], 1)
            g.memset(vst[:, :, :], 0.0).then_inc(once["zeros_set"], 1)
            g.memset(mhalf[:, :], -0.5).then_inc(once["ones_set"], 1)
            g.memset(st[:, :, :, :].bitcast(F32), 0.0).then_inc(once["zeros_set"], 1)
            g.wait_ge(once["early"], 16 * len(EARLY))
            g.wait_ge(once["zeros_set"], ZEROED)
            g.memset(vsth[0][:, :, HD:HD + 1], 1.0).then_inc(once["pool_step"], 1)
            for h in range(H):
                g.tensor_scalar(vsth[1][:, h, HD:HD + 1], vec[:, V_MM:V_MM + 1], 1.0, 0.0, ALU.mult, ALU.add).then_inc(once["pool_step"], 1)
                g.tensor_scalar(vsth[1][:, h, 2 * HD + 1:2 * HD + 2], vec[:, V_MM + 1:V_MM + 2], 1.0, 0.0, ALU.mult, ALU.add).then_inc(once["pool_step"], 1)

            def weights():
                for m in range(MM):
                    yield T["raw"] + DT["raw"] * m
                    i = QUANT + m
                    g.wait_ge(once["raw_hi"], m + 1)
                    g.tensor_tensor(w13_lo[:, m].rearrange("p k w c -> p (k w c)"), raw[:, i % RAW, :],
                                    w13_hi[:, m].rearrange("p k w c -> p (k w c)").bitcast(F32), ALU.subtract).then_inc(once["raw_lo"], 1)

            def rsqrt(b, var, n, src, dst, done, k, cols):
                g.wait_ge(*at(var, b, n))
                g.tensor_tensor(dst, src, mhalf[:, 0:cols], ALU.pow).then_inc(sem[done], 1)

            def mamba(b):
                yield T["in"]
                g.wait_ge(*at("zvar", b, 1))
                g.tensor_tensor(zr[:, :], zv[:, :], mhalf[:, 0:T2], ALU.pow).then_inc(sem["zrstd"], 1)
                for n in range(NS):
                    yield T["scan"] + DT["scan"] * n
                    g.wait_ge(*at("h", b, n + 1))
                    g.wait_ge(*at("c_sb", b, n + 1))
                    hn = hb[:, n % 3]
                    cb = cs[:, n % 2, :].rearrange("p (a l) -> p a l", a=1).to_broadcast([P, 2, L])
                    g.tensor_tensor(hn, hn, cb, ALU.mult).then_inc(sem["p"], 1)

            def rest(b):
                yield T["kv"]
                g.wait_ge(*at("kv", b, T2))
                g.wait_ge(*at("pv", b, 0))
                v = kvs[:, :, :].rearrange("p t (h c) -> p t h c", h=H)[:, :, :, HD:2 * HD]
                g.tensor_scalar(vsth[0][:, :, 0:HD], v[:, 0], 1.0, 0.0, ALU.mult, ALU.add).then_inc(sem["vst"], 1)
                g.tensor_scalar(vsth[1][:, :, 0:HD], v[:, 1], vec[:, V_MM:V_MM + 1], 0.0, ALU.mult, ALU.add).then_inc(sem["vst"], 1)
                g.tensor_scalar(vsth[1][:, :, HD + 1:2 * HD + 1], v[:, 1], vec[:, V_MM + 1:V_MM + 2], 0.0, ALU.mult, ALU.add).then_inc(sem["vst"], 1)
                g.wait_ge(*at("kvar", b, 1))
                g.tensor_tensor(hs[:, 3, :], hs[:, 2, :], mhalf[:, :], ALU.pow).then_inc(sem["krstd"], 1)
                yield T["ln0"]
                g.wait_ge(*at("lvar", b, 1))
                g.tensor_tensor(lr[:, :], lv[:, :], mhalf[:, 0:T2], ALU.pow).then_inc(sem["lrstd"], 1)
                yield T["x2"]
                g.wait_ge(*at("lvar", b, 2))
                g.tensor_tensor(lr[:, :], lv[:, :], mhalf[:, 0:T2], ALU.pow).then_inc(sem["lrstd"], 1)
                yield T["q"]
                g.wait_ge(*at("qvar", b, 1))
                g.tensor_tensor(hs[:, 3, :], hs[:, 2, :], mhalf[:, :], ALU.pow).then_inc(sem["qrstd"], 1)
                yield T["ln2"]
                g.wait_ge(*at("lvar", b, 3))
                g.tensor_tensor(lr[:, :], lv[:, :], mhalf[:, 0:T2], ALU.pow).then_inc(sem["lrstd"], 1)

            schedule(mamba, rest, weights)

        @block.scalar
        def _(a):
            a.wait_ge(once["early"], 16 * len(EARLY))
            al = vec[:, V_AL:V_AL + 2 * NS].rearrange("p (a n) -> p a n", a=2)
            a.activation(negA[:, :, :], al, ACT.Exp).then_inc(once["act_step"], 1)
            a.activation(tg[:, :], row[:, R_G:R_G + 4], ACT.Tanh).then_inc(once["act_step"], 1)
            a.activation(identR[:, :], ident, ACT.Copy).then_inc(once["ident_r"], 1)
            a.activation(selBC, cident[0:2 * BCR, P:P + BCR], ACT.Copy).then_inc(once["ident_r"], 1)
            a.activation(gselR, work[0:2 * E, 0:6, :].rearrange("p a b -> p (a b)")[:, 0:MG * P].rearrange("p (m c) -> p m c", m=MG), ACT.Copy).then_inc(once["ident_r"], 1)
            a.activation(wdt_hi[64:XR], work[64:XR, 9, :], ACT.Copy).then_inc(once["wdt_part"], 1)

            def weights():
                for m in range(MM):
                    yield T["raw"] + DT["raw"] * m
                    chunk_in(a, QUANT + m)
                    a.activation(w13_hi[:, m].rearrange("p k w c -> p (k w c)"), raw[:, (QUANT + m) % RAW, :], ACT.Copy).then_inc(once["raw_hi"], 1)

            def mamba(b):
                yield T["in"]
                a.wait_ge(*at("zhat", b, 2))
                a.wait_ge(*at("y_red", b, 0))
                a.activation(zt[:, :, :], zh[:, :, :], ACT.Tanh, scale=0.5).then_inc(sem["ztanh"], 1)
                a.wait_ge(*at("conv", b, 2))
                a.activation(u2[:, :, :], cv[:, :, :], ACT.Tanh, scale=0.5).then_inc(sem["conv_tanh"], 1)
                yield T["xproj"]
                a.wait_ge(*at("xdbl", b, 1))
                a.activation(stack[0:XR, :], ps[0:XR, 0, 0:L], ACT.Copy, scale=0.5).then_inc(sem["bc_hi"], 1)
                yield T["dt"]
                a.wait_ge(*at("dt_pre", b, 1))
                a.wait_ge(*at("y_red", b, 0))
                for e in range(2):
                    a.activation(sp_x[:, e, :], ps[:, 1, e * L:e * L + L], ACT.Abs, bias=vec[:, V_DTB + e:V_DTB + e + 1]).then_inc(sem["sp_abs"], 1)
                a.wait_ge(*at("sp_abs", b, 2))
                a.activation(sp_x, sp_x, ACT.Exp, scale=-1.0).then_inc(sem["sp_t"], 1)
                a.wait_ge(*at("sp_t", b, 1))
                a.activation(sp_l, sp_x, ACT.Ln, bias=1.0).then_inc(sem["sp_ln"], 1)
                a.wait_ge(*at("dt", b, 1))
                for n in range(NS):
                    yield T["scan"] + DT["scan"] * n
                    a.wait_ge(*at("bc", b, n + 1))
                    if n >= 2:
                        a.wait_ge(*at("p", b, n - 1))
                    a.activation(cs[:, n % 2, :], ps[:, n % 2, L:2 * L], ACT.Copy).then_inc(sem["c_sb"], 1)
                    if n >= 2:
                        a.wait_ge(*at("h", b, n - 1))
                    for e in range(2):
                        a.activation(dA[:, n % 2, e, 1:L], dt_sb[:, e, 1:L], ACT.Exp, scale=negA[:, e, n:n + 1]).then_inc(sem["dA"], 1)

            def rest(b):
                yield T["kT"]
                for t in range(T2):
                    a.wait_ge(*at("kT_ps", b, t + 1))
                    a.activation(kT[:, :, t * P:t * P + P], bankR(5 - 2 * t, 1024, 2).rearrange("p (j c) -> p j c", j=HP), ACT.Copy).then_inc(sem["kT"], 1)
                yield T["xT0"]
                a.wait_ge(*at("xT_ps", b, 1))
                a.activation(xhi[:, :, :], b7x, ACT.Copy).then_inc(sem["x_hi"], 1)
                for m in range(MF):
                    yield T["ffn"] + DT["ffn"] * m
                    a.wait_ge(*at("gu", b, m + 1))
                    if m >= 2:
                        a.wait_ge(*at("g_a", b, m - 1))
                    a.activation(work[:, m % 2, :], ps[:, 3 + m % 4, 0:L], ACT.Tanh, scale=halfgs[:, m:m + 1]).then_inc(sem["g_tanh"], 1)
                yield T["x2"]
                a.wait_ge(*at("xT_ps", b, 2))
                if b:
                    a.wait_ge(stored, b * 16)
                a.activation(xT[:, :, :], b7x, ACT.Copy).then_inc(sem["xT"], 1)
                for r in range(2):
                    for t in range(T2):
                        yield T["m"] if r else T["qT"]
                        a.wait_ge(*at("qT_ps", b, 2 * r + t + 1))
                        if r:
                            a.wait_ge(*at("s_ps", b, 8))
                        a.activation(qT[:, :, t * P:t * P + P], bankR(5 - 2 * t, 1024, 2).rearrange("p (j c) -> p j c", j=HP), ACT.Copy).then_inc(sem["qT"], 1)
                for h in range(H + 4):
                    yield T["heads"] + DT["heads"] * h
                    if h < H:
                        a.wait_ge(*at("st_ps", b, h + 1))
                        if h >= 4:
                            a.wait_ge(*at("pv", b, (h - 4) // 2 + 1))
                        slot = work[:, 2 * (h % 4):2 * (h % 4) + 2, :].rearrange("p a b -> p (a b)")
                        a.activation(slot, ps[:, 3 + h % 3, :], ACT.Exp).then_inc(sem["prob"], 1)
                    if h >= 4 and h % 2 == 0:
                        j = (h - 4) // 2
                        a.wait_ge(*at("pv", b, j + 1))
                        if j >= 2:
                            a.wait_ge(*at("oT_ps", b, j - 1))
                        a.activation(work[:, 8 + j % 2, :], ps[:, 6, 0:L], ACT.Copy).then_inc(sem["o_sb"], 1)
                yield T["wo"]
                a.wait_ge(*at("cT_ps", b, 1))
                a.activation(xT[:, :, :], ps[:, 3, :].rearrange("p (k c) -> p k c", k=K2), ACT.Copy).then_inc(sem["cT"], 1)
                yield T["xT2"]
                a.wait_ge(*at("xT_ps", b, 3))
                a.wait_ge(*at("wo_ps", b, 1))
                a.activation(xT[:, :, :], b7x, ACT.Copy).then_inc(sem["xT"], 1)
                a.activation(xhi[:, :, :], b7x, ACT.Copy).then_inc(sem["x_hi"], 1)
                yield T["router"]
                a.wait_ge(*at("lg", b, 1))
                a.activation(rt[:, 0], ps[:, 3, 0:T2 * E].rearrange("p (t e) -> p t e", t=T2), ACT.Tanh, scale=0.5).then_inc(sem["lg_tanh"], 1)
                a.wait_ge(*at("gT_ps", b, 1))
                a.activation(gT[:, :], psR[0:2 * E, 4, 0:L], ACT.Copy).then_inc(sem["gT"], 1)
                for m in range(MM):
                    yield T["moe"] + DT["moe"] * m
                    a.wait_ge(*at("h13", b, m + 1))
                    if m >= 2:
                        a.wait_ge(*at("m_a", b, m - 1))
                    a.activation(work[:, m % 2, :], ps[:, 3 + m % 3, 0:L], ACT.Tanh, scale=0.5).then_inc(sem["m_tanh"], 1)

            schedule(mamba, rest, weights)

        @block.vector
        def _(v):
            n_setup = 0

            def setup(i):
                nonlocal n_setup
                n_setup += 1
                i.then_inc(once["setup"], 1)
                v.wait_ge(once["setup"], n_setup)

            v.wait_ge(once["early"], 16 * len(EARLY))
            v.wait_ge(once["zeros_set"], ZEROED)
            v.wait_ge(once["act_step"], 2)
            v.wait_ge(once["wdt_part"], 1)
            setup(v.tensor_tensor(wdt_lo[64:XR], work[64:XR, 9, :], wdt_hi[64:XR].bitcast(F32), ALU.subtract))
            setup(v.tensor_scalar(negA[:, :, :], negA[:, :, :], -1.0, None, ALU.mult))
            setup(v.tensor_scalar(halfD[:, :], vec[:, V_D:V_D + 2], 0.5, None, ALU.mult))
            setup(v.tensor_scalar(tgh[:, :], tg[:, 0:1], 0.5, None, ALU.mult))
            setup(v.tensor_scalar(halfgs[:, :], vec[:, V_GS:V_GS + MF], 0.5, None, ALU.mult))
            setup(v.tensor_tensor(gsu[:, :], halfgs[:, :], vec[:, V_US:V_US + MF], ALU.mult))
            setup(v.tensor_scalar(dsb, dsb, tg[:, 2:3], None, ALU.mult))
            setup(v.tensor_scalar(gbo, gbo, tg[:, 1:2], None, ALU.mult))
            setup(v.tensor_scalar(qwb, qwb, HD ** -0.5, None, ALU.mult))

            def weights():
                for i in range(QUANT):
                    yield T["quant"] + DT["quant"] * i
                    kind, c = chunks[i]
                    chunk_in(v, i)
                    r = raw[:, i % RAW, :]
                    if i:
                        v.wait_ge(once["q_out"], i)
                    v.tensor_scalar(f8[:, 0, :], r, 240.0, -240.0, ALU.min, ALU.max, saturate=False).then_inc(once["q_clip"], 1)
                    v.tensor_scalar(f8[:, 1, :], r, 240.0, 0.5, ALU.max, ALU.mult, saturate=False).then_inc(once["q_big"], 1)
                    v.tensor_scalar(f8[:, 2, :], r, -240.0, 0.5, ALU.min, ALU.mult, saturate=False).then_inc(once["q_big"], 1)
                    v.wait_ge(once["q_big"], 2 * i + 2)
                    v.wait_ge(once["q_clip"], i + 1)
                    v.scalar_tensor_tensor(qtmp, f8[:, 1, :], 2.0, f8[:, 0, :], ALU.mult, ALU.add).then_inc(once["q_sum"], 1)
                    v.wait_ge(once["q_sum"], i + 1)
                    dst = wgu[:, c].rearrange("p k w c -> p (k w c)") if kind == "gu" else wdn[:, 2 * c:2 * c + 2, :].rearrange("p a b -> p (a b)")
                    v.scalar_tensor_tensor(dst, f8[:, 2, :], 2.0, qtmp, ALU.mult, ALU.add).then_inc(once["q_out"], 1)

            def mamba(b):
                yield T["in"]
                v.wait_ge(x_in, b * 16 + 16)
                for t in range(T2):
                    v.bn_stats(zst[:, t, :], xin[:, t, :]).then_inc(sem["zstat"], 1)
                v.wait_ge(*at("zstat", b, 2))
                for t in range(T2):
                    v.bn_aggr(zmv[:, t, :], zst[:, t, :]).then_inc(sem["zstat"], 1)
                v.wait_ge(*at("zstat", b, 4))
                v.tensor_scalar(zv[:, :], zmv[:, :, 1], LN_EPS, None, ALU.add).then_inc(sem["zvar"], 1)
                v.wait_ge(*at("xi", b, 1))
                v.tensor_copy(xpad[:, :, TAPS - 1:], ps[:, 0, :].rearrange("p (e l) -> p e l", e=2)).then_inc(sem["xpad"], 1)
                v.wait_ge(*at("xpad", b, 1))
                v.wait_ge(*at("conv_tanh", b, 0))
                for k in range(TAPS):
                    for e in range(2):
                        w = vec[:, V_CW + 4 * e + k:V_CW + 4 * e + k + 1]
                        if k:
                            v.wait_ge(*at("conv_step", b, 2 * (k - 1) + e + 1))
                        if k == 0:
                            i = v.tensor_scalar(cv[:, e, :], xpad[:, e, 0:L], w, vec[:, V_CB + e:V_CB + e + 1], ALU.mult, ALU.add)
                        else:
                            i = v.scalar_tensor_tensor(cv[:, e, :], xpad[:, e, k:k + L], w, cv[:, e, :], ALU.mult, ALU.add)
                        i.then_inc(sem["conv" if k == TAPS - 1 else "conv_step"], 1)
                v.wait_ge(*at("zrstd", b, 1))
                for t in range(T2):
                    v.tensor_scalar(zh[:, t, :], xin[:, t, :], zmv[:, t, 0:1], zr[:, t:t + 1], ALU.subtract, ALU.mult).then_inc(sem["zhat"], 1)
                v.wait_ge(*at("conv_tanh", b, 1))
                v.scalar_tensor_tensor(u2[:, :, :], u2[:, :, :], 1.0, cv[:, :, :], ALU.add, ALU.mult).then_inc(sem["u"], 1)
                v.wait_ge(*at("ztanh", b, 1))
                v.scalar_tensor_tensor(zg[:, :, :], zt[:, :, :], 1.0, zh[:, :, :], ALU.add, ALU.mult).then_inc(sem["zg"], 1)
                yield T["xproj"]
                v.wait_ge(*at("bc_hi", b, 1))
                for r in (BCR, 3 * BCR):
                    hi = stack[r:min(r + BCR, XR), :]
                    v.scalar_tensor_tensor(hi, ps[r:min(r + BCR, XR), 0, 0:L], 0.5, hi.bitcast(F32), ALU.mult, ALU.subtract).then_inc(sem["bc_lo"], 1)
                yield T["dt"]
                v.wait_ge(*at("dt_pre", b, 1))
                v.wait_ge(*at("zg", b, 1))
                v.wait_ge(*at("sp_abs", b, 2))
                for e in range(2):
                    v.tensor_scalar(sp_r[:, e, :], ps[:, 1, e * L:e * L + L], vec[:, V_DTB + e:V_DTB + e + 1], 0.0, ALU.add, ALU.max).then_inc(sem["sp_relu"], 1)
                v.wait_ge(*at("sp_t", b, 1))
                v.tensor_scalar(sp_q, sp_x, -0.25, 1.0 / 3.0, ALU.mult, ALU.add).then_inc(sem["sp_step"], 1)
                v.tensor_scalar(sp_m, sp_x, 1.0 / 32.0, None, ALU.is_lt).then_inc(sem["sp_step"], 1)
                v.wait_ge(*at("sp_step", b, 1))
                v.tensor_tensor(sp_q, sp_q, sp_x, ALU.mult).then_inc(sem["sp_step"], 1)
                v.wait_ge(*at("sp_step", b, 3))
                v.scalar_tensor_tensor(sp_q, sp_q, -0.5, sp_x, ALU.add, ALU.mult).then_inc(sem["sp_step"], 1)
                v.wait_ge(*at("sp_step", b, 4))
                v.scalar_tensor_tensor(sp_q, sp_q, 1.0, sp_x, ALU.add, ALU.mult).then_inc(sem["sp_step"], 1)
                v.wait_ge(*at("sp_step", b, 5))
                v.wait_ge(*at("sp_ln", b, 1))
                v.copy_predicated(sp_l, sp_m, sp_q).then_inc(sem["sp_step"], 1)
                v.wait_ge(*at("sp_step", b, 6))
                v.wait_ge(*at("sp_relu", b, 2))
                v.tensor_tensor(dt_sb[:, :, :], sp_l, sp_r[:, :, :], ALU.add).then_inc(sem["dt"], 1)
                v.wait_ge(*at("dt", b, 1))
                v.scalar_tensor_tensor(du[:, :, :], dt_sb[:, :, :], 0.5, u2[:, :, :], ALU.mult, ALU.mult).then_inc(sem["du"], 1)
                v.wait_ge(*at("du", b, 1))
                for n in range(NS):
                    yield T["scan"] + DT["scan"] * n
                    hn = hb[:, n % 3]
                    v.wait_ge(*at("c_sb", b, n + 1))
                    if n >= 3:
                        v.wait_ge(*at("y_red", b, n - 2))
                    bb = ps[:, n % 2, 0:L].rearrange("p (a l) -> p a l", a=1).to_broadcast([P, 2, L])
                    v.tensor_tensor(hn, du[:, :, :], bb, ALU.mult).then_inc(sem["dbu"], 1)
                    v.wait_ge(*at("dbu", b, n + 1))
                    v.wait_ge(*at("dA", b, 2 * n + 2))
                    hf = hn.rearrange("p e l -> p (e l)")
                    v.tensor_tensor_scan(hf, dA[:, n % 2].rearrange("p e l -> p (e l)"), hf, 0.0, ALU.mult, ALU.add).then_inc(sem["h"], 1)
                yield T["y"]
                v.wait_ge(*at("y_red", b, NS))
                for e in range(2):
                    v.scalar_tensor_tensor(cv[:, e, :], u2[:, e, :], halfD[:, e:e + 1], ps[:, 2, e * L:e * L + L], ALU.mult, ALU.add).then_inc(sem["ys"], 1)
                v.wait_ge(*at("ys", b, 2))
                v.tensor_tensor(cv[:, :, :], cv[:, :, :], zg[:, :, :], ALU.mult).then_inc(sem["yz"], 1)
                v.wait_ge(*at("yT", b, 1))
                v.wait_ge(*at("x2", b, 0))
                v.scalar_tensor_tensor(xa[:, :, :], ps[:, 0, :].rearrange("p (t d) -> p t d", t=T2), tgh[:, :], xin[:, :, :], ALU.mult, ALU.add).then_inc(sem["x1"], 1)

            def layer_norm(b, i, src):
                for t in range(T2):
                    v.bn_stats(lst[:, t, :], src[:, t, :]).then_inc(sem["lstat"], 1)
                v.wait_ge(*at("lstat", b, 4 * i + 2))
                for t in range(T2):
                    v.bn_aggr(lmv[:, t, :], lst[:, t, :]).then_inc(sem["lstat"], 1)
                v.wait_ge(*at("lstat", b, 4 * i + 4))
                v.tensor_scalar(lv[:, :], lmv[:, :, 1], LN_EPS, None, ALU.add).then_inc(sem["lvar"], 1)
                v.wait_ge(*at("lrstd", b, i + 1))
                for t in range(T2):
                    v.tensor_scalar(xh[:, t, :], src[:, t, :], lmv[:, t, 0:1], lr[:, t:t + 1], ALU.subtract, ALU.mult).then_inc(sem["xh"], 1)

            def head_norm(b, src, w, bias, step, var, rstd, last):
                mean, ssq, ve, rs_ = hs[:, 0, :], hs[:, 1, :], hs[:, 2, :], hs[:, 3, :]

                def wide(c):
                    return c.rearrange("p (t h a) -> p t h a", t=T2, a=1).to_broadcast([P, T2, H, HD])
                v.tensor_reduce(mean, src, AX_X, ALU.add).then_inc(sem[step], 1)
                v.wait_ge(*at(step, b, 1))
                v.tensor_scalar(mean, mean, 1.0 / HD, None, ALU.mult).then_inc(sem[step], 1)
                v.wait_ge(*at(step, b, 2))
                v.tensor_tensor(qk[:, :, :, :], src, wide(mean), ALU.subtract).then_inc(sem[step], 1)
                v.wait_ge(*at(step, b, 3))
                v.tensor_tensor(sq, qk[:, :, :, :], qk[:, :, :, :], ALU.mult).then_inc(sem[step], 1)
                v.wait_ge(*at(step, b, 4))
                v.tensor_reduce(ssq, sq, AX_X, ALU.add).then_inc(sem[step], 1)
                v.wait_ge(*at(step, b, 5))
                v.tensor_scalar(ve, ssq, 1.0 / HD, QK_EPS, ALU.mult, ALU.add).then_inc(sem[var], 1)
                v.wait_ge(*at(rstd, b, 1))
                v.tensor_tensor(qk[:, :, :, :], qk[:, :, :, :], wide(rs_), ALU.mult).then_inc(sem[step], 1)
                v.wait_ge(*at(step, b, 6))
                v.tensor_tensor(qk[:, :, :, :], qk[:, :, :, :], w, ALU.mult).then_inc(sem[last], 1)
                v.wait_ge(*at(last, b, 1))
                v.tensor_tensor(qk[:, :, :, :], qk[:, :, :, :], bias, ALU.add).then_inc(sem[last], 1)
                v.wait_ge(*at(last, b, 2))

            def rest(b):
                yield T["kv"]
                v.wait_ge(*at("kv_ps", b, 1))
                v.wait_ge(*at("vst", b, 0))
                for t in range(T2):
                    v.tensor_tensor(kvs[:, t, :], ps[:, 3 + t, :], kv_bias[:, t, :], ALU.add).then_inc(sem["kv"], 1)
                v.wait_ge(*at("kv", b, 2))
                k = kvs[:, :, :].rearrange("p t (h c) -> p t h c", h=H)[:, :, :, 0:HD]

                def by_token(c0):
                    return row[:, c0:c0 + T2 * HD].rearrange("p (t a c) -> p t a c", t=T2, a=1).to_broadcast([P, T2, H, HD])

                def by_head(i):
                    return qwb[:, i, :].rearrange("p (t a c) -> p t a c", t=1, a=1).to_broadcast([P, T2, H, HD])
                head_norm(b, k, by_token(R_KW), by_token(R_KB), "kstep", "kvar", "krstd", "kstack")
                yield T["kstack"]
                v.wait_ge(*at("qT_ps", b, 0))
                v.tensor_copy(st[:, :, :, 0:HD], qk[:, :, :, :]).then_inc(sem["kstack"], 1)
                v.tensor_copy(st[:, :, :, 2 * HD:3 * HD], qk[:, :, :, :]).then_inc(sem["kstack"], 1)
                km = row[:, R_KM:R_KM + T2 * 4].rearrange("p (t a c) -> p t a c", t=T2, a=1).to_broadcast([P, T2, H, 4])
                v.tensor_copy(st[:, :, :, 3 * HD:3 * HD + 4], km).then_inc(sem["k_m"], 1)
                v.wait_ge(*at("kstack", b, 3))
                v.tensor_tensor(st[:, :, :, HD:2 * HD], qk[:, :, :, :], st[:, :, :, 0:HD].bitcast(F32), ALU.subtract).then_inc(sem["kstack"], 1)
                yield T["ln0"]

                v.wait_ge(*at("x1", b, 1))
                layer_norm(b, 0, xa)
                yield T["xT0"]
                v.wait_ge(*at("x_hi", b, 1))
                v.tensor_tensor(xlo[:, :, :], b7x, xhi[:, :, :].bitcast(F32), ALU.subtract).then_inc(sem["x_lo"], 1)
                for m in range(MF):
                    yield T["ffn"] + DT["ffn"] * m
                    v.wait_ge(*at("g_tanh", b, m + 1))
                    g, u = ps[:, 3 + m % 4, 0:L], ps[:, 3 + m % 4, L:2 * L]
                    v.scalar_tensor_tensor(work[:, 2 + m % 2, :], work[:, m % 2, :], 1.0, g, ALU.add, ALU.mult).then_inc(sem["g_a"], 1)
                    v.wait_ge(*at("g_a", b, m + 1))
                    v.scalar_tensor_tensor(work[:, 4 + m, :], work[:, 2 + m % 2, :], gsu[:, m:m + 1], u, ALU.mult, ALU.mult).then_inc(sem["h_ff"], 1)
                yield T["down"]
                v.wait_ge(*at("down", b, 1))
                ds2 = dsb.rearrange("p (a d) -> p a d", a=1).to_broadcast([P, T2, D])
                v.tensor_tensor(xh[:, :, :], b7x, ds2, ALU.mult).then_inc(sem["dsc"], 1)
                v.wait_ge(*at("dsc", b, 1))
                v.tensor_tensor(xb[:, :, :], xh[:, :, :], xa[:, :, :], ALU.add).then_inc(sem["x2"], 1)
                yield T["x2"]

                v.wait_ge(*at("x2", b, 1))
                layer_norm(b, 1, xb)
                bo2 = gbo.rearrange("p (a d) -> p a d", a=1).to_broadcast([P, T2, D])
                v.wait_ge(*at("xh", b, 4))
                v.tensor_tensor(xb[:, :, :], xb[:, :, :], bo2, ALU.add).then_inc(sem["xbo"], 1)
                yield T["q"]
                v.wait_ge(*at("q_ps", b, 1))
                bq2 = row[:, R_BQ:R_BQ + D].rearrange("p (a d) -> p a d", a=1).to_broadcast([P, T2, D])
                v.tensor_tensor(qk[:, :, :, :].rearrange("p t h c -> p t (h c)"), ps[:, 3, :].rearrange("p (t d) -> p t d", t=T2), bq2, ALU.add).then_inc(sem["q"], 1)
                v.wait_ge(*at("q", b, 1))
                v.wait_ge(*at("kstack", b, 5))
                v.wait_ge(*at("kT_ps", b, 2))
                head_norm(b, qk[:, :, :, :], by_head(0), by_head(1), "qstep", "qvar", "qrstd", "qstack")
                v.tensor_copy(st[:, :, :, 0:HD], qk[:, :, :, :]).then_inc(sem["qstack"], 1)
                v.wait_ge(*at("qstack", b, 3))
                v.tensor_tensor(st[:, :, :, 2 * HD:3 * HD], qk[:, :, :, :], st[:, :, :, 0:HD].bitcast(F32), ALU.subtract).then_inc(sem["qstack"], 1)
                v.tensor_copy(st[:, :, :, HD:2 * HD], qk[:, :, :, :]).then_inc(sem["q_hi2"], 1)
                for i in range(8):
                    yield T["scores"] + DT["scores"] * i
                    t, hg = i // 4, i % 4
                    v.wait_ge(*at("s_ps", b, i + 1))
                    sc = bank(3 + 2 * (i % 2), 1024, 2).rearrange("p (b a c) -> p b a c", b=2, a=2)
                    mh = mx[:, t, 4 * hg:4 * hg + 4, :].rearrange("p (a b) w -> p b a w", b=2)
                    v.tensor_reduce(mh[:, :, :, 0], sc[:, :, :, 0:MAIN], AX_X, ALU.max).then_inc(sem["mx"], 1)
                    v.tensor_reduce(mh[:, :, :, 1], sc[:, :, :, MAIN:L], AX_X, ALU.max).then_inc(sem["mx"], 1)
                yield T["m"]
                ms = st[:, :, :, 3 * HD:3 * HD + 4].rearrange("p t h (w a) -> p t h w a", w=2)
                v.wait_ge(*at("mx", b, 16))
                v.wait_ge(*at("qT_ps", b, 2))
                v.tensor_copy(ms[:, :, :, :, 0], mx[:, :, :, :]).then_inc(sem["mstack"], 1)
                v.wait_ge(*at("mstack", b, 1))
                v.tensor_tensor(ms[:, :, :, :, 1], mx[:, :, :, :], ms[:, :, :, :, 0].bitcast(F32), ALU.subtract).then_inc(sem["mstack"], 1)
                for j in range(HP):
                    yield T["heads"] + DT["heads"] * (2 * j + 5)
                    v.wait_ge(*at("oT_ps", b, j + 1))
                    o = ps[:, 7, 0:L].rearrange("p (a c) -> p a c", a=4)
                    if j:
                        v.wait_ge(*at("ctok", b, j))
                    o2 = o[:, :, 0:2 * HD + 2].rearrange("p a (w c) -> p a w c", w=2)
                    v.reciprocal(rec[:, :, :], o2[:, :, :, HD]).then_inc(sem["o_step"], 1)
                    v.wait_ge(*at("o_step", b, 2 * j + 1))
                    v.tensor_tensor(opr[:, :, :, :], o2[:, :, :, 0:HD], rec[:, :, :].rearrange("p a (w c) -> p a w c", c=1).to_broadcast([P, 4, 2, HD]), ALU.mult).then_inc(sem["o_step"], 1)
                    v.wait_ge(*at("o_step", b, 2 * j + 2))
                    dst = ctok[:, :, 2 * j:2 * j + 2, :]
                    src = opr[:, :, :, :].rearrange("p (t h) w c -> p t h w c", t=T2)
                    v.tensor_tensor(dst, src[:, :, :, 0], src[:, :, :, 1], ALU.add).then_inc(sem["ctok"], 1)
                yield T["wo"]
                v.wait_ge(*at("wo_ps", b, 1))
                v.wait_ge(*at("xbo", b, 1))
                v.scalar_tensor_tensor(xb[:, :, :], ps[:, 5, :].rearrange("p (t d) -> p t d", t=T2), tg[:, 1:2], xb[:, :, :], ALU.mult, ALU.add).then_inc(sem["x3"], 1)
                yield T["ln2"]

                v.wait_ge(*at("x3", b, 1))
                layer_norm(b, 2, xb)
                yield T["xT2"]
                v.wait_ge(*at("x_hi", b, 2))
                v.tensor_tensor(xlo[:, :, :], b7x, xhi[:, :, :].bitcast(F32), ALU.subtract).then_inc(sem["x_lo"], 1)
                yield T["router"]
                k_ = 0

                def router(i):
                    nonlocal k_
                    k_ += 1
                    i.then_inc(sem["r_step"], 1)
                    v.wait_ge(*at("r_step", b, k_))
                v.wait_ge(*at("lg_tanh", b, 1))
                score, sel, rank = rt[:, 1], rt[:, 2], rt[:, 3]
                router(v.tensor_scalar(score, rt[:, 0], 0.5, 0.5, ALU.mult, ALU.add))
                rb = row[:, R_RB:R_RB + E].rearrange("p (a e) -> p a e", a=1).to_broadcast([P, T2, E])
                router(v.tensor_tensor(sel, score, rb, ALU.add))
                other = sel.rearrange("p t (a f) -> p t a f", a=1).to_broadcast([P, T2, E, E])
                own = sel.rearrange("p t (e a) -> p t e a", a=1).to_broadcast([P, T2, E, E])
                gt = rk[:, 0].rearrange("p t (e f) -> p t e f", e=E)
                eq = rk[:, 1].rearrange("p t (e f) -> p t e f", e=E)
                router(v.tensor_tensor(gt, other, own, ALU.is_gt))
                router(v.tensor_tensor(eq, other, own, ALU.is_equal))
                tri = row[:, R_TR:R_TR + E * E].rearrange("p (a f) -> p a f", a=1).to_broadcast([P, T2, E * E])
                router(v.tensor_tensor(rk[:, 1], rk[:, 1], tri, ALU.mult))
                router(v.tensor_tensor(rk[:, 0], rk[:, 0], rk[:, 1], ALU.add))
                router(v.tensor_reduce(rank, gt, AX_X, ALU.add))
                router(v.scalar_tensor_tensor(rt[:, 4], rank, 1.5, score, ALU.is_lt, ALU.mult))
                router(v.tensor_reduce(rs[:, :], rt[:, 4], AX_X, ALU.add))
                router(v.tensor_scalar(rs[:, :], rs[:, :], 1e-12, None, ALU.max))
                router(v.reciprocal(rs[:, :], rs[:, :]))
                router(v.tensor_tensor(rt[:, 5], rt[:, 4], rs[:, :].rearrange("p (t a) -> p t a", a=1).to_broadcast([P, T2, E]), ALU.mult))
                v.tensor_copy(gst[:, :, 0:E], rt[:, 5]).then_inc(sem["gates"], 1)
                v.wait_ge(*at("gates", b, 1))
                v.tensor_tensor(gst[:, :, E:2 * E], rt[:, 5], gst[:, :, 0:E].bitcast(F32), ALU.subtract).then_inc(sem["gates"], 1)
                for m in range(MM):
                    yield T["moe"] + DT["moe"] * m
                    v.wait_ge(*at("m_tanh", b, m + 1))
                    h1, h3 = ps[:, 3 + m % 3, 0:L], ps[:, 3 + m % 3, L:2 * L]
                    gate = ps[:, 6, 0:L]
                    t1, t2, hg = work[:, 2 + m % 2, :], work[:, 4 + m % 2, :], work[:, 6 + m % 3, :]
                    if m >= 3:
                        v.wait_ge(*at("y2_part", b, m - 2))
                    v.scalar_tensor_tensor(t1, work[:, m % 2, :], 1.0, h1, ALU.add, ALU.mult).then_inc(sem["m_a"], 1)
                    v.wait_ge(*at("m_a", b, m + 1))
                    if m < MG:
                        v.scalar_tensor_tensor(t2, t1, 0.5, h3, ALU.mult, ALU.mult).then_inc(sem["m_b"], 1)
                        v.wait_ge(*at("m_b", b, m + 1))
                        v.tensor_tensor(hg, t2, gate, ALU.mult).then_inc(sem["hg"], 1)
                    else:
                        v.scalar_tensor_tensor(hg, t1, 0.5, h3, ALU.mult, ALU.mult).then_inc(sem["hg"], 1)
                yield T["out"]
                v.wait_ge(*at("y2", b, 1))
                v.wait_ge(*at("lg", b, 1))
                v.scalar_tensor_tensor(xo[:, :, :], b7x, tg[:, 3:4], xb[:, :, :], ALU.mult, ALU.add).then_inc(sem["xo"], 1)

            schedule(mamba, rest, weights)

        @block.tensor
        def _(pe):
            def transposes(src, dst, id_):
                for i in range(2):
                    for k in range(2):
                        last = pe.transpose(dst(i, k), src[:, i, k * P:k * P + P], id_)
                return last

            def mamba(b):
                yield T["in"]
                pe.wait_ge(ctx_in, b * 16 + 16)
                pe.wait_ge(*at("x1", b, 0))
                for e in range(2):
                    mm = pe.matmul(ps[:, 0, e * L:e * L + L], win[:, e * P:e * P + P], ctx[:, :], start=True, stop=True)
                mm.then_inc(sem["xi"], 1)
                yield T["xproj"]
                pe.wait_ge(*at("u", b, 1))
                for k in range(2):
                    mm = pe.matmul(ps[0:XR, 0, 0:L], wxp[:, k, :], u2[:, k, :], start=(k == 0), stop=(k == 1))
                mm.then_inc(sem["xdbl"], 1)
                yield T["dt"]
                pe.wait_ge(*at("bc_lo", b, 2))
                pe.wait_ge(once["setup"], 1)
                for e in range(2):
                    o = ps[:, 1, e * L:e * L + L]
                    pe.matmul(o, wdt_hi[64:XR, e * P:e * P + P], stack[64:XR, :], start=True, stop=False)
                    mm = pe.matmul(o, wdt_lo[64:72, e * P:e * P + P], stack[64:72, :], start=False, stop=True)
                mm.then_inc(sem["dt_pre"], 1)

                def spread(n):
                    if n == 1:
                        pe.wait_ge(*at("dt", b, 1))
                    if n >= 2:
                        pe.wait_ge(*at("dbu", b, n - 1))
                        pe.wait_ge(*at("c_sb", b, n - 1))
                    for w in range(2):
                        r = w * NS + n
                        mm = pe.matmul(ps[:, n % 2, w * L:w * L + L], selBC[:, r:r + 1].to_broadcast([2 * BCR, P]), stack[0:2 * BCR, :], start=True, stop=True)
                    mm.then_inc(sem["bc"], 1)

                pe.wait_ge(*at("ys", b, 0))
                for n in range(NS + 3):
                    yield T["scan"] + DT["scan"] * n
                    if n < NS:
                        spread(n)
                    if n >= 3:
                        k = n - 3
                        pe.wait_ge(*at("p", b, k + 1))
                        pe.matmul(ps[:, 2, :], ident, hb[:, k % 3].rearrange("p e l -> p (e l)"), start=(k == 0), stop=(k == NS - 1)).then_inc(sem["y_red"], 1)
                yield T["y"]
                pe.wait_ge(*at("yz", b, 1))
                for e in range(2):
                    for t in range(T2):
                        mm = pe.transpose(ps[:, 0, t * D + e * P:t * D + e * P + P], cv[:, e, t * P:t * P + P], ident)
                mm.then_inc(sem["yT"], 1)

            def xh_transposes(b, i):
                pe.wait_ge(*at("xh", b, 2 * i + 2))
                for t in range(T2):
                    for k in range(K2):
                        mm = pe.transpose(b7x[:, k, t * P:t * P + P], xh[:, t, k * P:k * P + P], ident)
                mm.then_inc(sem["xT_ps"], 1)

            def stack_transposes(t, done):
                for j in range(HP):
                    src = st[:, t, 2 * j:2 * j + 2, :].rearrange("p h c -> p (h c)")
                    mm = pe.transpose(psR[:, 5 - 2 * t + j // 4, (j % 4) * P:(j % 4) * P + P], src, identR[:, :])
                mm.then_inc(sem[done], 1)

            def rest(b):
                yield T["kv"]
                pe.wait_ge(ctxR_in, b * 48 + 48)
                pe.wait_ge(*at("xo", b, 0))
                pe.wait_ge(once["later"], 16 * len(LATER))
                pe.matmul(ps[:, 3, :], ctxR[:, 0, :], wkv[:, :], start=True, stop=True)
                pe.matmul(ps[:, 4, :], ctxR[:, 1, :], wkv[:, :], start=True, stop=False)
                pe.matmul(ps[:, 4, :], ctxR[:, 2, :], wkvd[:, :], start=False, stop=True).then_inc(sem["kv_ps"], 1)
                yield T["kT"]
                pe.wait_ge(*at("kstack", b, 5))
                pe.wait_ge(*at("k_m", b, 1))
                pe.wait_ge(*at("kv", b, 2))
                for t in range(T2):
                    stack_transposes(t, "kT_ps")
                yield T["xT0"]

                xh_transposes(b, 0)
                pe.wait_ge(*at("x_lo", b, 1))
                pe.wait_ge(*at("kT", b, 2))

                def down(m):
                    pe.wait_ge(once["q_out"], QUANT)
                    pe.wait_ge(*at("h_ff", b, m + 1))
                    for t in range(T2):
                        mm = pe.matmul(ps[:, 7, t * D:t * D + D], work[:, 4 + m, t * P:t * P + P], wdn[:, m, :],
                                       start=(m == 0 and t == 0), stop=(m == MF - 1), skip_group_check=True)
                    if m == MF - 1:
                        mm.then_inc(sem["down"], 1)
                for m in range(MF):
                    yield T["ffn"] + DT["ffn"] * m
                    if m >= 4:
                        pe.wait_ge(*at("h_ff", b, m - 3))
                    pe.wait_ge(once["q_out"], m + 1)
                    for w in range(2):
                        o = ps[:, 3 + m % 4, w * L:w * L + L]
                        for k in range(K2):
                            pe.matmul(o, wgu[:, m, k, w, :], xhi[:, k, :], start=(k == 0), stop=False)
                        for k in range(K2):
                            mm = pe.matmul(o, wgu[:, m, k, w, :], xlo[:, k, :], start=False, stop=(k == K2 - 1))
                    mm.then_inc(sem["gu"], 1)
                    if m >= 2:
                        down(m - 2)
                yield T["down"]
                down(MF - 2)
                down(MF - 1)
                yield T["x2"]

                pe.wait_ge(*at("dsc", b, 1))
                xh_transposes(b, 1)
                pe.wait_ge(*at("xT", b, 1))
                for t in range(T2):
                    for k in range(K2):
                        mm = pe.matmul(ps[:, 3, t * D:t * D + D], xT[:, k, t * P:t * P + P], wq[:, k, :], start=(k == 0), stop=(k == K2 - 1))
                mm.then_inc(sem["q_ps"], 1)
                yield T["qT"]
                pe.wait_ge(*at("q_hi2", b, 1))
                for t in range(T2):
                    stack_transposes(t, "qT_ps")

                def half(t_, h):
                    return t_[64 * (h % 2):64 * (h % 2) + 3 * HD, h // 2, :]

                def whole(t_, h):
                    return t_[64 * (h % 2):64 * (h % 2) + 3 * HD + 4, h // 2, :]
                pe.wait_ge(*at("qT", b, 2))
                for i in range(8):
                    yield T["scores"] + DT["scores"] * i
                    t, hg = i // 4, i % 4
                    if i >= 2:
                        pe.wait_ge(*at("mx", b, 2 * (i - 1)))
                    for h in range(4):
                        hh = 4 * hg + h
                        mm = pe.matmul(ps[:, 3 + 2 * (i % 2) + h % 2, (h // 2) * L:(h // 2) * L + L], half(qT, hh)[:, t * P:t * P + P], half(kT, hh), start=True, stop=True)
                    mm.then_inc(sem["s_ps"], 1)
                yield T["m"]
                pe.wait_ge(*at("mstack", b, 2))
                for t in range(T2):
                    stack_transposes(t, "qT_ps")
                pe.wait_ge(*at("qT", b, 4))

                def weigh(j):
                    pe.wait_ge(*at("prob", b, 2 * j + 2))
                    if j == 0:
                        pe.wait_ge(*at("vst", b, 3))
                    if j >= 1:
                        pe.wait_ge(*at("o_sb", b, j))
                    for hh in range(2):
                        for kt in range(T2):
                            mm = pe.matmul(ps[64 * hh:64 * hh + 64, 6, 0:L], vst[:, kt, VW * (2 * j + hh):VW * (2 * j + hh) + 64], work[:, (4 * j + 2 * hh) % 8 + kt, :], start=(kt == 0), stop=(kt == 1))
                    mm.then_inc(sem["pv"], 1)

                def turn(j):
                    pe.wait_ge(*at("o_sb", b, j + 1))
                    if j >= 1:
                        pe.wait_ge(*at("o_step", b, 2 * j))
                    for t in range(T2):
                        mm = pe.transpose(ps[:, 7, t * P:t * P + P], work[:, 8 + j % 2, t * P:t * P + P], ident)
                    mm.then_inc(sem["oT_ps"], 1)
                for h in range(H + 4):
                    yield T["heads"] + DT["heads"] * h
                    if h < H:
                        if h >= 3:
                            pe.wait_ge(*at("prob", b, h - 2))
                        for kt in range(T2):
                            mm = pe.matmul(ps[:, 3 + h % 3, kt * L:kt * L + L], whole(kT, h)[:, kt * P:kt * P + P], whole(qT, h), start=True, stop=True)
                        mm.then_inc(sem["st_ps"], 1)
                    if h % 2 == 1 and 3 <= h <= H + 1:
                        weigh((h - 3) // 2)
                    if h % 2 == 1 and h >= 5:
                        turn((h - 5) // 2)
                yield T["wo"]
                pe.wait_ge(*at("ctok", b, HP))
                for t in range(T2):
                    for k in range(K2):
                        mm = pe.transpose(ps[:, 3, k * L + t * P:k * L + t * P + P], ctok[:, t, 8 * k:8 * k + 8, :].rearrange("p h c -> p (h c)"), ident)
                mm.then_inc(sem["cT_ps"], 1)
                pe.wait_ge(*at("cT", b, 1))
                for t in range(T2):
                    for k in range(K2):
                        mm = pe.matmul(ps[:, 5, t * D:t * D + D], xT[:, k, t * P:t * P + P], wo[:, k, :], start=(k == 0), stop=(k == K2 - 1))
                mm.then_inc(sem["wo_ps"], 1)
                yield T["xT2"]

                xh_transposes(b, 2)
                pe.wait_ge(*at("xT", b, 2))
                for t in range(T2):
                    for k in range(K2):
                        mm = pe.matmul(ps[:, 3, t * E:t * E + E], xT[:, k, t * P:t * P + P], wgate[:, k, :], start=(k == 0), stop=(k == K2 - 1))
                mm.then_inc(sem["lg"], 1)
                yield T["router"]
                pe.wait_ge(*at("x_lo", b, 2))

                def hidden(m):
                    if m == 0:
                        pe.wait_ge(*at("x3", b, 1))
                    if m >= 3:
                        pe.wait_ge(*at("hg", b, m - 2))
                    pe.wait_ge(once["raw_lo"], m + 1)
                    for w in range(2):
                        o = ps[:, bank_of(m), w * L:w * L + L]
                        for k in range(K2):
                            pe.matmul(o, w13_hi[:, m, k, w, :], xhi[:, k, :], start=(k == 0), stop=False)
                            pe.matmul(o, w13_hi[:, m, k, w, :], xlo[:, k, :], start=False, stop=False)
                            mm = pe.matmul(o, w13_lo[:, m, k, w, :], xhi[:, k, :], start=False, stop=(k == K2 - 1))
                    return mm

                def bank_of(m):
                    return 3 + m % 3
                pe.wait_ge(*at("lg_tanh", b, 1))
                pe.wait_ge(*at("gates", b, 2))
                for t in range(T2):
                    mm = pe.transpose(psR[0:2 * E, 4, t * P:t * P + P], gst[:, t, :], identR[:, :])
                mm.then_inc(sem["gT_ps"], 1)
                pe.wait_ge(*at("gT", b, 1))

                def second(m):
                    pe.wait_ge(*at("hg", b, m + 1))
                    for t in range(T2):
                        mm = pe.matmul(ps[:, 7, t * D:t * D + D], work[:, 6 + m % 3, t * P:t * P + P], w2s[:, m, :],
                                       start=(m == 0 and t == 0), stop=(m == MM - 1), skip_group_check=True)
                    if m == MM - 1:
                        mm.then_inc(sem["y2"], 1)
                    else:
                        mm.then_inc(sem["y2_part"], 1)
                for m in range(MM):
                    yield T["moe"] + DT["moe"] * m
                    mm = hidden(m)
                    if m < MG:
                        if m:
                            pe.wait_ge(*at("hg", b, m))
                        mm = pe.matmul(ps[:, 6, 0:L], gselR[:, m, :], gT[:, :], start=True, stop=True)
                    mm.then_inc(sem["h13"], 1)
                    if m >= 2:
                        second(m - 2)
                yield T["out"]
                second(MM - 2)
                second(MM - 1)

            pe.wait_ge(once["early"], 16 * len(EARLY))
            pe.wait_ge(once["ident_r"], 3)
            schedule(mamba, rest)


def by_k(w):
    k, n = w.shape
    return w.reshape(k // P, P, n).transpose(1, 0, 2)


def kernel(**inputs):
    import numpy as np
    import concourse.bacc as bacc
    from concourse.bass_utils import run_bass_kernel_spmd

    a = {k: np.asarray(v) for k, v in inputs.items()}
    m = {k[len("L0_xattn_"):]: v for k, v in a.items() if k.startswith("L0_xattn_")}
    f = {k[len("L0_ffn_"):]: v for k, v in a.items() if k.startswith("L0_ffn_")}
    q = {k[len("L1_xattn_"):]: v for k, v in a.items() if k.startswith("L1_xattn_")}
    e = {k[len("L1_ffn_"):]: v for k, v in a.items() if k.startswith("L1_ffn_")}
    z = lambda *s: np.zeros(s, np.float32)

    xp = m["x_proj_w"].T
    wxp = z(D, XR)
    wxp[:, 0:BCR] = wxp[:, BCR:2 * BCR] = xp[:, DTR:]
    wxp[:, 64:64 + DTR] = wxp[:, 96:96 + DTR] = xp[:, :DTR]
    wdt = z(P, D)
    wdt[64:64 + DTR] = wdt[96:96 + DTR] = m["dt_proj_w"].T

    gu = np.stack([by_k(f["gate_w"]), by_k(f["up_w"])], 2)
    gu = gu.reshape(P, K2, 2, MF, P).transpose(0, 3, 1, 2, 4).reshape(P, MF, 512)
    w1, w3, w2 = z(D, MM * P), z(D, MM * P), z(MM * P, D)
    w1[:, :HID] = np.concatenate([e["W1"].transpose(1, 0, 2).reshape(D, E * INTER), e["sw1"].T], 1)
    w3[:, :HID] = np.concatenate([e["W3"].transpose(1, 0, 2).reshape(D, E * INTER), e["sw3"].T], 1)
    w2[:HID] = np.concatenate([e["W2"].reshape(E * INTER, D), e["sw2"].T], 0)
    w13 = np.stack([by_k(w1), by_k(w3)], 2).reshape(P, K2, 2, MM, P).transpose(0, 3, 1, 2, 4).reshape(P, MM, 512)

    def heads(k, v):
        return np.stack([k.reshape(-1, H, HD), v.reshape(-1, H, HD)], 2).reshape(-1, 2 * D)
    wkv = np.concatenate([q["Wk"], q["Wv"]], 1)
    wkvd = heads(q["Wkv_dca"][:, :D], q["Wkv_dca"][:, D:])
    kvb = z(P, T2, 2 * D)
    kvb[:] = np.concatenate([q["bk"], q["bv"]])
    kvb[MAIN - P:, 1] = heads(q["bkv_dca"][None, :D], q["bkv_dca"][None, D:])[0]

    vecs = z(P, V_N)
    for i in range(2):
        s = slice(i * P, i * P + P)
        vecs[:, V_CW + 4 * i:V_CW + 4 * i + 4] = m["conv_w"][s, 0]
        vecs[:, V_CB + i] = m["conv_b"][s]
        vecs[:, V_DTB + i] = m["dt_proj_b"][s]
        vecs[:, V_AL + NS * i:V_AL + NS * i + NS] = m["A_log"][s]
        vecs[:, V_D + i] = m["D"][s]
    vecs[:, V_GS:V_GS + MF] = f["gate_scale"].reshape(MF, P).T
    vecs[:, V_US:V_US + MF] = f["up_scale"].reshape(MF, P).T
    vecs[:MAIN - P, V_MM] = 1.0
    vecs[MAIN - P:, V_MM + 1] = 1.0
    rows = z(P, R_N)
    rows[:, R_DS:R_DS + D] = f["down_scale"]
    rows[:, R_BQ:R_BQ + D] = q["bq"]
    rows[:, R_BO:R_BO + D] = q["bo"]
    rows[:, R_QW:R_QW + HD] = q["qn_w"]
    rows[:, R_QB:R_QB + HD] = q["qn_b"]
    rows[:, R_RB:R_RB + E] = e["router_bias"]
    for c, w, wd in ((R_KW, "kn_w", "kn_dca_w"), (R_KB, "kn_b", "kn_dca_b")):
        rows[:, c:c + HD] = rows[:, c + HD:c + 2 * HD] = q[w]
        rows[MAIN - P:, c + HD:c + 2 * HD] = q[wd]
    rows[:, R_G] = a["g_xattn"][0]
    rows[:, R_G + 1] = a["g_xattn"][1]
    rows[:, R_G + 2] = a["g_ffn"][0]
    rows[:, R_G + 3] = a["g_ffn"][1]
    rows[:, R_KM:R_KM + 8] = [-1, -1, 0, 0] * 2
    rows[MAIN - P:, R_KM + 4:R_KM + 8] = [0, 0, -1, -1]
    rows[:, R_TR:R_TR + E * E] = np.tril(np.ones((E, E), np.float32), -1).ravel()
    gsel = z(2 * E, MG * P)
    for i in range(E):
        gsel[i, i * INTER:(i + 1) * INTER] = gsel[E + i, i * INTER:(i + 1) * INTER] = 1.0
    cst = z(P, P + BCR)
    cst[:, :P] = np.eye(P)
    for i in range(2 * BCR):
        cst[i, P + i % BCR] = 1.0

    arrays = dict(
        x=a["x"], ctxT=a["ctx_1024"].transpose(0, 2, 1), w_in=m["in_proj_w"].T, w_xp=by_k(wxp), w_dt=wdt,
        w_gu=gu, w_dn=by_k(f["down_w"]).reshape(P, MF * D), w_q=by_k(q["Wq"]), w_kv=wkv, w_kvd=wkvd,
        w_o=by_k(q["Wo"]), w_gate=by_k(e["gate_w"].T), w13=w13, w2=by_k(w2), kvb=kvb, vecs=vecs, rows=rows,
        gsel=gsel, cst=cst,
    )
    nc = bacc.Bacc("TRN2", target_bir_lowering=False, num_devices=1)
    aps = {}
    for name, arr in arrays.items():
        arrays[name] = arr = np.ascontiguousarray(arr)
        aps[name] = nc.dram_tensor(f"in_{name}", arr.shape, F32, kind="ExternalInput").ap()
    out = nc.dram_tensor("out", (B, L, D), F32, kind="ExternalOutput").ap()
    build(nc, out=out, **aps)
    r = run_bass_kernel_spmd(nc, [{f"in_{k}": v for k, v in arrays.items()}], core_ids=[0])
    return r.results[0]["out"]
```

```python
from contextlib import ExitStack

import concourse.bass as bass
from concourse import mybir

P = 128
ALU = mybir.AluOpType
ACT = mybir.ActivationFunctionType
F32 = mybir.dt.float32
F32R = mybir.dt.float32r
F8 = mybir.dt.float8e4
U32 = mybir.dt.uint32
AX_X = mybir.AxisListType.X

B, L, D, DC = 4, 256, 256, 128
T2 = L // P
K2 = D // P
NS, DTR, TAPS = 16, 8, 4
FF = 768
MF = FF // P
H, HD = 16, 16
DCA = 16
MAIN = L - DCA
E, INTER, SHARED = 8, 176, 352
HID = E * INTER + SHARED
MM = -(-HID // P)
MG = E * INTER // P
HP = H // 2
LN_EPS, QK_EPS = 1e-5, 1e-6
BCR = 2 * NS
XR = 104

V_CW, V_CB, V_DTB, V_AL, V_D, V_GS, V_US = 0, 8, 10, 12, 44, 46, 52
V_MM, V_N = 58, 60
R_DS, R_BQ, R_BO, R_QW, R_QB, R_RB, R_KW, R_KB, R_G, R_KM, R_TR = 0, 256, 512, 768, 784, 800, 808, 840, 872, 876, 884
R_N = R_TR + E * E

PER = dict(
    zstat=4, zvar=1, zrstd=1, zhat=2, ztanh=1, zg=1,
    xi=1, xpad=1, conv_step=6, conv=2, conv_tanh=1, u=1, xdbl=1, bc_hi=1, bc_lo=2,
    dt_pre=1, sp_abs=2, sp_t=1, sp_ln=1, sp_relu=2, sp_step=6, dt=1, du=1,
    bc=NS, c_sb=NS, dA=2 * NS, dbu=NS, h=NS, p=NS, y_red=NS, ys=2, yT=1, yz=1, x1=1,
    kv_ps=1, kv=1, vst=3, kstep=3, kvar=1, krstd=1, kstack=5, k_m=1, kT_ps=2, kT=2,
    lstat=8, lvar=2, lrstd=2, xh=4, xT_ps=2, xT=1, x_hi=1, x_lo=1,
    gu=MF, g_tanh=MF, g_a=MF, h_ff=MF, down=1, dsc=1, x2=1,
    q_ps=1, q=1, q_hi2=1, qstep=3, qvar=1, qrstd=1, qstack=4, qT_ps=4, qT=4, s_ps=8, mx=16, mstack=2,
    st_ps=H, prob=H, pv=H, o_sb=HP, oT_ps=HP, o_step=2 * HP, ctok=HP,
    cT_ps=1, cT=1, wo_ps=1, xbo=1, x3=1,
    bstat=4, bvar=1, brstd=1, bxh=2, bT_ps=1, bT=1, b_hi=1, b_lo=1, xc=1,
    lg=1, lg_tanh=1, r_step=12, gates=2, gT_ps=1, gT=1,
    h13=MM, gate=MG, y2_part=MM - 1, m_tanh=MM, m_a=MM, m_b=MG, hg=MM, y2=1, xo=1,
)
ONCE = ["early", "later", "ident_r", "ones_set", "zeros_set", "act_step", "pool_step", "setup", "wdt_part", "raw_hi", "raw_lo", "q_clip", "q_big", "q_sum", "q_out", "centred"]


def build(nc, x, ctxT, w_in, w_xp, w_dt, w_gu, w_dn, w_q, w_kv, w_kvd, w_o, w_gate, w13, w2, kvb, vecs, rows, gsel, cst, out):
    with ExitStack() as es:
        def sb(name, shape, dt=F32):
            return es.enter_context(nc.sbuf_tensor(name, shape, dt))

        identR = sb("identR", [P, P], F32R)
        ident = identR[:, :].bitcast(F32)
        vec = sb("vec", [P, V_N])
        row = sb("row", [P, R_N])
        kv_bias = sb("kv_bias", [P, 5, D])
        win = sb("win", [DC, 2 * P])
        wxp = sb("wxp", [P, 2, XR])
        small = sb("small", [P, MG * P + BCR], F32R)
        gselR = small[0:2 * E, 0:MG * P].rearrange("p (m c) -> p m c", m=MG)
        wdt_hi = small[:, 0:2 * P]
        wdt_lo = small[:, 2 * P:4 * P]
        selBC = small[0:2 * BCR, MG * P:MG * P + BCR]
        wgu = sb("wgu", [P, MF, K2, 2, P], F32R)
        wdn = sb("wdn", [P, MF, D])
        wq = sb("wq", [P, K2, D])
        wkv = sb("wkv", [DC, 2 * D])
        wkvd = sb("wkvd", [DC, 2 * D])
        wo = sb("wo", [P, K2, D])
        wgate = sb("wgate", [P, K2, E])
        w13_hi = sb("w13_hi", [P, MM, K2, 2, P], F32R)
        w13_lo = sb("w13_lo", [P, MM, K2, 2, P], F32R)
        w2s = sb("w2s", [P, MM, D])
        negA = sb("negA", [P, 2, NS])
        halfD = sb("halfD", [P, 2])
        gsu = sb("gsu", [P, MF])
        halfgs = sb("halfgs", [P, MF])
        tg = sb("tg", [P, 4])
        tgh = sb("tgh", [P, 1])
        dsb = row[:, R_DS:R_DS + D]
        gbo = row[:, R_BO:R_BO + D]
        qwb = row[:, R_QW:R_QW + 2 * HD].rearrange("p (a c) -> p a c", a=2)
        mhalf = sb("mhalf", [P, 2 * H])

        xin = sb("xin", [P, T2, D])
        ctx = sb("ctx", [DC, L])
        zst = sb("zst", [P, T2, 6])
        zmv = sb("zmv", [P, T2, 2])
        zv = sb("zv", [P, T2])
        zr = sb("zr", [P, T2])
        zg = sb("zg", [P, T2, D])
        xpad = sb("xpad", [P, 2, TAPS - 1 + L])
        cv = sb("cv", [P, 2, L])
        u2 = sb("u2", [P, 2, L])
        stack = sb("stack", [P, L], F32R)
        dt_sb = sb("dt_sb", [P, 2, L])
        du = sb("du", [P, 2, L])
        zh, zt = dt_sb, du
        dA = sb("dA", [P, 2, 2, L])
        hb = sb("hb", [P, 3, 2, L])
        cs = xpad[:, :, TAPS - 1:]
        sp_x = hb[:, 0]
        sp_l = hb[:, 1]
        sp_q = hb[:, 2]
        sp_r = zt
        sp_m = zh[:, :, :].bitcast(U32)
        xa = sb("xa", [P, T2, D])

        ctxR = sb("ctxR", [DC, 3, P])
        xb = sb("xb", [P, T2, D])
        work = sb("work", [P, 10, L])
        xh = sb("xh", [P, T2, D])
        lst = sb("lst", [P, T2, 6])
        lmv = sb("lmv", [P, T2, 2])
        lv = sb("lv", [P, T2])
        lr = sb("lr", [P, T2])
        xT = xh
        xhi = sb("xhi", [P, K2, L], F32R)
        xlo = sb("xlo", [P, K2, L], F32R)
        VW = 2 * (HD + 1)
        vst = sb("vst", [P, T2, H * VW + 64 - VW])
        vsth = [vst[:, t, 0:H * VW].rearrange("p (h c) -> p h c", h=H) for t in range(T2)]
        qk = sb("qk", [P, T2, H, HD])
        sq = xh[:, :, :].rearrange("p t (h c) -> p t h c", h=H)
        hs = sb("hs", [P, 4, T2 * H])
        st = sb("st", [P, T2, H, 64], F32R)
        kT = sb("kT", [P, HP, L], F32R)
        qT = sb("qT", [P, HP, L], F32R)
        mx = sb("mx", [P, T2, H, 2])

        ctok = qk
        rec = sb("rec", [P, 4, 2])
        opr = sb("opr", [P, 4, 2, HD])
        rt = sb("rt", [P, 6, T2, E])
        rs = sb("rs", [P, T2])
        gst = sb("gst", [P, T2, 2 * E], F32R)
        gT = sb("gT", [2 * E, L], F32R)

        xc = sb("xc", [P, T2, D])
        bw = sb("bw", [P, 5, L])
        bxh = bw[:, 0:2, :]
        rk = bw[:, 4, :].rearrange("p (a t f) -> p a t f", a=2, t=T2)
        bst = sb("bst", [P, T2, 6])
        bmv = sb("bmv", [P, T2, 2])
        bv = sb("bv", [P, T2])
        br = sb("br", [P, T2])
        bT = sb("bT", [P, K2, L])
        bhi = sb("bhi", [P, K2, L], F32R)
        blo = sb("blo", [P, K2, L], F32R)
        xo = bT
        RAW = 4
        f8 = xb[:, :, :].rearrange("p t d -> p (t d)").bitcast(F8)[:, 0:3 * 512].rearrange("p (a c) -> p a c", a=3)

        ps = es.enter_context(nc.psum_tensor("ps", [P, 8, 512], F32))
        psR = ps[:, :, :].bitcast(F32R)

        sem = {name: es.enter_context(nc.semaphore(name)) for name in PER}
        once = {name: es.enter_context(nc.semaphore(name)) for name in ONCE}
        raw_in = [es.enter_context(nc.semaphore(f"raw_in{i}")) for i in range(RAW)]
        ctx_in = es.enter_context(nc.semaphore("ctx_in"))
        ctxR_in = es.enter_context(nc.semaphore("ctxR_in"))
        x_in = es.enter_context(nc.semaphore("x_in"))
        stored = es.enter_context(nc.semaphore("stored"))

        def at(name, b, n):
            return sem[name], b * PER[name] + n + 1

        def bank(i, w=512, n=1):
            return ps[:, i:i + n, :].rearrange("p a b -> p (a b)")[:, 0:w]

        chunks = [("w13", m) for m in range(MM)] + [("gu", m) for m in range(MF)] + [("dn", c) for c in range(3)]
        block = es.enter_context(nc.Block())

        QUANT = MF + 3

        def chunk_in(eng, i):
            eng.wait_ge(raw_in[i % RAW], 16 * (i // RAW + 1))

        cident = cv[:, 0, 0:P + BCR]
        EARLY = [(vec[:, :], vecs), (row[:, :], rows), (win[:, :], w_in), (wxp[:, :, :], w_xp), (cident, cst),
                 (du[:, 0, :], w_dt), (hb[0:2 * E].rearrange("p a b c -> p (a b c)")[:, 0:MG * P], gsel)]
        LATER = [(kv_bias[:, :, :], kvb), (wkv[:, :], w_kv), (wkvd[:, :], w_kvd), (wq[:, :, :], w_q),
                 (wgate[:, :, :], w_gate), (wo[:, :, :], w_o), (w2s[:, :, :], w2)]
        ZEROED = 5
        qtmp = bw[:, 0:2, :].rearrange("p a b -> p (a b)")
        b7x = ps[:, 7, :].rearrange("p (k c) -> p k c", k=2)
        b3x = ps[:, 3, :].rearrange("p (k c) -> p k c", k=2)

        def raw(i):
            return work[:, 2 * (i % RAW):2 * (i % RAW) + 2, :].rearrange("p a b -> p (a b)")

        def bankR(i, w, n):
            return psR[:, i:i + n, :].rearrange("p a b -> p (a b)")[:, 0:w]

        T = dict(
            ln0=0.7, xT0=2.6, ffn=5, down=11.1, x2=11.1, xT1=16.7, q=22.3, q2=31.1,
            qT=34.1, scores=39.5, m=54.4, heads=57, wo=70.9, x3=92.6,
            kv=92.9, k2=155.5, kT=145.2,
            bln=1.2, bxT=4.8, router=7.3, gT=9.5, moe=12.6, out=108.6,
            start=2.9, conv=4.7, u=10.5, xproj=13.3, dt=13.9, softplus=16.5, scan=21.4, y=124.8,
            quant=31.3, raw=3,
        )
        DT = dict(ffn=0.48, scores=1.61, heads=1.66, moe=4.79, scan=4.8, quant=5.9, raw=1.93)
        AFTER = 0.96

        def place(b):
            if b < B - 1:
                return [2], 2, [(bw[:, 0, :], bw[:, 1, :], bw[:, 2, :])]
            return [2, 4, 5], 6, [(bw[:, 0, :], bw[:, 1, :], bw[:, 2, :]), (work[:, 0, :], work[:, 1, :], work[:, 2, :])]

        def together(*parts):
            steps = [[next(p), i, p] for i, p in enumerate(parts)]
            while steps:
                step = min(steps, key=lambda s: s[:2])
                step[0] = next(step[2], None)
                if step[0] is None:
                    steps.remove(step)

        def schedule(mamba, keys, attention, mixture, *weights):
            together(mamba(0), keys(0), *(w() for w in weights))
            together(attention(0), mamba(1), keys(1))
            for b in range(2, B):
                together(attention(b - 1), mixture(b - 2), mamba(b), keys(b))
            together(attention(B - 1), mixture(B - 2))
            together(mixture(B - 1))

        @block.sync
        def _(sp):
            def load_ctx(b):
                sp.dma_start(ctx[:, :], ctxT[b]).then_inc(ctx_in, 16)

            def load_x(b):
                sp.dma_start(xin[:, :, :], x[b].rearrange("(t p) d -> p t d", p=P)).then_inc(x_in, 16)

            def load_ctxR(b):
                sp.dma_start(ctxR[:, 0, :], ctxT[b, :, 0:P]).then_inc(ctxR_in, 16)
                sp.dma_start(ctxR[:, 1, 0:MAIN - P], ctxT[b, :, P:MAIN]).then_inc(ctxR_in, 16)
                sp.dma_start(ctxR[:, 2, MAIN - P:P], ctxT[b, :, MAIN:L]).then_inc(ctxR_in, 16)

            def weights():
                yield T["start"] - 1
                for i, (kind, c) in enumerate(chunks):
                    if i == MM + 1:
                        for dst, src in LATER:
                            sp.dma_start(dst, src).then_inc(once["later"], 16)
                    if RAW <= i:
                        if i - RAW < MM:
                            sp.wait_ge(once["raw_lo"], i - RAW + 1)
                        else:
                            sp.wait_ge(once["q_clip"], i - RAW - MM + 1)
                            sp.wait_ge(once["q_big"], 2 * (i - RAW - MM + 1))
                    src = w_gu[:, c] if kind == "gu" else w_dn[:, 512 * c:512 * c + 512] if kind == "dn" else w13[:, c]
                    sp.dma_start(raw(i), src).then_inc(raw_in[i % RAW], 16)

            def mamba(b):
                yield T["xproj"]
                if b + 1 < B:
                    sp.wait_ge(*at("xi", b, 1))
                    load_ctx(b + 1)
                yield T["y"] + 3 * AFTER
                if b + 1 < B:
                    sp.wait_ge(*at("x1", b, 1))
                    load_x(b + 1)

            def keys(b):
                yield T["kT"]
                if b + 1 < B:
                    sp.wait_ge(*at("kv_ps", b, 1))
                    load_ctxR(b + 1)

            def attention(b):
                yield T["wo"]

            def mixture(b):
                yield T["out"] + 3 * AFTER
                sp.wait_ge(*at("xo", b, 1))
                sp.dma_start(out[b].rearrange("(t p) d -> p t d", p=P), xo[:, :, :]).then_inc(stored, 16)

            load_ctx(0)
            for dst, src in EARLY:
                sp.dma_start(dst, src).then_inc(once["early"], 16)
            load_x(0)
            sp.wait_ge(once["zeros_set"], ZEROED)
            load_ctxR(0)
            schedule(mamba, keys, attention, mixture, weights)
            sp.wait_ge(stored, 16 * B)

        @block.gpsimd
        def _(g):
            for name in PER:
                g.sem_inc(sem[name], 1)
            g.memset(ctxR[:, :, :], 0.0).then_inc(once["zeros_set"], 1)
            g.memset(xpad[:, :, :], 0.0).then_inc(once["zeros_set"], 1)
            g.memset(dA[:, :, :, :], 0.0).then_inc(once["zeros_set"], 1)
            g.memset(vst[:, :, :], 0.0).then_inc(once["zeros_set"], 1)
            g.memset(mhalf[:, :], -0.5).then_inc(once["ones_set"], 1)
            g.memset(st[:, :, :, :].bitcast(F32), 0.0).then_inc(once["zeros_set"], 1)
            g.wait_ge(once["early"], 16 * len(EARLY))
            g.wait_ge(once["zeros_set"], ZEROED)
            g.memset(vsth[0][:, :, HD:HD + 1], 1.0).then_inc(once["pool_step"], 1)
            for h in range(H):
                g.tensor_scalar(vsth[1][:, h, HD:HD + 1], vec[:, V_MM:V_MM + 1], 1.0, 0.0, ALU.mult, ALU.add).then_inc(once["pool_step"], 1)
                g.tensor_scalar(vsth[1][:, h, 2 * HD + 1:2 * HD + 2], vec[:, V_MM + 1:V_MM + 2], 1.0, 0.0, ALU.mult, ALU.add).then_inc(once["pool_step"], 1)

            def weights():
                for m in range(MM):
                    yield T["raw"] + DT["raw"] * m
                    g.wait_ge(once["raw_hi"], m + 1)
                    g.tensor_tensor(w13_lo[:, m].rearrange("p k w c -> p (k w c)"), raw(m),
                                    w13_hi[:, m].rearrange("p k w c -> p (k w c)").bitcast(F32), ALU.subtract).then_inc(once["raw_lo"], 1)

            def mamba(b):
                yield T["conv"]
                g.wait_ge(*at("zvar", b, 1))
                g.tensor_tensor(zr[:, :], zv[:, :], mhalf[:, 0:T2], ALU.pow).then_inc(sem["zrstd"], 1)
                for n in range(NS):
                    yield T["scan"] + DT["scan"] * n + AFTER
                    g.wait_ge(*at("h", b, n + 1))
                    g.wait_ge(*at("c_sb", b, n + 1))
                    hn = hb[:, n % 3]
                    cb = cs[:, n % 2, :].rearrange("p (a l) -> p a l", a=1).to_broadcast([P, 2, L])
                    g.tensor_tensor(hn, hn, cb, ALU.mult).then_inc(sem["p"], 1)

            def keys(b):
                yield T["k2"] - 5.5
                g.wait_ge(*at("kvar", b, 1))
                g.tensor_tensor(hs[:, 3, :], hs[:, 2, :], mhalf[:, :], ALU.pow).then_inc(sem["krstd"], 1)

            def attention(b):
                for i, key in enumerate(("ln0", "x2")):
                    yield T[key] + AFTER
                    g.wait_ge(*at("lvar", b, i + 1))
                    g.tensor_tensor(lr[:, :], lv[:, :], mhalf[:, 0:T2], ALU.pow).then_inc(sem["lrstd"], 1)
                yield T["q2"] - 5.5
                g.wait_ge(*at("qvar", b, 1))
                g.tensor_tensor(hs[:, 3, :], hs[:, 2, :], mhalf[:, :], ALU.pow).then_inc(sem["qrstd"], 1)

            def mixture(b):
                yield T["bln"] + AFTER
                g.wait_ge(*at("bvar", b, 1))
                g.tensor_tensor(br[:, :], bv[:, :], mhalf[:, 0:T2], ALU.pow).then_inc(sem["brstd"], 1)

            schedule(mamba, keys, attention, mixture, weights)

        @block.scalar
        def _(a):
            a.wait_ge(once["early"], 16 * len(EARLY))
            al = vec[:, V_AL:V_AL + 2 * NS].rearrange("p (a n) -> p a n", a=2)
            a.activation(negA[:, :, :], al, ACT.Exp).then_inc(once["act_step"], 1)
            a.activation(tg[:, :], row[:, R_G:R_G + 4], ACT.Tanh).then_inc(once["act_step"], 1)
            a.activation(identR[:, :], cident[:, 0:P], ACT.Copy).then_inc(once["ident_r"], 1)
            a.activation(selBC, cident[0:2 * BCR, P:P + BCR], ACT.Copy).then_inc(once["ident_r"], 1)
            a.activation(gselR, hb[0:2 * E].rearrange("p a b c -> p (a b c)")[:, 0:MG * P].rearrange("p (m c) -> p m c", m=MG), ACT.Copy).then_inc(once["ident_r"], 1)
            a.activation(wdt_hi[64:XR], du[64:XR, 0, :], ACT.Copy).then_inc(once["wdt_part"], 1)

            def weights():
                for m in range(MM):
                    yield T["raw"] + DT["raw"] * m
                    chunk_in(a, m)
                    a.activation(w13_hi[:, m].rearrange("p k w c -> p (k w c)"), raw(m), ACT.Copy).then_inc(once["raw_hi"], 1)

            def mamba(b):
                yield T["u"] - AFTER
                a.wait_ge(*at("conv", b, 2))
                a.activation(u2[:, :, :], cv[:, :, :], ACT.Tanh, scale=0.5).then_inc(sem["conv_tanh"], 1)
                a.wait_ge(*at("zhat", b, 2))
                a.wait_ge(*at("y_red", b, 0))
                a.activation(zt[:, :, :], zh[:, :, :], ACT.Tanh, scale=0.5).then_inc(sem["ztanh"], 1)
                yield T["xproj"] + AFTER
                a.wait_ge(*at("xdbl", b, 1))
                a.activation(stack[0:XR, :], ps[0:XR, 0, 0:L], ACT.Copy, scale=0.5).then_inc(sem["bc_hi"], 1)
                yield T["dt"] + AFTER
                a.wait_ge(*at("dt_pre", b, 1))
                a.wait_ge(*at("y_red", b, 0))
                for e in range(2):
                    a.activation(sp_x[:, e, :], ps[:, 1, e * L:e * L + L], ACT.Abs, bias=vec[:, V_DTB + e:V_DTB + e + 1]).then_inc(sem["sp_abs"], 1)
                a.wait_ge(*at("sp_abs", b, 2))
                a.activation(sp_x, sp_x, ACT.Exp, scale=-1.0).then_inc(sem["sp_t"], 1)
                a.wait_ge(*at("sp_t", b, 1))
                a.activation(sp_l, sp_x, ACT.Ln, bias=1.0).then_inc(sem["sp_ln"], 1)
                for n in range(NS):
                    yield T["scan"] + DT["scan"] * n - AFTER
                    if n == 0:
                        a.wait_ge(*at("dt", b, 1))
                    a.wait_ge(*at("bc", b, n + 1))
                    if n >= 2:
                        a.wait_ge(*at("p", b, n - 1))
                    a.activation(cs[:, n % 2, :], ps[:, 0, L:2 * L], ACT.Copy).then_inc(sem["c_sb"], 1)
                    if n >= 2:
                        a.wait_ge(*at("h", b, n - 1))
                    for e in range(2):
                        a.activation(dA[:, n % 2, e, 1:L], dt_sb[:, e, 1:L], ACT.Exp, scale=negA[:, e, n:n + 1]).then_inc(sem["dA"], 1)

            def keys(b):
                yield T["kT"] + AFTER
                for t in range(T2):
                    a.wait_ge(*at("kT_ps", b, t + 1))
                    a.activation(kT[:, :, t * P:t * P + P], bankR(6 - 2 * t, 1024, 2).rearrange("p (j c) -> p j c", j=HP), ACT.Copy).then_inc(sem["kT"], 1)

            def attention(b):
                yield T["xT0"] + AFTER
                a.wait_ge(*at("xT_ps", b, 1))
                a.activation(xhi[:, :, :], b7x, ACT.Copy).then_inc(sem["x_hi"], 1)
                for m in range(MF):
                    yield T["ffn"] + DT["ffn"] * m + AFTER
                    a.wait_ge(*at("gu", b, m + 1))
                    if m >= 2:
                        a.wait_ge(*at("g_a", b, m - 1))
                    a.activation(work[:, m % 2, :], ps[:, 4 + m % 3, 0:L], ACT.Tanh, scale=halfgs[:, m:m + 1]).then_inc(sem["g_tanh"], 1)
                yield T["xT1"] + AFTER / 2
                a.wait_ge(*at("xT_ps", b, 2))
                a.activation(xT[:, :, :], b7x, ACT.Copy).then_inc(sem["xT"], 1)
                for r in range(2):
                    yield (T["m"] if r else T["qT"]) + AFTER
                    for t in range(T2):
                        a.wait_ge(*at("qT_ps", b, 2 * r + t + 1))
                        if r:
                            a.wait_ge(*at("s_ps", b, 8))
                        a.activation(qT[:, :, t * P:t * P + P], bankR(6 - 2 * t, 1024, 2).rearrange("p (j c) -> p j c", j=HP), ACT.Copy).then_inc(sem["qT"], 1)
                for h in range(H + 2):
                    yield T["heads"] + DT["heads"] * h + AFTER / 2
                    if h < H:
                        a.wait_ge(*at("st_ps", b, h + 1))
                        if h >= 4:
                            a.wait_ge(*at("pv", b, h - 3))
                        slot = work[:, 2 * (h % 4):2 * (h % 4) + 2, :].rearrange("p a b -> p (a b)")
                        a.activation(slot, ps[:, 4 + h % 2, :], ACT.Exp).then_inc(sem["prob"], 1)
                    if h >= 3 and h % 2:
                        j = (h - 3) // 2
                        a.wait_ge(*at("pv", b, 2 * j + 2))
                        if j >= 2:
                            a.wait_ge(*at("oT_ps", b, j - 1))
                        a.activation(work[:, 8 + j % 2, :], ps[:, 6 + j % 2, 0:L], ACT.Copy).then_inc(sem["o_sb"], 1)
                yield T["wo"] + AFTER
                a.wait_ge(*at("cT_ps", b, 1))
                a.activation(xT[:, :, :], ps[:, 4, :].rearrange("p (k c) -> p k c", k=K2), ACT.Copy).then_inc(sem["cT"], 1)

            def mixture(b):
                yield T["bln"]
                a.wait_ge(*at("x3", b, 1))
                a.wait_ge(*at("xo", b, 0))
                a.activation(xc[:, :, :], xb[:, :, :], ACT.Copy).then_inc(sem["xc"], 1)
                yield T["bxT"] + AFTER
                if b:
                    a.wait_ge(stored, b * 16)
                a.wait_ge(*at("bT_ps", b, 1))
                a.activation(bT[:, :, :], b3x, ACT.Copy).then_inc(sem["bT"], 1)
                a.activation(bhi[:, :, :], b3x, ACT.Copy).then_inc(sem["b_hi"], 1)
                yield T["router"]
                a.wait_ge(*at("lg", b, 1))
                a.activation(rt[:, 0], ps[:, 2, 0:T2 * E].rearrange("p (t e) -> p t e", t=T2), ACT.Tanh, scale=0.5).then_inc(sem["lg_tanh"], 1)
                yield T["gT"] + AFTER
                a.wait_ge(*at("gT_ps", b, 1))
                a.activation(gT[:, :], psR[0:2 * E, 2, 0:L], ACT.Copy).then_inc(sem["gT"], 1)
                hidden_banks, gate_bank, temps = place(b)
                for m in range(MM):
                    yield T["moe"] + DT["moe"] * m + AFTER
                    a.wait_ge(*at("h13", b, m + 1))
                    if m >= len(temps):
                        a.wait_ge(*at("m_a", b, m - len(temps) + 1))
                    a.activation(temps[m % len(temps)][0], ps[:, hidden_banks[m % len(hidden_banks)], 0:L], ACT.Tanh, scale=0.5).then_inc(sem["m_tanh"], 1)

            schedule(mamba, keys, attention, mixture, weights)

        @block.vector
        def _(v):
            n_setup = 0

            def setup(i):
                nonlocal n_setup
                n_setup += 1
                i.then_inc(once["setup"], 1)
                v.wait_ge(once["setup"], n_setup)

            v.wait_ge(once["early"], 16 * len(EARLY))
            v.wait_ge(once["zeros_set"], ZEROED)
            v.wait_ge(once["act_step"], 2)
            v.wait_ge(once["wdt_part"], 1)
            v.wait_ge(once["ident_r"], 2)
            setup(v.tensor_tensor(wdt_lo[64:XR], du[64:XR, 0, :], wdt_hi[64:XR].bitcast(F32), ALU.subtract))
            setup(v.tensor_scalar(negA[:, :, :], negA[:, :, :], -1.0, None, ALU.mult))
            setup(v.tensor_scalar(halfD[:, :], vec[:, V_D:V_D + 2], 0.5, None, ALU.mult))
            setup(v.tensor_scalar(tgh[:, :], tg[:, 0:1], 0.5, None, ALU.mult))
            setup(v.tensor_scalar(halfgs[:, :], vec[:, V_GS:V_GS + MF], 0.5, None, ALU.mult))
            setup(v.tensor_tensor(gsu[:, :], halfgs[:, :], vec[:, V_US:V_US + MF], ALU.mult))
            setup(v.tensor_scalar(dsb, dsb, tg[:, 2:3], None, ALU.mult))
            setup(v.tensor_scalar(gbo, gbo, tg[:, 1:2], None, ALU.mult))
            setup(v.tensor_scalar(qwb, qwb, HD ** -0.5, None, ALU.mult))

            def weights():
                for i in range(QUANT):
                    yield T["quant"] + DT["quant"] * i
                    kind, c = chunks[MM + i]
                    chunk_in(v, MM + i)
                    r = raw(MM + i)
                    if i:
                        v.wait_ge(once["q_out"], i)
                    v.tensor_scalar(f8[:, 0, :], r, 240.0, -240.0, ALU.min, ALU.max, saturate=False).then_inc(once["q_clip"], 1)
                    v.tensor_scalar(f8[:, 1, :], r, 240.0, 0.5, ALU.max, ALU.mult, saturate=False).then_inc(once["q_big"], 1)
                    v.tensor_scalar(f8[:, 2, :], r, -240.0, 0.5, ALU.min, ALU.mult, saturate=False).then_inc(once["q_big"], 1)
                    v.wait_ge(once["q_big"], 2 * i + 2)
                    v.wait_ge(once["q_clip"], i + 1)
                    v.scalar_tensor_tensor(qtmp, f8[:, 1, :], 2.0, f8[:, 0, :], ALU.mult, ALU.add).then_inc(once["q_sum"], 1)
                    v.wait_ge(once["q_sum"], i + 1)
                    dst = wgu[:, c].rearrange("p k w c -> p (k w c)") if kind == "gu" else wdn[:, 2 * c:2 * c + 2, :].rearrange("p a b -> p (a b)")
                    v.scalar_tensor_tensor(dst, f8[:, 2, :], 2.0, qtmp, ALU.mult, ALU.add).then_inc(once["q_out"], 1)
                yield T["kv"] - 10
                v.wait_ge(once["later"], 16 * len(LATER))
                wide_w = (wq[:, :, :].rearrange("p k (h c) -> p (k h) c", h=H),
                          wkv[:, :].rearrange("p (h c) -> p h c", h=H)[:, :, 0:HD],
                          wkvd[:, :].rearrange("p (h c) -> p h c", h=H)[:, :, 0:HD],
                          kv_bias[:, 0:2, :].rearrange("p t (h c) -> p (t h) c", h=H),
                          row[:, R_BQ:R_BQ + D].rearrange("p (h c) -> p h c", h=H))
                for i, w in enumerate(wide_w):
                    heads = w.shape[1]
                    mean = hs[:, i % 2, 0:heads]
                    if i >= 2:
                        v.wait_ge(once["centred"], 3 * (i - 1))
                    v.tensor_reduce(mean, w, AX_X, ALU.add).then_inc(once["centred"], 1)
                    v.wait_ge(once["centred"], 3 * i + 1)
                    v.tensor_scalar(mean, mean, 1.0 / HD, None, ALU.mult).then_inc(once["centred"], 1)
                    v.wait_ge(once["centred"], 3 * i + 2)
                    v.tensor_tensor(w, w, mean.rearrange("p (h a) -> p h a", a=1).to_broadcast([P, heads, HD]), ALU.subtract).then_inc(once["centred"], 1)

            def mamba(b):
                yield T["start"]
                v.wait_ge(x_in, b * 16 + 16)
                for t in range(T2):
                    v.bn_stats(zst[:, t, :], xin[:, t, :]).then_inc(sem["zstat"], 1)
                v.wait_ge(*at("zstat", b, 2))
                for t in range(T2):
                    v.bn_aggr(zmv[:, t, :], zst[:, t, :]).then_inc(sem["zstat"], 1)
                v.wait_ge(*at("zstat", b, 4))
                v.tensor_scalar(zv[:, :], zmv[:, :, 1], LN_EPS, None, ALU.add).then_inc(sem["zvar"], 1)
                yield T["conv"]
                v.wait_ge(*at("xi", b, 1))
                v.wait_ge(*at("p", b, 0))
                v.tensor_copy(xpad[:, :, TAPS - 1:], ps[:, 0, :].rearrange("p (e l) -> p e l", e=2)).then_inc(sem["xpad"], 1)
                v.wait_ge(*at("xpad", b, 1))
                v.wait_ge(*at("conv_tanh", b, 0))
                for k in range(TAPS):
                    for e in range(2):
                        w = vec[:, V_CW + 4 * e + k:V_CW + 4 * e + k + 1]
                        if k:
                            v.wait_ge(*at("conv_step", b, 2 * (k - 1) + e + 1))
                        if k == 0:
                            i = v.tensor_scalar(cv[:, e, :], xpad[:, e, 0:L], w, vec[:, V_CB + e:V_CB + e + 1], ALU.mult, ALU.add)
                        else:
                            i = v.scalar_tensor_tensor(cv[:, e, :], xpad[:, e, k:k + L], w, cv[:, e, :], ALU.mult, ALU.add)
                        i.then_inc(sem["conv" if k == TAPS - 1 else "conv_step"], 1)
                v.wait_ge(*at("zrstd", b, 1))
                for t in range(T2):
                    v.tensor_scalar(zh[:, t, :], xin[:, t, :], zmv[:, t, 0:1], zr[:, t:t + 1], ALU.subtract, ALU.mult).then_inc(sem["zhat"], 1)
                yield T["u"]
                v.wait_ge(*at("conv_tanh", b, 1))
                v.scalar_tensor_tensor(u2[:, :, :], u2[:, :, :], 1.0, cv[:, :, :], ALU.add, ALU.mult).then_inc(sem["u"], 1)
                v.wait_ge(*at("ztanh", b, 1))
                v.scalar_tensor_tensor(zg[:, :, :], zt[:, :, :], 1.0, zh[:, :, :], ALU.add, ALU.mult).then_inc(sem["zg"], 1)
                yield T["xproj"] + 2 * AFTER
                v.wait_ge(*at("bc_hi", b, 1))
                for r in (BCR, 3 * BCR):
                    hi = stack[r:min(r + BCR, XR), :]
                    v.scalar_tensor_tensor(hi, ps[r:min(r + BCR, XR), 0, 0:L], 0.5, hi.bitcast(F32), ALU.mult, ALU.subtract).then_inc(sem["bc_lo"], 1)
                yield T["softplus"]
                v.wait_ge(*at("dt_pre", b, 1))
                v.wait_ge(*at("zg", b, 1))
                v.wait_ge(*at("sp_abs", b, 2))
                for e in range(2):
                    v.tensor_scalar(sp_r[:, e, :], ps[:, 1, e * L:e * L + L], vec[:, V_DTB + e:V_DTB + e + 1], 0.0, ALU.add, ALU.max).then_inc(sem["sp_relu"], 1)
                yield T["softplus"] + AFTER
                v.wait_ge(*at("sp_t", b, 1))
                v.tensor_scalar(sp_q, sp_x, -0.25, 1.0 / 3.0, ALU.mult, ALU.add).then_inc(sem["sp_step"], 1)
                v.tensor_scalar(sp_m, sp_x, 1.0 / 32.0, None, ALU.is_lt).then_inc(sem["sp_step"], 1)
                v.wait_ge(*at("sp_step", b, 1))
                v.tensor_tensor(sp_q, sp_q, sp_x, ALU.mult).then_inc(sem["sp_step"], 1)
                v.wait_ge(*at("sp_step", b, 3))
                v.scalar_tensor_tensor(sp_q, sp_q, -0.5, sp_x, ALU.add, ALU.mult).then_inc(sem["sp_step"], 1)
                v.wait_ge(*at("sp_step", b, 4))
                v.scalar_tensor_tensor(sp_q, sp_q, 1.0, sp_x, ALU.add, ALU.mult).then_inc(sem["sp_step"], 1)
                yield T["softplus"] + 3 * AFTER
                v.wait_ge(*at("sp_step", b, 5))
                v.wait_ge(*at("sp_ln", b, 1))
                v.copy_predicated(sp_l, sp_m, sp_q).then_inc(sem["sp_step"], 1)
                v.wait_ge(*at("sp_step", b, 6))
                v.wait_ge(*at("sp_relu", b, 2))
                v.tensor_tensor(dt_sb[:, :, :], sp_l, sp_r[:, :, :], ALU.add).then_inc(sem["dt"], 1)
                v.wait_ge(*at("dt", b, 1))
                v.scalar_tensor_tensor(du[:, :, :], dt_sb[:, :, :], 0.5, u2[:, :, :], ALU.mult, ALU.mult).then_inc(sem["du"], 1)
                v.wait_ge(*at("du", b, 1))
                for n in range(NS):
                    yield T["scan"] + DT["scan"] * n
                    hn = hb[:, n % 3]
                    v.wait_ge(*at("c_sb", b, n + 1))
                    if n >= 3:
                        v.wait_ge(*at("y_red", b, n - 2))
                    bb = ps[:, 0, 0:L].rearrange("p (a l) -> p a l", a=1).to_broadcast([P, 2, L])
                    v.tensor_tensor(hn, du[:, :, :], bb, ALU.mult).then_inc(sem["dbu"], 1)
                    v.wait_ge(*at("dbu", b, n + 1))
                    v.wait_ge(*at("dA", b, 2 * n + 2))
                    hf = hn.rearrange("p e l -> p (e l)")
                    v.tensor_tensor_scan(hf, dA[:, n % 2].rearrange("p e l -> p (e l)"), hf, 0.0, ALU.mult, ALU.add).then_inc(sem["h"], 1)
                yield T["y"]
                v.wait_ge(*at("y_red", b, NS))
                for e in range(2):
                    v.scalar_tensor_tensor(cv[:, e, :], u2[:, e, :], halfD[:, e:e + 1], ps[:, 1, e * L:e * L + L], ALU.mult, ALU.add).then_inc(sem["ys"], 1)
                v.wait_ge(*at("ys", b, 2))
                v.tensor_tensor(cv[:, :, :], cv[:, :, :], zg[:, :, :], ALU.mult).then_inc(sem["yz"], 1)
                yield T["y"] + 2 * AFTER
                v.wait_ge(*at("yT", b, 1))
                v.wait_ge(*at("x2", b, 0))
                v.scalar_tensor_tensor(xa[:, :, :], ps[:, 0, :].rearrange("p (t d) -> p t d", t=T2), tgh[:, :], xin[:, :, :], ALU.mult, ALU.add).then_inc(sem["x1"], 1)

            def head_norm(b, key, w, bias, step, var, rstd, last):
                ssq, ve, rs_ = hs[:, 1, :], hs[:, 2, :], hs[:, 3, :]
                v.tensor_tensor(sq, qk[:, :, :, :], qk[:, :, :, :], ALU.mult).then_inc(sem[step], 1)
                v.wait_ge(*at(step, b, 1))
                v.tensor_reduce(ssq, sq, AX_X, ALU.add).then_inc(sem[step], 1)
                v.wait_ge(*at(step, b, 2))
                v.tensor_scalar(ve, ssq, 1.0 / HD, QK_EPS, ALU.mult, ALU.add).then_inc(sem[var], 1)
                yield key
                v.wait_ge(*at(rstd, b, 1))
                v.tensor_tensor(qk[:, :, :, :], qk[:, :, :, :], rs_.rearrange("p (t h a) -> p t h a", t=T2, a=1).to_broadcast([P, T2, H, HD]), ALU.mult).then_inc(sem[step], 1)
                v.wait_ge(*at(step, b, 3))
                v.tensor_tensor(qk[:, :, :, :], qk[:, :, :, :], w, ALU.mult).then_inc(sem[last], 1)
                v.wait_ge(*at(last, b, 1))
                v.tensor_tensor(qk[:, :, :, :], qk[:, :, :, :], bias, ALU.add).then_inc(sem[last], 1)
                v.wait_ge(*at(last, b, 2))

            def keys(b):
                yield T["kv"] + AFTER
                v.wait_ge(*at("kv_ps", b, 1))
                kv = ps[:, 4:6, :].rearrange("p t (h c) -> p t h c", h=H)

                def bias(i, n):
                    return kv_bias[:, i:i + n, :].rearrange("p t (h c) -> p t h c", h=H)

                def by_token(c0):
                    return row[:, c0:c0 + T2 * HD].rearrange("p (t a c) -> p t a c", t=T2, a=1).to_broadcast([P, T2, H, HD])
                v.tensor_tensor(qk[:, :, :, :], kv[:, :, :, 0:HD], bias(0, 2), ALU.add).then_inc(sem["kv"], 1)
                v.tensor_tensor(vsth[0][:, :, 0:HD], kv[:, 0, :, HD:], bias(2, 1)[:, 0], ALU.add).then_inc(sem["vst"], 1)
                for i, c in ((0, 0), (1, HD + 1)):
                    v.scalar_tensor_tensor(vsth[1][:, :, c:c + HD], kv[:, 1, :, HD:], vec[:, V_MM + i:V_MM + i + 1], bias(3 + i, 1)[:, 0], ALU.mult, ALU.add).then_inc(sem["vst"], 1)
                v.wait_ge(*at("kv", b, 1))
                yield from head_norm(b, T["k2"], by_token(R_KW), by_token(R_KB), "kstep", "kvar", "krstd", "kstack")
                v.tensor_copy(st[:, :, :, 0:HD], qk[:, :, :, :]).then_inc(sem["kstack"], 1)
                v.tensor_copy(st[:, :, :, 2 * HD:3 * HD], qk[:, :, :, :]).then_inc(sem["kstack"], 1)
                km = row[:, R_KM:R_KM + T2 * 4].rearrange("p (t a c) -> p t a c", t=T2, a=1).to_broadcast([P, T2, H, 4])
                v.tensor_copy(st[:, :, :, 3 * HD:3 * HD + 4], km).then_inc(sem["k_m"], 1)
                v.wait_ge(*at("kstack", b, 3))
                v.tensor_tensor(st[:, :, :, HD:2 * HD], qk[:, :, :, :], st[:, :, :, 0:HD].bitcast(F32), ALU.subtract).then_inc(sem["kstack"], 1)

            def layer_norm(b, i, key, src, dst, stats, names):
                stat, var, rstd, done = names
                part, mv, ve, rs_ = stats
                for t in range(T2):
                    v.bn_stats(part[:, t, :], src[:, t, :]).then_inc(sem[stat], 1)
                v.wait_ge(*at(stat, b, 4 * i + 2))
                for t in range(T2):
                    v.bn_aggr(mv[:, t, :], part[:, t, :]).then_inc(sem[stat], 1)
                v.wait_ge(*at(stat, b, 4 * i + 4))
                v.tensor_scalar(ve[:, :], mv[:, :, 1], LN_EPS, None, ALU.add).then_inc(sem[var], 1)
                yield key
                v.wait_ge(*at(rstd, b, i + 1))
                for t in range(T2):
                    v.tensor_scalar(dst[:, t, :], src[:, t, :], mv[:, t, 0:1], rs_[:, t:t + 1], ALU.subtract, ALU.mult).then_inc(sem[done], 1)

            def attention(b):
                a_norm = ((lst, lmv, lv, lr), ("lstat", "lvar", "lrstd", "xh"))

                def by_head(i):
                    return qwb[:, i, :].rearrange("p (t a c) -> p t a c", t=1, a=1).to_broadcast([P, T2, H, HD])

                yield T["ln0"]
                v.wait_ge(*at("x1", b, 1))
                yield from layer_norm(b, 0, T["xT0"] - AFTER, xa, xh, *a_norm)
                yield T["xT0"] + 2 * AFTER
                v.wait_ge(*at("x_hi", b, 1))
                v.tensor_tensor(xlo[:, :, :], b7x, xhi[:, :, :].bitcast(F32), ALU.subtract).then_inc(sem["x_lo"], 1)
                for m in range(MF):
                    yield T["ffn"] + DT["ffn"] * m + 2 * AFTER
                    v.wait_ge(*at("g_tanh", b, m + 1))
                    g, u = ps[:, 4 + m % 3, 0:L], ps[:, 4 + m % 3, L:2 * L]
                    v.scalar_tensor_tensor(work[:, 2 + m % 2, :], work[:, m % 2, :], 1.0, g, ALU.add, ALU.mult).then_inc(sem["g_a"], 1)
                    v.wait_ge(*at("g_a", b, m + 1))
                    v.scalar_tensor_tensor(work[:, 4 + m, :], work[:, 2 + m % 2, :], gsu[:, m:m + 1], u, ALU.mult, ALU.mult).then_inc(sem["h_ff"], 1)
                yield T["down"] + AFTER
                v.wait_ge(*at("down", b, 1))
                ds2 = dsb.rearrange("p (a d) -> p a d", a=1).to_broadcast([P, T2, D])
                v.tensor_tensor(xh[:, :, :], b7x, ds2, ALU.mult).then_inc(sem["dsc"], 1)
                v.wait_ge(*at("dsc", b, 1))
                v.wait_ge(*at("xc", b, 0))
                v.tensor_tensor(xb[:, :, :], xh[:, :, :], xa[:, :, :], ALU.add).then_inc(sem["x2"], 1)

                yield T["x2"]
                v.wait_ge(*at("x2", b, 1))
                yield from layer_norm(b, 1, T["xT1"] - AFTER, xb, xh, *a_norm)
                bo2 = gbo.rearrange("p (a d) -> p a d", a=1).to_broadcast([P, T2, D])
                v.wait_ge(*at("xh", b, 4))
                v.tensor_tensor(xb[:, :, :], xb[:, :, :], bo2, ALU.add).then_inc(sem["xbo"], 1)
                yield T["q"]
                v.wait_ge(*at("q_ps", b, 1))
                bq2 = row[:, R_BQ:R_BQ + D].rearrange("p (a d) -> p a d", a=1).to_broadcast([P, T2, D])
                v.tensor_tensor(qk[:, :, :, :].rearrange("p t h c -> p t (h c)"), ps[:, 4, :].rearrange("p (t d) -> p t d", t=T2), bq2, ALU.add).then_inc(sem["q"], 1)
                v.wait_ge(*at("q", b, 1))
                yield from head_norm(b, T["q2"], by_head(0), by_head(1), "qstep", "qvar", "qrstd", "qstack")
                v.tensor_copy(st[:, :, :, 0:HD], qk[:, :, :, :]).then_inc(sem["qstack"], 1)
                v.wait_ge(*at("qstack", b, 3))
                v.tensor_tensor(st[:, :, :, 2 * HD:3 * HD], qk[:, :, :, :], st[:, :, :, 0:HD].bitcast(F32), ALU.subtract).then_inc(sem["qstack"], 1)
                v.tensor_copy(st[:, :, :, HD:2 * HD], qk[:, :, :, :]).then_inc(sem["q_hi2"], 1)
                for i in range(8):
                    yield T["scores"] + DT["scores"] * i + AFTER
                    t, hg = i // 4, i % 4
                    v.wait_ge(*at("s_ps", b, i + 1))
                    sc = bank(4 + 2 * (i % 2), 1024, 2).rearrange("p (b a c) -> p b a c", b=2, a=2)
                    mh = mx[:, t, 4 * hg:4 * hg + 4, :].rearrange("p (a b) w -> p b a w", b=2)
                    v.tensor_reduce(mh[:, :, :, 0], sc[:, :, :, 0:MAIN], AX_X, ALU.max).then_inc(sem["mx"], 1)
                    v.tensor_reduce(mh[:, :, :, 1], sc[:, :, :, MAIN:L], AX_X, ALU.max).then_inc(sem["mx"], 1)
                yield T["m"]
                ms = st[:, :, :, 3 * HD:3 * HD + 4].rearrange("p t h (w a) -> p t h w a", w=2)
                v.wait_ge(*at("mx", b, 16))
                v.wait_ge(*at("qT_ps", b, 2))
                v.tensor_copy(ms[:, :, :, :, 0], mx[:, :, :, :]).then_inc(sem["mstack"], 1)
                v.wait_ge(*at("mstack", b, 1))
                v.tensor_tensor(ms[:, :, :, :, 1], mx[:, :, :, :], ms[:, :, :, :, 0].bitcast(F32), ALU.subtract).then_inc(sem["mstack"], 1)
                for j in range(HP):
                    yield T["heads"] + DT["heads"] * (2 * j + 5)
                    v.wait_ge(*at("oT_ps", b, j + 1))
                    o = ps[:, 6 + j % 2, L:2 * L].rearrange("p (a c) -> p a c", a=4)
                    if j:
                        v.wait_ge(*at("ctok", b, j))
                    o2 = o[:, :, 0:2 * HD + 2].rearrange("p a (w c) -> p a w c", w=2)
                    v.reciprocal(rec[:, :, :], o2[:, :, :, HD]).then_inc(sem["o_step"], 1)
                    v.wait_ge(*at("o_step", b, 2 * j + 1))
                    v.tensor_tensor(opr[:, :, :, :], o2[:, :, :, 0:HD], rec[:, :, :].rearrange("p a (w c) -> p a w c", c=1).to_broadcast([P, 4, 2, HD]), ALU.mult).then_inc(sem["o_step"], 1)
                    v.wait_ge(*at("o_step", b, 2 * j + 2))
                    dst = ctok[:, :, 2 * j:2 * j + 2, :]
                    src = opr[:, :, :, :].rearrange("p (t h) w c -> p t h w c", t=T2)
                    v.tensor_tensor(dst, src[:, :, :, 0], src[:, :, :, 1], ALU.add).then_inc(sem["ctok"], 1)
                yield T["x3"]
                v.wait_ge(*at("wo_ps", b, 1))
                v.wait_ge(*at("xbo", b, 1))
                v.scalar_tensor_tensor(xb[:, :, :], ps[:, 5, :].rearrange("p (t d) -> p t d", t=T2), tg[:, 1:2], xb[:, :, :], ALU.mult, ALU.add).then_inc(sem["x3"], 1)

            def mixture(b):
                yield T["bln"]
                v.wait_ge(*at("x3", b, 1))
                yield from layer_norm(b, 0, T["bxT"] - AFTER, xb, bxh, (bst, bmv, bv, br), ("bstat", "bvar", "brstd", "bxh"))
                yield T["bxT"] + 2 * AFTER
                v.wait_ge(*at("b_hi", b, 1))
                v.tensor_tensor(blo[:, :, :], b3x, bhi[:, :, :].bitcast(F32), ALU.subtract).then_inc(sem["b_lo"], 1)
                yield T["router"] + AFTER
                k_ = 0

                def router(i):
                    nonlocal k_
                    k_ += 1
                    i.then_inc(sem["r_step"], 1)
                    v.wait_ge(*at("r_step", b, k_))
                v.wait_ge(*at("lg_tanh", b, 1))
                score, sel, rank = rt[:, 1], rt[:, 2], rt[:, 3]
                router(v.tensor_scalar(score, rt[:, 0], 0.5, 0.5, ALU.mult, ALU.add))
                rb = row[:, R_RB:R_RB + E].rearrange("p (a e) -> p a e", a=1).to_broadcast([P, T2, E])
                router(v.tensor_tensor(sel, score, rb, ALU.add))
                other = sel.rearrange("p t (a f) -> p t a f", a=1).to_broadcast([P, T2, E, E])
                own = sel.rearrange("p t (e a) -> p t e a", a=1).to_broadcast([P, T2, E, E])
                gt = rk[:, 0].rearrange("p t (e f) -> p t e f", e=E)
                eq = rk[:, 1].rearrange("p t (e f) -> p t e f", e=E)
                router(v.tensor_tensor(gt, other, own, ALU.is_gt))
                router(v.tensor_tensor(eq, other, own, ALU.is_equal))
                tri = row[:, R_TR:R_TR + E * E].rearrange("p (a f) -> p a f", a=1).to_broadcast([P, T2, E * E])
                router(v.tensor_tensor(rk[:, 1], rk[:, 1], tri, ALU.mult))
                router(v.tensor_tensor(rk[:, 0], rk[:, 0], rk[:, 1], ALU.add))
                router(v.tensor_reduce(rank, gt, AX_X, ALU.add))
                router(v.scalar_tensor_tensor(rt[:, 4], rank, 1.5, score, ALU.is_lt, ALU.mult))
                router(v.tensor_reduce(rs[:, :], rt[:, 4], AX_X, ALU.add))
                router(v.tensor_scalar(rs[:, :], rs[:, :], 1e-12, None, ALU.max))
                router(v.reciprocal(rs[:, :], rs[:, :]))
                router(v.tensor_tensor(rt[:, 5], rt[:, 4], rs[:, :].rearrange("p (t a) -> p t a", a=1).to_broadcast([P, T2, E]), ALU.mult))
                v.tensor_copy(gst[:, :, 0:E], rt[:, 5]).then_inc(sem["gates"], 1)
                v.wait_ge(*at("gates", b, 1))
                v.tensor_tensor(gst[:, :, E:2 * E], rt[:, 5], gst[:, :, 0:E].bitcast(F32), ALU.subtract).then_inc(sem["gates"], 1)
                hidden_banks, gate_bank, temps = place(b)
                for m in range(MM):
                    yield T["moe"] + DT["moe"] * m + 2 * AFTER
                    v.wait_ge(*at("m_tanh", b, m + 1))
                    hidden_bank = hidden_banks[m % len(hidden_banks)]
                    h1, h3 = ps[:, hidden_bank, 0:L], ps[:, hidden_bank, L:2 * L]
                    th, t1, t2 = temps[m % len(temps)]
                    hg = bw[:, 3 + m % 2, :]
                    if m >= len(temps):
                        v.wait_ge(*(at("m_b", b, m - len(temps) + 1) if m - len(temps) < MG else at("hg", b, m - len(temps) + 1)))
                    v.scalar_tensor_tensor(t1, th, 1.0, h1, ALU.add, ALU.mult).then_inc(sem["m_a"], 1)
                    v.wait_ge(*at("m_a", b, m + 1))
                    if m < MG:
                        if m >= len(temps):
                            v.wait_ge(*at("hg", b, m - len(temps) + 1))
                        v.scalar_tensor_tensor(t2, t1, 0.5, h3, ALU.mult, ALU.mult).then_inc(sem["m_b"], 1)
                        yield T["moe"] + DT["moe"] * m + 4 * AFTER
                        v.wait_ge(*at("gate", b, m + 1))
                        v.wait_ge(*at("m_b", b, m + 1))
                        if m >= 2:
                            v.wait_ge(*at("y2_part", b, m - 1))
                        v.tensor_tensor(hg, t2, ps[:, gate_bank, 0:L], ALU.mult).then_inc(sem["hg"], 1)
                    else:
                        if m >= 2:
                            v.wait_ge(*at("y2_part", b, m - 1))
                        v.scalar_tensor_tensor(hg, t1, 0.5, h3, ALU.mult, ALU.mult).then_inc(sem["hg"], 1)
                yield T["out"] + 2 * AFTER
                v.wait_ge(*at("y2", b, 1))
                v.wait_ge(*at("xc", b, 1))
                v.scalar_tensor_tensor(xo[:, :, :], b3x, tg[:, 3:4], xc[:, :, :], ALU.mult, ALU.add).then_inc(sem["xo"], 1)

            schedule(mamba, keys, attention, mixture, weights)

        @block.tensor
        def _(pe):
            def transposes(src, dst, id_):
                for i in range(2):
                    for k in range(2):
                        last = pe.transpose(dst(i, k), src[:, i, k * P:k * P + P], id_)
                return last

            def mamba(b):
                yield T["start"]
                pe.wait_ge(ctx_in, b * 16 + 16)
                pe.wait_ge(*at("x1", b, 0))
                for e in range(2):
                    mm = pe.matmul(ps[:, 0, e * L:e * L + L], win[:, e * P:e * P + P], ctx[:, :], start=True, stop=True)
                mm.then_inc(sem["xi"], 1)
                yield T["xproj"]
                pe.wait_ge(*at("u", b, 1))
                for k in range(2):
                    mm = pe.matmul(ps[0:XR, 0, 0:L], wxp[:, k, :], u2[:, k, :], start=(k == 0), stop=(k == 1))
                mm.then_inc(sem["xdbl"], 1)
                yield T["dt"]
                pe.wait_ge(*at("bc_lo", b, 2))
                pe.wait_ge(*at("ys", b, 0))
                pe.wait_ge(once["setup"], 1)
                for e in range(2):
                    o = ps[:, 1, e * L:e * L + L]
                    pe.matmul(o, wdt_hi[64:XR, e * P:e * P + P], stack[64:XR, :], start=True, stop=False)
                    mm = pe.matmul(o, wdt_lo[64:72, e * P:e * P + P], stack[64:72, :], start=False, stop=True)
                mm.then_inc(sem["dt_pre"], 1)

                def spread(n):
                    if n:
                        pe.wait_ge(*at("dbu", b, n))
                        pe.wait_ge(*at("c_sb", b, n))
                    for w in range(2):
                        r = w * NS + n
                        mm = pe.matmul(ps[:, 0, w * L:w * L + L], selBC[:, r:r + 1].to_broadcast([2 * BCR, P]), stack[0:2 * BCR, :], start=True, stop=True)
                    mm.then_inc(sem["bc"], 1)
                for n in range(NS + 3):
                    yield T["scan"] + DT["scan"] * min(n, NS) + AFTER * max(n - NS, 0) - 2 * AFTER
                    if n < NS:
                        spread(n)
                    if n >= 3:
                        k = n - 3
                        pe.wait_ge(*at("p", b, k + 1))
                        pe.matmul(ps[:, 1, :], ident, hb[:, k % 3].rearrange("p e l -> p (e l)"), start=(k == 0), stop=(k == NS - 1)).then_inc(sem["y_red"], 1)
                yield T["y"] + AFTER
                pe.wait_ge(*at("yz", b, 1))
                for e in range(2):
                    for t in range(T2):
                        mm = pe.transpose(ps[:, 0, t * D + e * P:t * D + e * P + P], cv[:, e, t * P:t * P + P], ident)
                mm.then_inc(sem["yT"], 1)

            def stack_transposes(t, done):
                for j in range(HP):
                    src = st[:, t, 2 * j:2 * j + 2, :].rearrange("p h c -> p (h c)")
                    mm = pe.transpose(psR[:, 6 - 2 * t + j // 4, (j % 4) * P:(j % 4) * P + P], src, identR[:, :])
                mm.then_inc(sem[done], 1)

            def keys(b):
                yield T["kv"]
                pe.wait_ge(ctxR_in, b * 48 + 48)
                pe.wait_ge(*at("x3", b, 0))
                pe.wait_ge(once["later"], 16 * len(LATER))
                pe.wait_ge(once["centred"], 15)
                pe.matmul(ps[:, 4, :], ctxR[:, 0, :], wkv[:, :], start=True, stop=True)
                pe.matmul(ps[:, 5, :], ctxR[:, 1, :], wkv[:, :], start=True, stop=False)
                pe.matmul(ps[:, 5, :], ctxR[:, 2, :], wkvd[:, :], start=False, stop=True).then_inc(sem["kv_ps"], 1)
                yield T["kT"]
                pe.wait_ge(*at("kstack", b, 5))
                pe.wait_ge(*at("k_m", b, 1))
                pe.wait_ge(*at("vst", b, 3))
                for t in range(T2):
                    stack_transposes(t, "kT_ps")

            def xh_transposes(b, i):
                pe.wait_ge(*at("xh", b, 2 * i + 2))
                for t in range(T2):
                    for k in range(K2):
                        mm = pe.transpose(b7x[:, k, t * P:t * P + P], xh[:, t, k * P:k * P + P], ident)
                mm.then_inc(sem["xT_ps"], 1)

            def attention(b):
                yield T["xT0"]
                pe.wait_ge(*at("kT", b, 2))
                xh_transposes(b, 0)

                def down(m):
                    pe.wait_ge(*at("h_ff", b, m + 1))
                    for t in range(T2):
                        mm = pe.matmul(ps[:, 7, t * D:t * D + D], work[:, 4 + m, t * P:t * P + P], wdn[:, m, :],
                                       start=(m == 0 and t == 0), stop=(m == MF - 1), skip_group_check=True)
                    if m == MF - 1:
                        mm.then_inc(sem["down"], 1)
                if b == 0:
                    pe.wait_ge(once["q_out"], QUANT)
                for m in range(MF):
                    yield T["ffn"] + DT["ffn"] * m
                    if m == 0:
                        pe.wait_ge(*at("x_lo", b, 1))
                    if m >= 3:
                        pe.wait_ge(*at("h_ff", b, m - 2))
                    for w in range(2):
                        o = ps[:, 4 + m % 3, w * L:w * L + L]
                        for k in range(K2):
                            pe.matmul(o, wgu[:, m, k, w, :], xhi[:, k, :], start=(k == 0), stop=False)
                        for k in range(K2):
                            mm = pe.matmul(o, wgu[:, m, k, w, :], xlo[:, k, :], start=False, stop=(k == K2 - 1))
                    mm.then_inc(sem["gu"], 1)
                    if m >= 2:
                        down(m - 2)
                yield T["down"]
                down(MF - 2)
                down(MF - 1)

                yield T["xT1"]
                pe.wait_ge(*at("dsc", b, 1))
                xh_transposes(b, 1)
                yield T["xT1"] + AFTER
                pe.wait_ge(*at("xT", b, 1))
                for t in range(T2):
                    for k in range(K2):
                        mm = pe.matmul(ps[:, 4, t * D:t * D + D], xT[:, k, t * P:t * P + P], wq[:, k, :], start=(k == 0), stop=(k == K2 - 1))
                mm.then_inc(sem["q_ps"], 1)
                yield T["qT"]
                pe.wait_ge(*at("q_hi2", b, 1))
                pe.wait_ge(*at("qstack", b, 4))
                for t in range(T2):
                    stack_transposes(t, "qT_ps")

                def rows_of(t_, h, n):
                    return t_[64 * (h % 2):64 * (h % 2) + n, h // 2, :]
                for i in range(8):
                    yield T["scores"] + DT["scores"] * i
                    t, hg = i // 4, i % 4
                    if i == 0:
                        pe.wait_ge(*at("qT", b, 2))
                    if i >= 2:
                        pe.wait_ge(*at("mx", b, 2 * (i - 1)))
                    for h in range(4):
                        hh = 4 * hg + h
                        mm = pe.matmul(ps[:, 4 + 2 * (i % 2) + h % 2, (h // 2) * L:(h // 2) * L + L],
                                       rows_of(qT, hh, 3 * HD)[:, t * P:t * P + P], rows_of(kT, hh, 3 * HD), start=True, stop=True)
                    mm.then_inc(sem["s_ps"], 1)
                yield T["m"] + AFTER / 2
                pe.wait_ge(*at("mstack", b, 2))
                for t in range(T2):
                    stack_transposes(t, "qT_ps")
                for h in range(H + 3):
                    yield T["heads"] + DT["heads"] * h
                    if h == 0:
                        pe.wait_ge(*at("qT", b, 4))
                    if h < H:
                        if h >= 2:
                            pe.wait_ge(*at("prob", b, h - 1))
                        for kt in range(T2):
                            mm = pe.matmul(ps[:, 4 + h % 2, kt * L:kt * L + L], rows_of(kT, h, 3 * HD + 4)[:, kt * P:kt * P + P],
                                           rows_of(qT, h, 3 * HD + 4), start=True, stop=True)
                        mm.then_inc(sem["st_ps"], 1)
                    if 2 <= h < H + 2:
                        g = h - 2
                        pe.wait_ge(*at("prob", b, g + 1))
                        if g >= 4 and g % 2 == 0:
                            pe.wait_ge(*at("o_step", b, g - 2))
                        for kt in range(T2):
                            mm = pe.matmul(ps[64 * (g % 2):64 * (g % 2) + 64, 6 + g // 2 % 2, 0:L], vst[:, kt, VW * g:VW * g + 64],
                                           work[:, 2 * (g % 4) + kt, :], start=(kt == 0), stop=(kt == 1))
                        mm.then_inc(sem["pv"], 1)
                    if h >= 4 and h % 2 == 0:
                        j = (h - 4) // 2
                        pe.wait_ge(*at("o_sb", b, j + 1))
                        for t in range(T2):
                            mm = pe.transpose(ps[:, 6 + j % 2, L + t * P:L + t * P + P], work[:, 8 + j % 2, t * P:t * P + P], ident)
                        mm.then_inc(sem["oT_ps"], 1)
                yield T["wo"]
                pe.wait_ge(*at("ctok", b, HP))
                for t in range(T2):
                    for k in range(K2):
                        mm = pe.transpose(ps[:, 4, k * L + t * P:k * L + t * P + P], ctok[:, t, 8 * k:8 * k + 8, :].rearrange("p h c -> p (h c)"), ident)
                mm.then_inc(sem["cT_ps"], 1)
                yield T["wo"] + 1.5 * AFTER
                pe.wait_ge(*at("cT", b, 1))
                for t in range(T2):
                    for k in range(K2):
                        mm = pe.matmul(ps[:, 5, t * D:t * D + D], xT[:, k, t * P:t * P + P], wo[:, k, :], start=(k == 0), stop=(k == K2 - 1))
                mm.then_inc(sem["wo_ps"], 1)

            def mixture(b):
                yield T["bxT"]
                pe.wait_ge(*at("xo", b, 0))
                pe.wait_ge(*at("bxh", b, 2))
                for t in range(T2):
                    for k in range(K2):
                        mm = pe.transpose(b3x[:, k, t * P:t * P + P], bxh[:, t, k * P:k * P + P], ident)
                mm.then_inc(sem["bT_ps"], 1)
                yield T["bxT"] + 1.5 * AFTER
                pe.wait_ge(*at("bT", b, 1))
                for t in range(T2):
                    for k in range(K2):
                        mm = pe.matmul(ps[:, 2, t * E:t * E + E], bT[:, k, t * P:t * P + P], wgate[:, k, :], start=(k == 0), stop=(k == K2 - 1))
                mm.then_inc(sem["lg"], 1)
                yield T["gT"]
                pe.wait_ge(*at("lg_tanh", b, 1))
                pe.wait_ge(*at("gates", b, 2))
                for t in range(T2):
                    mm = pe.transpose(psR[0:2 * E, 2, t * P:t * P + P], gst[:, t, :], identR[:, :])
                mm.then_inc(sem["gT_ps"], 1)
                yield T["moe"] - AFTER / 4
                pe.wait_ge(*at("gT", b, 1))
                pe.wait_ge(*at("b_lo", b, 1))
                if b == 0:
                    pe.wait_ge(once["raw_lo"], MM)
                hidden_banks, gate_bank, temps = place(b)

                def second(m):
                    pe.wait_ge(*at("hg", b, m + 1))
                    for t in range(T2):
                        mm = pe.matmul(ps[:, 3, t * D:t * D + D], bw[:, 3 + m % 2, t * P:t * P + P], w2s[:, m, :],
                                       start=(m == 0 and t == 0), stop=(m == MM - 1), skip_group_check=True)
                    mm.then_inc(sem["y2" if m == MM - 1 else "y2_part"], 1)
                for m in range(MM):
                    yield T["moe"] + DT["moe"] * m
                    hidden_bank = hidden_banks[m % len(hidden_banks)]
                    if m >= len(hidden_banks):
                        pe.wait_ge(*at("hg", b, m - len(hidden_banks) + 1))
                    for w in range(2):
                        o = ps[:, hidden_bank, w * L:w * L + L]
                        for k in range(K2):
                            pe.matmul(o, w13_hi[:, m, k, w, :], bhi[:, k, :], start=(k == 0), stop=False)
                            pe.matmul(o, w13_hi[:, m, k, w, :], blo[:, k, :], start=False, stop=False)
                            mm = pe.matmul(o, w13_lo[:, m, k, w, :], bhi[:, k, :], start=False, stop=(k == K2 - 1))
                    mm.then_inc(sem["h13"], 1)
                    if m >= 2:
                        second(m - 2)
                    if m < MG:
                        yield T["moe"] + DT["moe"] * m + 3 * AFTER
                        if gate_bank == hidden_bank:
                            pe.wait_ge(*at("m_b", b, m + 1))
                        elif m:
                            pe.wait_ge(*at("hg", b, m))
                        pe.matmul(ps[:, gate_bank, 0:L], gselR[:, m, :], gT[:, :], start=True, stop=True).then_inc(sem["gate"], 1)
                yield T["out"]
                second(MM - 2)
                second(MM - 1)

            pe.wait_ge(once["early"], 16 * len(EARLY))
            pe.wait_ge(once["ident_r"], 3)
            schedule(mamba, keys, attention, mixture)


def by_k(w):
    k, n = w.shape
    return w.reshape(k // P, P, n).transpose(1, 0, 2)


def kernel(**inputs):
    import numpy as np
    import concourse.bacc as bacc
    from concourse.bass_utils import run_bass_kernel_spmd

    a = {k: np.asarray(v) for k, v in inputs.items()}
    m = {k[len("L0_xattn_"):]: v for k, v in a.items() if k.startswith("L0_xattn_")}
    f = {k[len("L0_ffn_"):]: v for k, v in a.items() if k.startswith("L0_ffn_")}
    q = {k[len("L1_xattn_"):]: v for k, v in a.items() if k.startswith("L1_xattn_")}
    e = {k[len("L1_ffn_"):]: v for k, v in a.items() if k.startswith("L1_ffn_")}
    z = lambda *s: np.zeros(s, np.float32)

    xp = m["x_proj_w"].T
    wxp = z(D, XR)
    wxp[:, 0:BCR] = wxp[:, BCR:2 * BCR] = xp[:, DTR:]
    wxp[:, 64:64 + DTR] = wxp[:, 96:96 + DTR] = xp[:, :DTR]
    wdt = z(P, D)
    wdt[64:64 + DTR] = wdt[96:96 + DTR] = m["dt_proj_w"].T

    gu = np.stack([by_k(f["gate_w"]), by_k(f["up_w"])], 2)
    gu = gu.reshape(P, K2, 2, MF, P).transpose(0, 3, 1, 2, 4).reshape(P, MF, 512)
    w1, w3, w2 = z(D, MM * P), z(D, MM * P), z(MM * P, D)
    w1[:, :HID] = np.concatenate([e["W1"].transpose(1, 0, 2).reshape(D, E * INTER), e["sw1"].T], 1)
    w3[:, :HID] = np.concatenate([e["W3"].transpose(1, 0, 2).reshape(D, E * INTER), e["sw3"].T], 1)
    w2[:HID] = np.concatenate([e["W2"].reshape(E * INTER, D), e["sw2"].T], 0)
    w13 = np.stack([by_k(w1), by_k(w3)], 2).reshape(P, K2, 2, MM, P).transpose(0, 3, 1, 2, 4).reshape(P, MM, 512)

    def heads(k, v):
        return np.stack([k.reshape(-1, H, HD), v.reshape(-1, H, HD)], 2).reshape(-1, 2 * D)

    def heads_apart(c):
        return c.reshape(H, 2, HD).transpose(1, 0, 2).reshape(2, D)
    wkv = np.concatenate([q["Wk"], q["Wv"]], 1)
    wkvd = heads(q["Wkv_dca"][:, :D], q["Wkv_dca"][:, D:])
    kvb = z(P, 5, D)
    hb = heads_apart(np.concatenate([q["bk"], q["bv"]]))
    kvb[:, 0:2], kvb[:, 2:4] = hb[0], hb[1]
    kvb[MAIN - P:, 1], kvb[MAIN - P:, 3], kvb[MAIN - P:, 4] = q["bkv_dca"][:D], 0.0, q["bkv_dca"][D:]

    vecs = z(P, V_N)
    for i in range(2):
        s = slice(i * P, i * P + P)
        vecs[:, V_CW + 4 * i:V_CW + 4 * i + 4] = m["conv_w"][s, 0]
        vecs[:, V_CB + i] = m["conv_b"][s]
        vecs[:, V_DTB + i] = m["dt_proj_b"][s]
        vecs[:, V_AL + NS * i:V_AL + NS * i + NS] = m["A_log"][s]
        vecs[:, V_D + i] = m["D"][s]
    vecs[:, V_GS:V_GS + MF] = f["gate_scale"].reshape(MF, P).T
    vecs[:, V_US:V_US + MF] = f["up_scale"].reshape(MF, P).T
    vecs[:MAIN - P, V_MM] = 1.0
    vecs[MAIN - P:, V_MM + 1] = 1.0
    rows = z(P, R_N)
    rows[:, R_DS:R_DS + D] = f["down_scale"]
    rows[:, R_BQ:R_BQ + D] = q["bq"]
    rows[:, R_BO:R_BO + D] = q["bo"]
    rows[:, R_QW:R_QW + HD] = q["qn_w"]
    rows[:, R_QB:R_QB + HD] = q["qn_b"]
    rows[:, R_RB:R_RB + E] = e["router_bias"]
    for c, w, wd in ((R_KW, "kn_w", "kn_dca_w"), (R_KB, "kn_b", "kn_dca_b")):
        rows[:, c:c + HD] = rows[:, c + HD:c + 2 * HD] = q[w]
        rows[MAIN - P:, c + HD:c + 2 * HD] = q[wd]
    rows[:, R_G] = a["g_xattn"][0]
    rows[:, R_G + 1] = a["g_xattn"][1]
    rows[:, R_G + 2] = a["g_ffn"][0]
    rows[:, R_G + 3] = a["g_ffn"][1]
    rows[:, R_KM:R_KM + 8] = [-1, -1, 0, 0] * 2
    rows[MAIN - P:, R_KM + 4:R_KM + 8] = [0, 0, -1, -1]
    rows[:, R_TR:R_TR + E * E] = np.tril(np.ones((E, E), np.float32), -1).ravel()
    gsel = z(2 * E, MG * P)
    for i in range(E):
        gsel[i, i * INTER:(i + 1) * INTER] = gsel[E + i, i * INTER:(i + 1) * INTER] = 1.0
    cst = z(P, P + BCR)
    cst[:, :P] = np.eye(P)
    for i in range(2 * BCR):
        cst[i, P + i % BCR] = 1.0

    arrays = dict(
        x=a["x"], ctxT=a["ctx_1024"].transpose(0, 2, 1), w_in=m["in_proj_w"].T, w_xp=by_k(wxp), w_dt=wdt,
        w_gu=gu, w_dn=by_k(f["down_w"]).reshape(P, MF * D), w_q=by_k(q["Wq"]), w_kv=wkv, w_kvd=wkvd,
        w_o=by_k(q["Wo"]), w_gate=by_k(e["gate_w"].T), w13=w13, w2=by_k(w2), kvb=kvb, vecs=vecs, rows=rows,
        gsel=gsel, cst=cst,
    )
    nc = bacc.Bacc("TRN2", target_bir_lowering=False, num_devices=1)
    aps = {}
    for name, arr in arrays.items():
        arrays[name] = arr = np.ascontiguousarray(arr)
        aps[name] = nc.dram_tensor(f"in_{name}", arr.shape, F32, kind="ExternalInput").ap()
    out = nc.dram_tensor("out", (B, L, D), F32, kind="ExternalOutput").ap()
    build(nc, out=out, **aps)
    r = run_bass_kernel_spmd(nc, [{f"in_{k}": v for k, v in arrays.items()}], core_ids=[0])
    return r.results[0]["out"]
```

```python
from contextlib import ExitStack

import concourse.bass as bass
from concourse import mybir

P = 128
ALU = mybir.AluOpType
ACT = mybir.ActivationFunctionType
F32 = mybir.dt.float32
F32R = mybir.dt.float32r
F8 = mybir.dt.float8e4
U32 = mybir.dt.uint32
AX_X = mybir.AxisListType.X

B, L, D, DC = 4, 256, 256, 128
T2 = L // P
K2 = D // P
NS, DTR, TAPS = 16, 8, 4
FF = 768
MF = FF // P
H, HD = 16, 16
DCA = 16
MAIN = L - DCA
E, INTER, SHARED = 8, 176, 352
HID = E * INTER + SHARED
MM = -(-HID // P)
MG = E * INTER // P
HP = H // 2
LN_EPS, QK_EPS = 1e-5, 1e-6
BCR = 2 * NS
XR = 104

V_CW, V_CB, V_DTB, V_AL, V_D, V_GS, V_US = 0, 8, 10, 12, 44, 46, 52
V_MM, V_N = 58, 60
R_DS, R_BQ, R_BO, R_QW, R_QB, R_RB, R_KW, R_KB, R_G, R_KM, R_TR = 0, 256, 512, 768, 784, 800, 808, 840, 872, 876, 884
R_N = R_TR + E * E

PER = dict(
    zstat=4, zvar=1, zrstd=1, zhat=2, ztanh=1, zg=1,
    xi=1, xpad=1, conv_step=6, conv=2, conv_tanh=1, u=1, xdbl=1, bc_hi=1, bc_lo=2,
    dt_pre=1, sp_abs=2, sp_t=1, sp_ln=1, sp_relu=2, sp_step=6, dt=1, du=1,
    bc=NS, b_sb=NS, c_sb=NS, dA=2 * NS, dbu=NS, h=NS, p=NS, p_pair=NS // 2, y_red=NS // 2, ys=2, yT=1, yz=1, x1=1,
    kv_ps=1, kv=1, vst=3, kstep=6, kvar=1, kln=1, krstd=1, kstack=5, k_m=1, kT_ps=2, kT=2,
    lstat=8, lvar=2, lrstd=2, xh=4, xT_ps=2, xT=1, x_hi=1, x_lo=1,
    gu=MF, g_tanh=MF, g_a=MF, h_ff=MF, down=1, dsc=1, x2=1,
    q_ps=1, q=1, q_hi2=1, qstep=6, qvar=1, qln=1, qrstd=1, qstack=4, qT_ps=4, qT=4, s_ps=8, mx=16, mstack=2,
    st_ps=H, prob=H, pv=H, o_sb=HP, oT_ps=HP, o_step=2 * HP, ctok=HP,
    cT_ps=1, cT=1, wo_ps=1, xbo=1, x3=1,
    bstat=4, bvar=1, brstd=1, bxh=2, bT_ps=1, bT=1, b_hi=1, b_lo=1, xc=1,
    lg=1, lg_tanh=1, r_step=12, gates=2, gT_ps=1, gT=1,
    h13=MM, gate=MG, y2_part=MM - 1, m_tanh=MM, m_a=MM, m_b=MG, hg=MM, y2=1, xo=1,
)
ONCE = ["early", "early_too", "last", "later", "ident_r", "ones_set", "zeros_set", "act_step", "pool_step", "setup", "wdt_part", "raw_hi", "raw_lo", "q_clip", "q_big", "q_wide", "q_sum", "q_out", "centred"]


def build(nc, x, ctxT, w_in, w_xp, w_dt, w_gu, w_dn, w_q, w_kv, w_kvd, w_o, w_gate, w13, w2, kvb, vecs, rows, gsel, cst, out):
    with ExitStack() as es:
        def sb(name, shape, dt=F32):
            return es.enter_context(nc.sbuf_tensor(name, shape, dt))

        identR = sb("identR", [P, P], F32R)
        ident = identR[:, :].bitcast(F32)
        vec = sb("vec", [P, V_N])
        row = sb("row", [P, R_N])
        kv_bias = sb("kv_bias", [P, 5, D])
        win = sb("win", [DC, 2 * P])
        wxp = sb("wxp", [P, 2, XR])
        small = sb("small", [P, MG * P + BCR], F32R)
        gselR = small[0:2 * E, 0:MG * P].rearrange("p (m c) -> p m c", m=MG)
        wdt_hi = small[:, 0:2 * P]
        wdt_lo = small[:, 2 * P:4 * P]
        selBC = small[0:2 * BCR, MG * P:MG * P + BCR]
        wgu = sb("wgu", [P, MF, K2, 2, P], F32R)
        wdn = sb("wdn", [P, MF, D])
        wq = sb("wq", [P, K2, D])
        wkv = sb("wkv", [DC, 2 * D])
        wkvd = sb("wkvd", [DC, 2 * D])
        wo = sb("wo", [P, K2, D])
        wgate = sb("wgate", [P, K2, E])
        w13_hi = sb("w13_hi", [P, MM, K2, 2, P], F32R)
        w13_lo = sb("w13_lo", [P, MM, K2, 2, P], F32R)
        w2s = sb("w2s", [P, MM, D])
        negA = sb("negA", [P, 2, NS])
        halfD = sb("halfD", [P, 2])
        gsu = sb("gsu", [P, MF])
        halfgs = sb("halfgs", [P, MF])
        tg = sb("tg", [P, 4])
        tgh = sb("tgh", [P, 1])
        dsb = row[:, R_DS:R_DS + D]
        gbo = row[:, R_BO:R_BO + D]
        qwb = row[:, R_QW:R_QW + 2 * HD].rearrange("p (a c) -> p a c", a=2)
        mhalf = sb("mhalf", [P, T2])

        xin = sb("xin", [P, T2, D])
        ctx = sb("ctx", [DC, L])
        zst = sb("zst", [P, T2, 6])
        zmv = sb("zmv", [P, T2, 2])
        zv = sb("zv", [P, T2])
        zr = sb("zr", [P, T2])
        zg = sb("zg", [P, T2, D])
        xpad = sb("xpad", [P, 2, TAPS - 1 + L])
        cv = sb("cv", [P, 2, L])
        u2 = sb("u2", [P, 2, L])
        stack = sb("stack", [P, L], F32R)
        dt_sb = sb("dt_sb", [P, 2, L])
        du = sb("du", [P, 2, L])
        zh, zt = dt_sb, du
        dA = sb("dA", [P, 2, 2, L])
        hb = sb("hb", [P, 3, 2, L])
        bs = ctx
        cs = xpad[:, :, TAPS - 1:]
        sp_x = hb[:, 0]
        sp_l = hb[:, 1]
        sp_q = hb[:, 2]
        sp_r = zt
        sp_m = zh[:, :, :].bitcast(U32)
        xa = sb("xa", [P, T2, D])

        ctxR = sb("ctxR", [DC, 3, P])
        xb = sb("xb", [P, T2, D])
        work = sb("work", [P, 10, L])
        xh = sb("xh", [P, T2, D])
        lst = sb("lst", [P, T2, 6])
        lmv = sb("lmv", [P, T2, 2])
        lv = sb("lv", [P, T2])
        lr = sb("lr", [P, T2])
        xT = xh
        xhi = sb("xhi", [P, K2, L], F32R)
        xlo = sb("xlo", [P, K2, L], F32R)
        VW = 2 * (HD + 1)
        vst = sb("vst", [P, T2, H * VW + 64 - VW])
        vsth = [vst[:, t, 0:H * VW].rearrange("p (h c) -> p h c", h=H) for t in range(T2)]
        qk = sb("qk", [P, T2, H, HD])
        sq = xh[:, :, :].rearrange("p t (h c) -> p t h c", h=H)
        hs = sb("hs", [P, 4, T2 * H])
        st = sb("st", [P, T2, H, 64], F32R)
        kT = sb("kT", [P, HP, L], F32R)
        qT = sb("qT", [P, HP, L], F32R)
        mx = sb("mx", [P, T2, H, 2])

        ctok = qk
        rec = sb("rec", [P, 4, 2])
        opr = sb("opr", [P, 4, 2, HD])
        rt = sb("rt", [P, 6, T2, E])
        rs = sb("rs", [P, T2])
        gst = sb("gst", [P, T2, 2 * E], F32R)
        gT = sb("gT", [2 * E, L], F32R)

        xc = sb("xc", [P, T2, D])
        bw = sb("bw", [P, 5, L])
        bxh = bw[:, 0:2, :]
        rk = bw[:, 4, :].rearrange("p (a t f) -> p a t f", a=2, t=T2)
        bst = sb("bst", [P, T2, 6])
        bmv = sb("bmv", [P, T2, 2])
        bv = sb("bv", [P, T2])
        br = sb("br", [P, T2])
        bT = sb("bT", [P, K2, L])
        bhi = sb("bhi", [P, K2, L], F32R)
        blo = sb("blo", [P, K2, L], F32R)
        xo = bT
        RAW = 4
        f8 = xb[:, :, :].rearrange("p t d -> p (t d)").bitcast(F8)[:, 0:3 * 512].rearrange("p (a c) -> p a c", a=3)

        ps = es.enter_context(nc.psum_tensor("ps", [P, 8, 512], F32))
        psR = ps[:, :, :].bitcast(F32R)

        sem = {name: es.enter_context(nc.semaphore(name)) for name in PER}
        once = {name: es.enter_context(nc.semaphore(name)) for name in ONCE}
        raw_in = [es.enter_context(nc.semaphore(f"raw_in{i}")) for i in range(RAW)]
        ctx_in = es.enter_context(nc.semaphore("ctx_in"))
        ctxR_in = es.enter_context(nc.semaphore("ctxR_in"))
        x_in = es.enter_context(nc.semaphore("x_in"))
        stored = es.enter_context(nc.semaphore("stored"))

        def at(name, b, n):
            return sem[name], b * PER[name] + n + 1

        def bank(i, w=512, n=1):
            return ps[:, i:i + n, :].rearrange("p a b -> p (a b)")[:, 0:w]

        chunks = [("w13", m) for m in range(MM)] + [("gu", m) for m in range(MF)] + [("dn", c) for c in range(3)]
        block = es.enter_context(nc.Block())

        QUANT = MF + 3

        def chunk_in(eng, i):
            eng.wait_ge(raw_in[i % RAW], 16 * (i // RAW + 1))

        cident = cv[:, 0, 0:P + BCR]
        EARLY = [(vec[:, :], vecs), (win[:, :], w_in), (cident, cst), (wxp[:, :, :], w_xp)]
        EARLY_TOO = [(xc[:, 0, :], w_dt), (row[:, :], rows), (hb[0:2 * E].rearrange("p a b c -> p (a b c)")[:, 0:MG * P], gsel)]
        LATER = [(wkv[:, :], w_kv), (wkvd[:, :], w_kvd), (kv_bias[:, :, :], kvb), (wq[:, :, :], w_q)]
        LAST = [(wo[:, :, :], w_o), (wgate[:, :, :], w_gate), (w2s[:, :, :], w2)]
        ZEROED = 5
        q0, q1, q2 = (w[:, 0:2, :].rearrange("p a b -> p (a b)") for w in (xc, bT, bw))
        b7x = ps[:, 7, :].rearrange("p (k c) -> p k c", k=2)
        b3x = ps[:, 3, :].rearrange("p (k c) -> p k c", k=2)

        def raw(i):
            return work[:, 2 * (i % RAW):2 * (i % RAW) + 2, :].rearrange("p a b -> p (a b)")

        def bankR(i, w, n):
            return psR[:, i:i + n, :].rearrange("p a b -> p (a b)")[:, 0:w]

        PLACES = [
            dict(kv=79.4, k2=94.9, kT=143,
                 start=35.6, conv=12.3, u=23.7, xproj=14.9, dt=31.9, softplus=24.8, scan=28.1, d_scan=4.23, y=154.5,
                 l_spread=0.17, l_copy=2.37, l_du=0.5, l_p=0.25,
                 raw=13.8, d_raw=2.8, quant=49.6, d_quant=5.99, centre=72.4),
            dict(ln0=0, xT0=0, ffn=9.5, down=18.7, x2=2.8, xT1=24.5, q=28.4, q2=36.7,
                 qT=45.2, scores=44.6, m=64.6, heads=67.5, wo=96.1, x3=98.3, d_ffn=0.29, d_scores=2.09, d_heads=1.48,
                 l_exp=1.41, l_o=0.53, l_mx=0.17, l_fa=0.08, l_fv=1.3,
                 kv=101.1, k2=138.7, kT=151.5,
                 start=1.4, conv=2.5, u=11.7, xproj=11.7, dt=21.9, softplus=21.1, scan=28.1, d_scan=5.22, y=146.5,
                 l_spread=3.21, l_copy=0.66, l_du=15.83, l_p=1),
            dict(ln0=0, xT0=3.1, ffn=7.3, down=8.8, x2=9.3, xT1=15.7, q=20.7, q2=28.8,
                 qT=32.4, scores=36.2, m=51.8, heads=55.2, wo=87.4, x3=89.7, d_ffn=0.1, d_scores=1.58, d_heads=1.67,
                 l_exp=0.09, l_o=0.16, l_mx=0.17, l_fa=0.59, l_fv=0.33,
                 kv=93, k2=145.6, kT=151.1,
                 bln=0.1, bxT=5.5, router=0.8, gT=9.5, moe=12.2, d_moe=4.67, out=90.9, l_tanh=0.06, l_ma=0.1, l_gate=2.48, l_hg=2.33,
                 start=2.1, conv=7.1, u=9.9, xproj=9.8, dt=13.2, softplus=14.7, scan=21.2, d_scan=4.62, y=145.6,
                 l_spread=2.7, l_copy=1.8, l_du=2.39, l_p=0.1),
            dict(ln0=0.2, xT0=1.9, ffn=4.7, down=15.7, x2=23.7, xT1=31.3, q=35.5, q2=47.3,
                 qT=54.6, scores=63, m=93.7, heads=187.7, wo=1.5, x3=51.8, d_ffn=0.3, d_scores=2.97, d_heads=12.61,
                 l_exp=0.71, l_o=0.45, l_mx=0.05, l_fa=0.09, l_fv=0.06,
                 bln=0.3, bxT=1.9, router=4.4, gT=6.1, moe=9.6, d_moe=6.37, out=149.1, l_tanh=0.06, l_ma=1.65, l_gate=3.56, l_hg=5.47),
            dict(bln=0, bxT=3, router=6, gT=9, moe=13, d_moe=5, out=99,
                 l_tanh=1, l_ma=2, l_gate=3, l_hg=4),
        ]
        T = {}
        AFTER = 1.2

        def start_at_one(e, i):
            for name in list(PER)[i::4]:
                e.sem_inc(sem[name], 1)

        def slot_is_free(e, b, n):
            if n >= 3 and n % 2:
                e.wait_ge(*at("p_pair" if b else "y_red", b, (n - 1) // 2))
            elif n >= 3:
                e.wait_ge(*at("y_red", b, (n - 2) // 2))
            elif n == 0:
                e.wait_ge(*at("du", b, 1))

        def wide_b():
            return bs[:, :].rearrange("p (a l) -> p a l", a=1).to_broadcast([P, 2, L])

        def place(b):
            own = (bw[:, 0, :], bw[:, 1, :], bw[:, 2, :])
            if b == B - 1:
                return [2, 4, 5], 6, [own, (work[:, 0, :], work[:, 1, :], work[:, 2, :])]
            if b == B - 2:
                return [2, 0], 1, [own, (hb[:, 0, 0, :], hb[:, 0, 1, :], hb[:, 1, 0, :])]
            return [2], 2, [own]

        def nothing(b):
            return
            yield

        def together(*parts):
            steps = [[next(p, None), i, p] for i, p in enumerate(parts)]
            steps = [s for s in steps if s[0] is not None]
            while steps:
                step = min(steps, key=lambda s: s[:2])
                step[0] = next(step[2], None)
                if step[0] is None:
                    steps.remove(step)

        def schedule(mamba, keys, attention, mixture, *weights):
            T.update(PLACES[0])
            together(mamba(0), keys(0), *(w() for w in weights))
            T.update(PLACES[1])
            together(attention(0), mamba(1), keys(1))
            T.update(PLACES[2])
            for b in range(2, B):
                together(attention(b - 1), mixture(b - 2), mamba(b), keys(b))
            T.update(PLACES[3])
            together(attention(B - 1), mixture(B - 2))
            T.update(PLACES[4])
            together(mixture(B - 1))

        @block.sync
        def _(sp):
            def load_ctx(b):
                sp.dma_start(ctx[:, :], ctxT[b]).then_inc(ctx_in, 16)

            def load_x(b):
                sp.dma_start(xin[:, :, :], x[b].rearrange("(t p) d -> p t d", p=P)).then_inc(x_in, 16)

            def load_ctxR(b):
                sp.dma_start(ctxR[:, 0, :], ctxT[b, :, 0:P]).then_inc(ctxR_in, 16)
                sp.dma_start(ctxR[:, 1, 0:MAIN - P], ctxT[b, :, P:MAIN]).then_inc(ctxR_in, 16)
                sp.dma_start(ctxR[:, 2, MAIN - P:P], ctxT[b, :, MAIN:L]).then_inc(ctxR_in, 16)

            def weights():
                yield T["start"] - 1
                for i, (kind, c) in enumerate(chunks):
                    if i == MM + 1:
                        for dst, src in LATER:
                            sp.dma_start(dst, src).then_inc(once["later"], 16)
                    if RAW <= i:
                        if i - RAW < MM:
                            sp.wait_ge(once["raw_lo"], i - RAW + 1)
                        else:
                            sp.wait_ge(once["q_clip"], i - RAW - MM + 1)
                            sp.wait_ge(once["q_big"], 2 * (i - RAW - MM + 1))
                    src = w_gu[:, c] if kind == "gu" else w_dn[:, 512 * c:512 * c + 512] if kind == "dn" else w13[:, c]
                    sp.dma_start(raw(i), src).then_inc(raw_in[i % RAW], 16)
                for dst, src in LAST:
                    sp.dma_start(dst, src).then_inc(once["last"], 16)

            def mamba(b):
                yield T["y"] + 3 * AFTER
                if b + 1 < B:
                    sp.wait_ge(*at("dbu", b, NS))
                    load_ctx(b + 1)
                if b + 1 < B:
                    sp.wait_ge(*at("x1", b, 1))
                    load_x(b + 1)

            def keys(b):
                yield T["kT"]
                if b + 1 < B:
                    sp.wait_ge(*at("kv_ps", b, 1))
                    load_ctxR(b + 1)

            def attention(b):
                yield T["wo"]

            def mixture(b):
                yield T["out"] + 3 * AFTER
                sp.wait_ge(*at("xo", b, 1))
                sp.dma_start(out[b].rearrange("(t p) d -> p t d", p=P), xo[:, :, :]).then_inc(stored, 16)

            load_ctx(0)
            for dst, src in EARLY:
                sp.dma_start(dst, src).then_inc(once["early"], 16)
            load_x(0)
            sp.wait_ge(once["zeros_set"], ZEROED)
            load_ctxR(0)
            schedule(mamba, keys, attention, mixture, weights)
            sp.wait_ge(stored, 16 * B)

        @block.gpsimd
        def _(g):
            start_at_one(g, 0)
            g.sem_inc(sem["p_pair"], NS // 2)
            g.memset(xpad[:, :, :], 0.0).then_inc(once["zeros_set"], 1)
            g.memset(ctxR[:, :, :], 0.0).then_inc(once["zeros_set"], 1)
            g.memset(dA[:, :, :, :], 0.0).then_inc(once["zeros_set"], 1)
            g.memset(vst[:, :, :], 0.0).then_inc(once["zeros_set"], 1)
            g.memset(mhalf[:, :], -0.5).then_inc(once["ones_set"], 1)
            g.memset(st[:, :, :, :].bitcast(F32), 0.0).then_inc(once["zeros_set"], 1)
            g.wait_ge(once["early"], 16 * len(EARLY))
            g.wait_ge(once["zeros_set"], ZEROED)
            g.memset(vsth[0][:, :, HD:HD + 1], 1.0).then_inc(once["pool_step"], 1)
            for h in range(H):
                g.tensor_scalar(vsth[1][:, h, HD:HD + 1], vec[:, V_MM:V_MM + 1], 1.0, 0.0, ALU.mult, ALU.add).then_inc(once["pool_step"], 1)
                g.tensor_scalar(vsth[1][:, h, 2 * HD + 1:2 * HD + 2], vec[:, V_MM + 1:V_MM + 2], 1.0, 0.0, ALU.mult, ALU.add).then_inc(once["pool_step"], 1)

            def lower_parts():
                for m in range(MM):
                    yield T["raw"] + T["d_raw"] * m
                    g.wait_ge(once["raw_hi"], m + 1)
                    g.tensor_tensor(w13_lo[:, m].rearrange("p k w c -> p (k w c)"), raw(m),
                                    w13_hi[:, m].rearrange("p k w c -> p (k w c)").bitcast(F32), ALU.subtract).then_inc(once["raw_lo"], 1)

            def rounded():
                for i in range(QUANT):
                    kind, c = chunks[MM + i]
                    yield T["quant"] + T["d_quant"] * i + 3 * AFTER
                    g.wait_ge(once["q_wide"], 3 * i + 3)
                    g.tensor_tensor(q0, q0, q1, ALU.add).then_inc(once["q_sum"], 1)
                    g.wait_ge(once["q_sum"], i + 1)
                    dst = wgu[:, c].rearrange("p k w c -> p (k w c)") if kind == "gu" else wdn[:, 2 * c:2 * c + 2, :].rearrange("p a b -> p (a b)")
                    g.tensor_tensor(dst, q0, q2, ALU.add).then_inc(once["q_out"], 1)

            def mamba(b):
                yield T["conv"]
                g.wait_ge(*at("zvar", b, 1))
                g.tensor_tensor(zr[:, :], zv[:, :], mhalf[:, 0:T2], ALU.pow).then_inc(sem["zrstd"], 1)
                for n in range(NS):
                    if b:
                        yield T["scan"] + T["d_scan"] * n - T["l_du"]
                        slot_is_free(g, b, n)
                        g.wait_ge(*at("b_sb", b, n + 1))
                        g.tensor_tensor(hb[:, n % 3], du[:, :, :], wide_b(), ALU.mult).then_inc(sem["dbu"], 1)
                    yield T["scan"] + T["d_scan"] * n + T["l_p"]
                    g.wait_ge(*at("h", b, n + 1))
                    g.wait_ge(*at("c_sb", b, n + 1))
                    hn = hb[:, n % 3]
                    cb = cs[:, n % 2, :].rearrange("p (a l) -> p a l", a=1).to_broadcast([P, 2, L])
                    g.tensor_tensor(hn, hn, cb, ALU.mult).then_inc(sem["p"], 1)
                    if n % 2 and b:
                        g.wait_ge(*at("p", b, n + 1))
                        g.tensor_tensor(hn, hn, hb[:, (n - 1) % 3], ALU.add).then_inc(sem["p_pair"], 1)

            def attention(b):
                for i, key in enumerate(("ln0", "x2")):
                    yield T[key] + AFTER
                    g.wait_ge(*at("lvar", b, i + 1))
                    g.tensor_tensor(lr[:, :], lv[:, :], mhalf[:, 0:T2], ALU.pow).then_inc(sem["lrstd"], 1)

            def mixture(b):
                yield T["bln"] + AFTER
                g.wait_ge(*at("bvar", b, 1))
                g.tensor_tensor(br[:, :], bv[:, :], mhalf[:, 0:T2], ALU.pow).then_inc(sem["brstd"], 1)

            schedule(mamba, nothing, attention, mixture, lower_parts, rounded)

        @block.scalar
        def _(a):
            for dst, src in EARLY_TOO:
                a.dma_start(dst, src).then_inc(once["early_too"], 16)
            start_at_one(a, 1)
            a.wait_ge(once["early"], 16 * len(EARLY))
            a.activation(identR[:, :], cident[:, 0:P], ACT.Copy).then_inc(once["ident_r"], 1)
            a.activation(selBC, cident[0:2 * BCR, P:P + BCR], ACT.Copy).then_inc(once["ident_r"], 1)
            a.wait_ge(once["early_too"], 16 * len(EARLY_TOO))
            al = vec[:, V_AL:V_AL + 2 * NS].rearrange("p (a n) -> p a n", a=2)
            a.activation(negA[:, :, :], al, ACT.Exp).then_inc(once["act_step"], 1)
            a.activation(tg[:, :], row[:, R_G:R_G + 4], ACT.Tanh).then_inc(once["act_step"], 1)
            a.activation(gselR, hb[0:2 * E].rearrange("p a b c -> p (a b c)")[:, 0:MG * P].rearrange("p (m c) -> p m c", m=MG), ACT.Copy).then_inc(once["ident_r"], 1)
            a.activation(wdt_hi[64:XR], xc[64:XR, 0, :], ACT.Copy).then_inc(once["wdt_part"], 1)

            def upper_parts():
                for m in range(MM):
                    yield T["raw"] + T["d_raw"] * m
                    chunk_in(a, m)
                    a.activation(w13_hi[:, m].rearrange("p k w c -> p (k w c)"), raw(m), ACT.Copy).then_inc(once["raw_hi"], 1)

            def rounded():
                for i in range(QUANT):
                    yield T["quant"] + T["d_quant"] * i + 2 * AFTER
                    if i:
                        a.wait_ge(once["q_out"], i)
                    for j, (q, n) in enumerate(((q0, 1), (q1, 2), (q2, 2))):
                        if j == 0:
                            a.wait_ge(once["q_clip"], i + 1)
                        elif j == 1:
                            a.wait_ge(once["q_big"], 2 * i + 2)
                        a.activation(q, f8[:, j, :], ACT.Copy, scale=float(n)).then_inc(once["q_wide"], 1)

            def mamba(b):
                yield T["u"] - AFTER
                a.wait_ge(*at("conv", b, 2))
                a.activation(u2[:, :, :], cv[:, :, :], ACT.Tanh, scale=0.5).then_inc(sem["conv_tanh"], 1)
                a.wait_ge(*at("zhat", b, 2))
                a.wait_ge(*at("y_red", b, 0))
                a.activation(zt[:, :, :], zh[:, :, :], ACT.Tanh, scale=0.5).then_inc(sem["ztanh"], 1)
                yield T["xproj"] + AFTER
                a.wait_ge(*at("xdbl", b, 1))
                a.activation(stack[0:XR, :], ps[0:XR, 0, 0:L], ACT.Copy, scale=0.5).then_inc(sem["bc_hi"], 1)
                yield T["dt"] + AFTER
                a.wait_ge(*at("dt_pre", b, 1))
                a.wait_ge(*at("y_red", b, 0))
                for e in range(2):
                    a.activation(sp_x[:, e, :], ps[:, 1, e * L:e * L + L], ACT.Abs, bias=vec[:, V_DTB + e:V_DTB + e + 1]).then_inc(sem["sp_abs"], 1)
                a.wait_ge(*at("sp_abs", b, 2))
                a.activation(sp_x, sp_x, ACT.Exp, scale=-1.0).then_inc(sem["sp_t"], 1)
                a.wait_ge(*at("sp_t", b, 1))
                a.activation(sp_l, sp_x, ACT.Ln, bias=1.0).then_inc(sem["sp_ln"], 1)
                for n in range(NS):
                    yield T["scan"] + T["d_scan"] * n - T["l_copy"]
                    if n == 0:
                        a.wait_ge(*at("dt", b, 1))
                    a.wait_ge(*at("bc", b, n + 1))
                    a.wait_ge(*at("dbu", b, n))
                    a.activation(bs[:, :], ps[:, 0, 0:L], ACT.Copy).then_inc(sem["b_sb"], 1)
                    if n >= 2:
                        a.wait_ge(*at("p", b, n - 1))
                    a.activation(cs[:, n % 2, :], ps[:, 0, L:2 * L], ACT.Copy).then_inc(sem["c_sb"], 1)
                    if n >= 2:
                        a.wait_ge(*at("h", b, n - 1))
                    for e in range(2):
                        a.activation(dA[:, n % 2, e, 1:L], dt_sb[:, e, 1:L], ACT.Exp, scale=negA[:, e, n:n + 1]).then_inc(sem["dA"], 1)

            def rsqrt(b, key, var, log, done):
                yield key - 2 * AFTER
                a.wait_ge(*at(var, b, 1))
                a.activation(hs[:, 0, :], hs[:, 2, :], ACT.Ln).then_inc(sem[log], 1)
                a.wait_ge(*at(log, b, 1))
                a.activation(hs[:, 3, :], hs[:, 0, :], ACT.Exp, scale=-0.5).then_inc(sem[done], 1)

            def keys(b):
                yield from rsqrt(b, T["k2"], "kvar", "kln", "krstd")
                yield T["kT"] + AFTER
                for t in range(T2):
                    a.wait_ge(*at("kT_ps", b, t + 1))
                    a.activation(kT[:, :, t * P:t * P + P], bankR(6 - 2 * t, 1024, 2).rearrange("p (j c) -> p j c", j=HP), ACT.Copy).then_inc(sem["kT"], 1)

            def attention(b):
                yield T["xT0"] + AFTER
                a.wait_ge(*at("xT_ps", b, 1))
                a.activation(xhi[:, :, :], b7x, ACT.Copy).then_inc(sem["x_hi"], 1)
                for m in range(MF):
                    yield T["ffn"] + T["d_ffn"] * m + T["l_fa"]
                    a.wait_ge(*at("gu", b, m + 1))
                    if m >= 2:
                        a.wait_ge(*at("g_a", b, m - 1))
                    a.activation(work[:, m % 2, :], ps[:, 4 + m % 3, 0:L], ACT.Tanh, scale=halfgs[:, m:m + 1]).then_inc(sem["g_tanh"], 1)
                yield T["xT1"] + AFTER / 2
                a.wait_ge(*at("xT_ps", b, 2))
                a.activation(xT[:, :, :], b7x, ACT.Copy).then_inc(sem["xT"], 1)
                yield from rsqrt(b, T["q2"], "qvar", "qln", "qrstd")
                for r in range(2):
                    yield (T["m"] if r else T["qT"]) + AFTER
                    for t in range(T2):
                        a.wait_ge(*at("qT_ps", b, 2 * r + t + 1))
                        if r:
                            a.wait_ge(*at("s_ps", b, 8))
                        a.activation(qT[:, :, t * P:t * P + P], bankR(6 - 2 * t, 1024, 2).rearrange("p (j c) -> p j c", j=HP), ACT.Copy).then_inc(sem["qT"], 1)
                for h in range(H + 2):
                    yield T["heads"] + T["d_heads"] * h + T["l_exp"]
                    if h < H:
                        a.wait_ge(*at("st_ps", b, h + 1))
                        if h >= 4:
                            a.wait_ge(*at("pv", b, h - 3))
                        slot = work[:, 2 * (h % 4):2 * (h % 4) + 2, :].rearrange("p a b -> p (a b)")
                        a.activation(slot, ps[:, 4 + h % 2, :], ACT.Exp).then_inc(sem["prob"], 1)
                    if h >= 3 and h % 2:
                        j = (h - 3) // 2
                        a.wait_ge(*at("pv", b, 2 * j + 2))
                        if j >= 2:
                            a.wait_ge(*at("oT_ps", b, j - 1))
                        a.activation(work[:, 8 + j % 2, :], ps[:, 6 + j % 2, 0:L], ACT.Copy).then_inc(sem["o_sb"], 1)
                yield T["wo"] + AFTER
                a.wait_ge(*at("cT_ps", b, 1))
                a.activation(xT[:, :, :], ps[:, 4, :].rearrange("p (k c) -> p k c", k=K2), ACT.Copy).then_inc(sem["cT"], 1)

            def mixture(b):
                yield T["bln"]
                a.wait_ge(*at("x3", b, 1))
                a.wait_ge(*at("xo", b, 0))
                a.activation(xc[:, :, :], xb[:, :, :], ACT.Copy).then_inc(sem["xc"], 1)
                yield T["bxT"] + AFTER
                if b:
                    a.wait_ge(stored, b * 16)
                a.wait_ge(*at("bT_ps", b, 1))
                a.activation(bT[:, :, :], b3x, ACT.Copy).then_inc(sem["bT"], 1)
                a.activation(bhi[:, :, :], b3x, ACT.Copy).then_inc(sem["b_hi"], 1)
                yield T["router"]
                a.wait_ge(*at("lg", b, 1))
                a.activation(rt[:, 0], ps[:, 2, 0:T2 * E].rearrange("p (t e) -> p t e", t=T2), ACT.Tanh, scale=0.5).then_inc(sem["lg_tanh"], 1)
                yield T["gT"] + AFTER
                a.wait_ge(*at("gT_ps", b, 1))
                a.activation(gT[:, :], psR[0:2 * E, 2, 0:L], ACT.Copy).then_inc(sem["gT"], 1)
                hidden_banks, gate_bank, temps = place(b)
                for m in range(MM):
                    yield T["moe"] + T["d_moe"] * m + T["l_tanh"]
                    a.wait_ge(*at("h13", b, m + 1))
                    if m >= len(temps):
                        a.wait_ge(*at("m_a", b, m - len(temps) + 1))
                    a.activation(temps[m % len(temps)][0], ps[:, hidden_banks[m % len(hidden_banks)], 0:L], ACT.Tanh, scale=0.5).then_inc(sem["m_tanh"], 1)

            schedule(mamba, keys, attention, mixture, upper_parts, rounded)

        @block.vector
        def _(v):
            start_at_one(v, 2)
            v.wait_ge(once["early"], 16 * len(EARLY))
            v.wait_ge(once["zeros_set"], 1)
            v.wait_ge(once["ident_r"], 2)

            def constants():
                yield T["u"] - AFTER / 2
                v.wait_ge(once["zeros_set"], ZEROED)
                v.wait_ge(once["early_too"], 16 * len(EARLY_TOO))
                v.wait_ge(once["act_step"], 2)
                v.wait_ge(once["wdt_part"], 1)
                v.tensor_tensor(wdt_lo[64:XR], xc[64:XR, 0, :], wdt_hi[64:XR].bitcast(F32), ALU.subtract).then_inc(once["setup"], 1)
                v.tensor_scalar(negA[:, :, :], negA[:, :, :], -1.0, None, ALU.mult).then_inc(once["setup"], 1)
                v.tensor_scalar(halfD[:, :], vec[:, V_D:V_D + 2], 0.5, None, ALU.mult).then_inc(once["setup"], 1)
                v.tensor_scalar(tgh[:, :], tg[:, 0:1], 0.5, None, ALU.mult).then_inc(once["setup"], 1)
                v.tensor_scalar(halfgs[:, :], vec[:, V_GS:V_GS + MF], 0.5, None, ALU.mult).then_inc(once["setup"], 1)
                v.tensor_scalar(dsb, dsb, tg[:, 2:3], None, ALU.mult).then_inc(once["setup"], 1)
                v.tensor_scalar(gbo, gbo, tg[:, 1:2], None, ALU.mult).then_inc(once["setup"], 1)
                v.tensor_scalar(qwb, qwb, HD ** -0.5, None, ALU.mult).then_inc(once["setup"], 1)
                v.wait_ge(once["setup"], 8)
                v.tensor_tensor(gsu[:, :], halfgs[:, :], vec[:, V_US:V_US + MF], ALU.mult).then_inc(once["setup"], 1)
                v.wait_ge(once["setup"], 9)

            def rounded():
                for i in range(QUANT):
                    yield T["quant"] + T["d_quant"] * i
                    chunk_in(v, MM + i)
                    r = raw(MM + i)
                    if i:
                        v.wait_ge(once["q_wide"], 3 * i)
                    v.tensor_scalar(f8[:, 0, :], r, 240.0, -240.0, ALU.min, ALU.max, saturate=False).then_inc(once["q_clip"], 1)
                    v.tensor_scalar(f8[:, 1, :], r, 240.0, 0.5, ALU.max, ALU.mult, saturate=False).then_inc(once["q_big"], 1)
                    v.tensor_scalar(f8[:, 2, :], r, -240.0, 0.5, ALU.min, ALU.mult, saturate=False).then_inc(once["q_big"], 1)

            def centred():
                yield T["centre"]
                v.wait_ge(once["later"], 16 * len(LATER))
                wide_w = (wq[:, :, :].rearrange("p k (h c) -> p (k h) c", h=H),
                          wkv[:, :].rearrange("p (h c) -> p h c", h=H)[:, :, 0:HD],
                          wkvd[:, :].rearrange("p (h c) -> p h c", h=H)[:, :, 0:HD],
                          kv_bias[:, 0:2, :].rearrange("p t (h c) -> p (t h) c", h=H),
                          row[:, R_BQ:R_BQ + D].rearrange("p (h c) -> p h c", h=H))
                for i, w in enumerate(wide_w):
                    heads = w.shape[1]
                    mean = hs[:, i % 2, 0:heads]
                    if i >= 2:
                        v.wait_ge(once["centred"], 3 * (i - 1))
                    v.tensor_reduce(mean, w, AX_X, ALU.add).then_inc(once["centred"], 1)
                    v.wait_ge(once["centred"], 3 * i + 1)
                    v.tensor_scalar(mean, mean, 1.0 / HD, None, ALU.mult).then_inc(once["centred"], 1)
                    v.wait_ge(once["centred"], 3 * i + 2)
                    v.tensor_tensor(w, w, mean.rearrange("p (h a) -> p h a", a=1).to_broadcast([P, heads, HD]), ALU.subtract).then_inc(once["centred"], 1)

            def mamba(b):
                yield T["start"]
                v.wait_ge(x_in, b * 16 + 16)
                for t in range(T2):
                    v.bn_stats(zst[:, t, :], xin[:, t, :]).then_inc(sem["zstat"], 1)
                v.wait_ge(*at("zstat", b, 2))
                for t in range(T2):
                    v.bn_aggr(zmv[:, t, :], zst[:, t, :]).then_inc(sem["zstat"], 1)
                v.wait_ge(*at("zstat", b, 4))
                v.tensor_scalar(zv[:, :], zmv[:, :, 1], LN_EPS, None, ALU.add).then_inc(sem["zvar"], 1)
                yield T["conv"]
                v.wait_ge(*at("xi", b, 1))
                v.wait_ge(*at("p", b, 0))
                v.tensor_copy(xpad[:, :, TAPS - 1:], ps[:, 0, :].rearrange("p (e l) -> p e l", e=2)).then_inc(sem["xpad"], 1)
                v.wait_ge(*at("xpad", b, 1))
                v.wait_ge(*at("conv_tanh", b, 0))
                for k in range(TAPS):
                    for e in range(2):
                        w = vec[:, V_CW + 4 * e + k:V_CW + 4 * e + k + 1]
                        if k:
                            v.wait_ge(*at("conv_step", b, 2 * (k - 1) + e + 1))
                        if k == 0:
                            i = v.tensor_scalar(cv[:, e, :], xpad[:, e, 0:L], w, vec[:, V_CB + e:V_CB + e + 1], ALU.mult, ALU.add)
                        else:
                            i = v.scalar_tensor_tensor(cv[:, e, :], xpad[:, e, k:k + L], w, cv[:, e, :], ALU.mult, ALU.add)
                        i.then_inc(sem["conv" if k == TAPS - 1 else "conv_step"], 1)
                v.wait_ge(*at("zrstd", b, 1))
                for t in range(T2):
                    v.tensor_scalar(zh[:, t, :], xin[:, t, :], zmv[:, t, 0:1], zr[:, t:t + 1], ALU.subtract, ALU.mult).then_inc(sem["zhat"], 1)
                yield T["u"]
                v.wait_ge(*at("conv_tanh", b, 1))
                v.scalar_tensor_tensor(u2[:, :, :], u2[:, :, :], 1.0, cv[:, :, :], ALU.add, ALU.mult).then_inc(sem["u"], 1)
                v.wait_ge(*at("ztanh", b, 1))
                v.scalar_tensor_tensor(zg[:, :, :], zt[:, :, :], 1.0, zh[:, :, :], ALU.add, ALU.mult).then_inc(sem["zg"], 1)
                yield T["xproj"] + 2 * AFTER
                v.wait_ge(*at("bc_hi", b, 1))
                for r in (BCR, 3 * BCR):
                    hi = stack[r:min(r + BCR, XR), :]
                    v.scalar_tensor_tensor(hi, ps[r:min(r + BCR, XR), 0, 0:L], 0.5, hi.bitcast(F32), ALU.mult, ALU.subtract).then_inc(sem["bc_lo"], 1)
                yield T["softplus"]
                v.wait_ge(*at("dt_pre", b, 1))
                v.wait_ge(*at("zg", b, 1))
                v.wait_ge(*at("sp_abs", b, 2))
                for e in range(2):
                    v.tensor_scalar(sp_r[:, e, :], ps[:, 1, e * L:e * L + L], vec[:, V_DTB + e:V_DTB + e + 1], 0.0, ALU.add, ALU.max).then_inc(sem["sp_relu"], 1)
                yield T["softplus"] + AFTER
                v.wait_ge(*at("sp_t", b, 1))
                v.tensor_scalar(sp_q, sp_x, -0.25, 1.0 / 3.0, ALU.mult, ALU.add).then_inc(sem["sp_step"], 1)
                v.tensor_scalar(sp_m, sp_x, 1.0 / 32.0, None, ALU.is_lt).then_inc(sem["sp_step"], 1)
                v.wait_ge(*at("sp_step", b, 1))
                v.tensor_tensor(sp_q, sp_q, sp_x, ALU.mult).then_inc(sem["sp_step"], 1)
                v.wait_ge(*at("sp_step", b, 3))
                v.scalar_tensor_tensor(sp_q, sp_q, -0.5, sp_x, ALU.add, ALU.mult).then_inc(sem["sp_step"], 1)
                v.wait_ge(*at("sp_step", b, 4))
                v.scalar_tensor_tensor(sp_q, sp_q, 1.0, sp_x, ALU.add, ALU.mult).then_inc(sem["sp_step"], 1)
                yield T["softplus"] + 3 * AFTER
                v.wait_ge(*at("sp_step", b, 5))
                v.wait_ge(*at("sp_ln", b, 1))
                v.copy_predicated(sp_l, sp_m, sp_q).then_inc(sem["sp_step"], 1)
                v.wait_ge(*at("sp_step", b, 6))
                v.wait_ge(*at("sp_relu", b, 2))
                v.tensor_tensor(dt_sb[:, :, :], sp_l, sp_r[:, :, :], ALU.add).then_inc(sem["dt"], 1)
                v.wait_ge(*at("dt", b, 1))
                v.scalar_tensor_tensor(du[:, :, :], dt_sb[:, :, :], 0.5, u2[:, :, :], ALU.mult, ALU.mult).then_inc(sem["du"], 1)
                v.wait_ge(*at("du", b, 1))
                for n in range(NS):
                    yield T["scan"] + T["d_scan"] * n
                    hn = hb[:, n % 3]
                    if b == 0:
                        slot_is_free(v, b, n)
                        v.wait_ge(*at("b_sb", b, n + 1))
                        v.tensor_tensor(hn, du[:, :, :], wide_b(), ALU.mult).then_inc(sem["dbu"], 1)
                    v.wait_ge(*at("dbu", b, n + 1))
                    v.wait_ge(*at("dA", b, 2 * n + 2))
                    hf = hn.rearrange("p e l -> p (e l)")
                    v.tensor_tensor_scan(hf, dA[:, n % 2].rearrange("p e l -> p (e l)"), hf, 0.0, ALU.mult, ALU.add).then_inc(sem["h"], 1)
                yield T["y"]
                v.wait_ge(*at("y_red", b, NS // 2))
                for e in range(2):
                    v.scalar_tensor_tensor(cv[:, e, :], u2[:, e, :], halfD[:, e:e + 1], ps[:, 1, e * L:e * L + L], ALU.mult, ALU.add).then_inc(sem["ys"], 1)
                v.wait_ge(*at("ys", b, 2))
                v.tensor_tensor(cv[:, :, :], cv[:, :, :], zg[:, :, :], ALU.mult).then_inc(sem["yz"], 1)
                yield T["y"] + 2 * AFTER
                v.wait_ge(*at("yT", b, 1))
                v.wait_ge(*at("x2", b, 0))
                v.scalar_tensor_tensor(xa[:, :, :], ps[:, 0, :].rearrange("p (t d) -> p t d", t=T2), tgh[:, :], xin[:, :, :], ALU.mult, ALU.add).then_inc(sem["x1"], 1)

            def head_norm(b, key, w, bias, step, var, rstd, last):
                ssq, ve, rs_ = hs[:, 1, :], hs[:, 2, :], hs[:, 3, :]
                newton = ssq
                v.tensor_tensor(sq, qk[:, :, :, :], qk[:, :, :, :], ALU.mult).then_inc(sem[step], 1)
                v.wait_ge(*at(step, b, 1))
                v.tensor_reduce(ssq, sq, AX_X, ALU.add).then_inc(sem[step], 1)
                v.wait_ge(*at(step, b, 2))
                v.tensor_scalar(ve, ssq, 1.0 / HD, QK_EPS, ALU.mult, ALU.add).then_inc(sem[var], 1)
                yield key
                v.wait_ge(*at(rstd, b, 1))
                v.scalar_tensor_tensor(newton, rs_, -0.5, rs_, ALU.mult, ALU.mult).then_inc(sem[step], 1)
                v.wait_ge(*at(step, b, 3))
                v.tensor_tensor(newton, newton, ve, ALU.mult).then_inc(sem[step], 1)
                v.wait_ge(*at(step, b, 4))
                v.scalar_tensor_tensor(rs_, newton, 1.5, rs_, ALU.add, ALU.mult).then_inc(sem[step], 1)
                v.wait_ge(*at(step, b, 5))
                v.tensor_tensor(qk[:, :, :, :], qk[:, :, :, :], rs_.rearrange("p (t h a) -> p t h a", t=T2, a=1).to_broadcast([P, T2, H, HD]), ALU.mult).then_inc(sem[step], 1)
                v.wait_ge(*at(step, b, 6))
                v.tensor_tensor(qk[:, :, :, :], qk[:, :, :, :], w, ALU.mult).then_inc(sem[last], 1)
                v.wait_ge(*at(last, b, 1))
                v.tensor_tensor(qk[:, :, :, :], qk[:, :, :, :], bias, ALU.add).then_inc(sem[last], 1)
                v.wait_ge(*at(last, b, 2))

            def keys(b):
                yield T["kv"] + AFTER
                v.wait_ge(*at("kv_ps", b, 1))
                kv = ps[:, 4:6, :].rearrange("p t (h c) -> p t h c", h=H)

                def bias(i, n):
                    return kv_bias[:, i:i + n, :].rearrange("p t (h c) -> p t h c", h=H)

                def by_token(c0):
                    return row[:, c0:c0 + T2 * HD].rearrange("p (t a c) -> p t a c", t=T2, a=1).to_broadcast([P, T2, H, HD])
                v.tensor_tensor(qk[:, :, :, :], kv[:, :, :, 0:HD], bias(0, 2), ALU.add).then_inc(sem["kv"], 1)
                v.tensor_tensor(vsth[0][:, :, 0:HD], kv[:, 0, :, HD:], bias(2, 1)[:, 0], ALU.add).then_inc(sem["vst"], 1)
                for i, c in ((0, 0), (1, HD + 1)):
                    v.scalar_tensor_tensor(vsth[1][:, :, c:c + HD], kv[:, 1, :, HD:], vec[:, V_MM + i:V_MM + i + 1], bias(3 + i, 1)[:, 0], ALU.mult, ALU.add).then_inc(sem["vst"], 1)
                v.wait_ge(*at("kv", b, 1))
                yield from head_norm(b, T["k2"], by_token(R_KW), by_token(R_KB), "kstep", "kvar", "krstd", "kstack")
                v.tensor_copy(st[:, :, :, 0:HD], qk[:, :, :, :]).then_inc(sem["kstack"], 1)
                v.tensor_copy(st[:, :, :, 2 * HD:3 * HD], qk[:, :, :, :]).then_inc(sem["kstack"], 1)
                km = row[:, R_KM:R_KM + T2 * 4].rearrange("p (t a c) -> p t a c", t=T2, a=1).to_broadcast([P, T2, H, 4])
                v.tensor_copy(st[:, :, :, 3 * HD:3 * HD + 4], km).then_inc(sem["k_m"], 1)
                v.wait_ge(*at("kstack", b, 3))
                v.tensor_tensor(st[:, :, :, HD:2 * HD], qk[:, :, :, :], st[:, :, :, 0:HD].bitcast(F32), ALU.subtract).then_inc(sem["kstack"], 1)

            def layer_norm(b, i, key, src, dst, stats, names):
                stat, var, rstd, done = names
                part, mv, ve, rs_ = stats
                for t in range(T2):
                    v.bn_stats(part[:, t, :], src[:, t, :]).then_inc(sem[stat], 1)
                v.wait_ge(*at(stat, b, 4 * i + 2))
                for t in range(T2):
                    v.bn_aggr(mv[:, t, :], part[:, t, :]).then_inc(sem[stat], 1)
                v.wait_ge(*at(stat, b, 4 * i + 4))
                v.tensor_scalar(ve[:, :], mv[:, :, 1], LN_EPS, None, ALU.add).then_inc(sem[var], 1)
                yield key
                v.wait_ge(*at(rstd, b, i + 1))
                for t in range(T2):
                    v.tensor_scalar(dst[:, t, :], src[:, t, :], mv[:, t, 0:1], rs_[:, t:t + 1], ALU.subtract, ALU.mult).then_inc(sem[done], 1)

            def attention(b):
                a_norm = ((lst, lmv, lv, lr), ("lstat", "lvar", "lrstd", "xh"))

                def by_head(i):
                    return qwb[:, i, :].rearrange("p (t a c) -> p t a c", t=1, a=1).to_broadcast([P, T2, H, HD])

                yield T["ln0"]
                v.wait_ge(*at("x1", b, 1))
                yield from layer_norm(b, 0, T["xT0"] - AFTER, xa, xh, *a_norm)
                yield T["xT0"] + 2 * AFTER
                v.wait_ge(*at("x_hi", b, 1))
                v.tensor_tensor(xlo[:, :, :], b7x, xhi[:, :, :].bitcast(F32), ALU.subtract).then_inc(sem["x_lo"], 1)
                for m in range(MF):
                    yield T["ffn"] + T["d_ffn"] * m + T["l_fv"]
                    v.wait_ge(*at("g_tanh", b, m + 1))
                    g, u = ps[:, 4 + m % 3, 0:L], ps[:, 4 + m % 3, L:2 * L]
                    v.scalar_tensor_tensor(work[:, 2 + m % 2, :], work[:, m % 2, :], 1.0, g, ALU.add, ALU.mult).then_inc(sem["g_a"], 1)
                    v.wait_ge(*at("g_a", b, m + 1))
                    v.scalar_tensor_tensor(work[:, 4 + m, :], work[:, 2 + m % 2, :], gsu[:, m:m + 1], u, ALU.mult, ALU.mult).then_inc(sem["h_ff"], 1)
                yield T["down"] + AFTER
                v.wait_ge(*at("down", b, 1))
                ds2 = dsb.rearrange("p (a d) -> p a d", a=1).to_broadcast([P, T2, D])
                v.tensor_tensor(xh[:, :, :], b7x, ds2, ALU.mult).then_inc(sem["dsc"], 1)
                v.wait_ge(*at("dsc", b, 1))
                v.wait_ge(*at("xc", b, 0))
                v.tensor_tensor(xb[:, :, :], xh[:, :, :], xa[:, :, :], ALU.add).then_inc(sem["x2"], 1)

                yield T["x2"]
                v.wait_ge(*at("x2", b, 1))
                yield from layer_norm(b, 1, T["xT1"] - AFTER, xb, xh, *a_norm)
                bo2 = gbo.rearrange("p (a d) -> p a d", a=1).to_broadcast([P, T2, D])
                v.wait_ge(*at("xh", b, 4))
                v.tensor_tensor(xb[:, :, :], xb[:, :, :], bo2, ALU.add).then_inc(sem["xbo"], 1)
                yield T["q"]
                v.wait_ge(*at("q_ps", b, 1))
                bq2 = row[:, R_BQ:R_BQ + D].rearrange("p (a d) -> p a d", a=1).to_broadcast([P, T2, D])
                v.tensor_tensor(qk[:, :, :, :].rearrange("p t h c -> p t (h c)"), ps[:, 4, :].rearrange("p (t d) -> p t d", t=T2), bq2, ALU.add).then_inc(sem["q"], 1)
                v.wait_ge(*at("q", b, 1))
                yield from head_norm(b, T["q2"], by_head(0), by_head(1), "qstep", "qvar", "qrstd", "qstack")
                v.tensor_copy(st[:, :, :, 0:HD], qk[:, :, :, :]).then_inc(sem["qstack"], 1)
                v.wait_ge(*at("qstack", b, 3))
                v.tensor_tensor(st[:, :, :, 2 * HD:3 * HD], qk[:, :, :, :], st[:, :, :, 0:HD].bitcast(F32), ALU.subtract).then_inc(sem["qstack"], 1)
                v.tensor_copy(st[:, :, :, HD:2 * HD], qk[:, :, :, :]).then_inc(sem["q_hi2"], 1)
                for i in range(8):
                    yield T["scores"] + T["d_scores"] * i + T["l_mx"]
                    t, hg = i // 4, i % 4
                    v.wait_ge(*at("s_ps", b, i + 1))
                    sc = bank(4 + 2 * (i % 2), 1024, 2).rearrange("p (b a c) -> p b a c", b=2, a=2)
                    mh = mx[:, t, 4 * hg:4 * hg + 4, :].rearrange("p (a b) w -> p b a w", b=2)
                    v.tensor_reduce(mh[:, :, :, 0], sc[:, :, :, 0:MAIN], AX_X, ALU.max).then_inc(sem["mx"], 1)
                    v.tensor_reduce(mh[:, :, :, 1], sc[:, :, :, MAIN:L], AX_X, ALU.max).then_inc(sem["mx"], 1)
                yield T["m"]
                ms = st[:, :, :, 3 * HD:3 * HD + 4].rearrange("p t h (w a) -> p t h w a", w=2)
                v.wait_ge(*at("mx", b, 16))
                v.wait_ge(*at("qT_ps", b, 2))
                v.tensor_copy(ms[:, :, :, :, 0], mx[:, :, :, :]).then_inc(sem["mstack"], 1)
                v.wait_ge(*at("mstack", b, 1))
                v.tensor_tensor(ms[:, :, :, :, 1], mx[:, :, :, :], ms[:, :, :, :, 0].bitcast(F32), ALU.subtract).then_inc(sem["mstack"], 1)
                for j in range(HP):
                    yield T["heads"] + T["d_heads"] * (2 * j + 4) + T["l_o"]
                    v.wait_ge(*at("oT_ps", b, j + 1))
                    o = ps[:, 6 + j % 2, L:2 * L].rearrange("p (a c) -> p a c", a=4)
                    if j:
                        v.wait_ge(*at("ctok", b, j))
                    o2 = o[:, :, 0:2 * HD + 2].rearrange("p a (w c) -> p a w c", w=2)
                    v.reciprocal(rec[:, :, :], o2[:, :, :, HD]).then_inc(sem["o_step"], 1)
                    v.wait_ge(*at("o_step", b, 2 * j + 1))
                    v.tensor_tensor(opr[:, :, :, :], o2[:, :, :, 0:HD], rec[:, :, :].rearrange("p a (w c) -> p a w c", c=1).to_broadcast([P, 4, 2, HD]), ALU.mult).then_inc(sem["o_step"], 1)
                    v.wait_ge(*at("o_step", b, 2 * j + 2))
                    dst = ctok[:, :, 2 * j:2 * j + 2, :]
                    src = opr[:, :, :, :].rearrange("p (t h) w c -> p t h w c", t=T2)
                    v.tensor_tensor(dst, src[:, :, :, 0], src[:, :, :, 1], ALU.add).then_inc(sem["ctok"], 1)
                yield T["x3"]
                v.wait_ge(*at("wo_ps", b, 1))
                v.wait_ge(*at("xbo", b, 1))
                v.scalar_tensor_tensor(xb[:, :, :], ps[:, 5, :].rearrange("p (t d) -> p t d", t=T2), tg[:, 1:2], xb[:, :, :], ALU.mult, ALU.add).then_inc(sem["x3"], 1)

            def mixture(b):
                yield T["bln"]
                v.wait_ge(*at("x3", b, 1))
                yield from layer_norm(b, 0, T["bxT"] - AFTER, xb, bxh, (bst, bmv, bv, br), ("bstat", "bvar", "brstd", "bxh"))
                yield T["bxT"] + 2 * AFTER
                v.wait_ge(*at("b_hi", b, 1))
                v.tensor_tensor(blo[:, :, :], b3x, bhi[:, :, :].bitcast(F32), ALU.subtract).then_inc(sem["b_lo"], 1)
                yield T["router"] + AFTER
                k_ = 0

                def router(i):
                    nonlocal k_
                    k_ += 1
                    i.then_inc(sem["r_step"], 1)
                    v.wait_ge(*at("r_step", b, k_))
                v.wait_ge(*at("lg_tanh", b, 1))
                score, sel, rank = rt[:, 1], rt[:, 2], rt[:, 3]
                router(v.tensor_scalar(score, rt[:, 0], 0.5, 0.5, ALU.mult, ALU.add))
                rb = row[:, R_RB:R_RB + E].rearrange("p (a e) -> p a e", a=1).to_broadcast([P, T2, E])
                router(v.tensor_tensor(sel, score, rb, ALU.add))
                other = sel.rearrange("p t (a f) -> p t a f", a=1).to_broadcast([P, T2, E, E])
                own = sel.rearrange("p t (e a) -> p t e a", a=1).to_broadcast([P, T2, E, E])
                gt = rk[:, 0].rearrange("p t (e f) -> p t e f", e=E)
                eq = rk[:, 1].rearrange("p t (e f) -> p t e f", e=E)
                router(v.tensor_tensor(gt, other, own, ALU.is_gt))
                router(v.tensor_tensor(eq, other, own, ALU.is_equal))
                tri = row[:, R_TR:R_TR + E * E].rearrange("p (a f) -> p a f", a=1).to_broadcast([P, T2, E * E])
                router(v.tensor_tensor(rk[:, 1], rk[:, 1], tri, ALU.mult))
                router(v.tensor_tensor(rk[:, 0], rk[:, 0], rk[:, 1], ALU.add))
                router(v.tensor_reduce(rank, gt, AX_X, ALU.add))
                router(v.scalar_tensor_tensor(rt[:, 4], rank, 1.5, score, ALU.is_lt, ALU.mult))
                router(v.tensor_reduce(rs[:, :], rt[:, 4], AX_X, ALU.add))
                router(v.tensor_scalar(rs[:, :], rs[:, :], 1e-12, None, ALU.max))
                router(v.reciprocal(rs[:, :], rs[:, :]))
                router(v.tensor_tensor(rt[:, 5], rt[:, 4], rs[:, :].rearrange("p (t a) -> p t a", a=1).to_broadcast([P, T2, E]), ALU.mult))
                v.tensor_copy(gst[:, :, 0:E], rt[:, 5]).then_inc(sem["gates"], 1)
                v.wait_ge(*at("gates", b, 1))
                v.tensor_tensor(gst[:, :, E:2 * E], rt[:, 5], gst[:, :, 0:E].bitcast(F32), ALU.subtract).then_inc(sem["gates"], 1)
                hidden_banks, gate_bank, temps = place(b)
                for m in range(MM):
                    yield T["moe"] + T["d_moe"] * m + T["l_ma"]
                    v.wait_ge(*at("m_tanh", b, m + 1))
                    hidden_bank = hidden_banks[m % len(hidden_banks)]
                    h1, h3 = ps[:, hidden_bank, 0:L], ps[:, hidden_bank, L:2 * L]
                    th, t1, t2 = temps[m % len(temps)]
                    hg = bw[:, 3 + m % 2, :]
                    if m >= len(temps):
                        v.wait_ge(*(at("m_b", b, m - len(temps) + 1) if m - len(temps) < MG else at("hg", b, m - len(temps) + 1)))
                    v.scalar_tensor_tensor(t1, th, 1.0, h1, ALU.add, ALU.mult).then_inc(sem["m_a"], 1)
                    v.wait_ge(*at("m_a", b, m + 1))
                    if m < MG:
                        if m >= len(temps):
                            v.wait_ge(*at("hg", b, m - len(temps) + 1))
                        v.scalar_tensor_tensor(t2, t1, 0.5, h3, ALU.mult, ALU.mult).then_inc(sem["m_b"], 1)
                        yield T["moe"] + T["d_moe"] * m + T["l_hg"]
                        v.wait_ge(*at("gate", b, m + 1))
                        v.wait_ge(*at("m_b", b, m + 1))
                        if m >= 2:
                            v.wait_ge(*at("y2_part", b, m - 1))
                        v.tensor_tensor(hg, t2, ps[:, gate_bank, 0:L], ALU.mult).then_inc(sem["hg"], 1)
                    else:
                        if m >= 2:
                            v.wait_ge(*at("y2_part", b, m - 1))
                        v.scalar_tensor_tensor(hg, t1, 0.5, h3, ALU.mult, ALU.mult).then_inc(sem["hg"], 1)
                yield T["out"] + 2 * AFTER
                v.wait_ge(*at("y2", b, 1))
                v.wait_ge(*at("xc", b, 1))
                v.scalar_tensor_tensor(xo[:, :, :], b3x, tg[:, 3:4], xc[:, :, :], ALU.mult, ALU.add).then_inc(sem["xo"], 1)

            schedule(mamba, keys, attention, mixture, constants, rounded, centred)

        @block.tensor
        def _(pe):
            def transposes(src, dst, id_):
                for i in range(2):
                    for k in range(2):
                        last = pe.transpose(dst(i, k), src[:, i, k * P:k * P + P], id_)
                return last

            def mamba(b):
                yield T["start"]
                pe.wait_ge(ctx_in, b * 16 + 16)
                pe.wait_ge(*at("x1", b, 0))
                for e in range(2):
                    mm = pe.matmul(ps[:, 0, e * L:e * L + L], win[:, e * P:e * P + P], ctx[:, :], start=True, stop=True)
                mm.then_inc(sem["xi"], 1)
                yield T["xproj"]
                pe.wait_ge(*at("u", b, 1))
                for k in range(2):
                    mm = pe.matmul(ps[0:XR, 0, 0:L], wxp[:, k, :], u2[:, k, :], start=(k == 0), stop=(k == 1))
                mm.then_inc(sem["xdbl"], 1)
                yield T["dt"]
                pe.wait_ge(*at("bc_lo", b, 2))
                pe.wait_ge(*at("ys", b, 0))
                pe.wait_ge(once["setup"], 9)
                for e in range(2):
                    o = ps[:, 1, e * L:e * L + L]
                    pe.matmul(o, wdt_hi[64:XR, e * P:e * P + P], stack[64:XR, :], start=True, stop=False)
                    mm = pe.matmul(o, wdt_lo[64:72, e * P:e * P + P], stack[64:72, :], start=False, stop=True)
                mm.then_inc(sem["dt_pre"], 1)

                def spread(n):
                    if n:
                        pe.wait_ge(*at("c_sb", b, n))
                    for w in range(2):
                        r = w * NS + n
                        mm = pe.matmul(ps[:, 0, w * L:w * L + L], selBC[:, r:r + 1].to_broadcast([2 * BCR, P]), stack[0:2 * BCR, :], start=True, stop=True)
                    mm.then_inc(sem["bc"], 1)
                for n in range(NS + 2):
                    yield T["scan"] + T["d_scan"] * min(n, NS) + AFTER * max(n - NS, 0) - T["l_spread"]
                    if n < NS:
                        spread(n)
                    if n >= 3 and n % 2:
                        k = (n - 3) // 2
                        last = k == NS // 2 - 1
                        if b:
                            pe.wait_ge(*at("p_pair", b, k + 1))
                        else:
                            pe.wait_ge(*at("p", b, 2 * k + 2))
                            pe.matmul(ps[:, 1, :], ident, hb[:, 2 * k % 3].rearrange("p e l -> p (e l)"), start=(k == 0), stop=False)
                        pe.matmul(ps[:, 1, :], ident, hb[:, (2 * k + 1) % 3].rearrange("p e l -> p (e l)"), start=(b > 0 and k == 0), stop=last).then_inc(sem["y_red"], 1)
                yield T["y"] + AFTER
                pe.wait_ge(*at("yz", b, 1))
                for e in range(2):
                    for t in range(T2):
                        mm = pe.transpose(ps[:, 0, t * D + e * P:t * D + e * P + P], cv[:, e, t * P:t * P + P], ident)
                mm.then_inc(sem["yT"], 1)

            def stack_transposes(t, done):
                for j in range(HP):
                    src = st[:, t, 2 * j:2 * j + 2, :].rearrange("p h c -> p (h c)")
                    mm = pe.transpose(psR[:, 6 - 2 * t + j // 4, (j % 4) * P:(j % 4) * P + P], src, identR[:, :])
                mm.then_inc(sem[done], 1)

            def keys(b):
                yield T["kv"]
                pe.wait_ge(ctxR_in, b * 48 + 48)
                pe.wait_ge(*at("x3", b, 0))
                pe.wait_ge(once["later"], 16 * len(LATER))
                pe.wait_ge(once["centred"], 15)
                pe.matmul(ps[:, 4, :], ctxR[:, 0, :], wkv[:, :], start=True, stop=True)
                pe.matmul(ps[:, 5, :], ctxR[:, 1, :], wkv[:, :], start=True, stop=False)
                pe.matmul(ps[:, 5, :], ctxR[:, 2, :], wkvd[:, :], start=False, stop=True).then_inc(sem["kv_ps"], 1)
                yield T["kT"]
                pe.wait_ge(*at("kstack", b, 5))
                pe.wait_ge(*at("k_m", b, 1))
                pe.wait_ge(*at("vst", b, 3))
                for t in range(T2):
                    stack_transposes(t, "kT_ps")

            def xh_transposes(b, i):
                pe.wait_ge(*at("xh", b, 2 * i + 2))
                for t in range(T2):
                    for k in range(K2):
                        mm = pe.transpose(b7x[:, k, t * P:t * P + P], xh[:, t, k * P:k * P + P], ident)
                mm.then_inc(sem["xT_ps"], 1)

            def attention(b):
                yield T["xT0"]
                pe.wait_ge(*at("kT", b, 2))
                xh_transposes(b, 0)

                def down(m):
                    pe.wait_ge(*at("h_ff", b, m + 1))
                    for t in range(T2):
                        mm = pe.matmul(ps[:, 7, t * D:t * D + D], work[:, 4 + m, t * P:t * P + P], wdn[:, m, :],
                                       start=(m == 0 and t == 0), stop=(m == MF - 1), skip_group_check=True)
                    if m == MF - 1:
                        mm.then_inc(sem["down"], 1)
                if b == 0:
                    pe.wait_ge(once["q_out"], QUANT)
                for m in range(MF):
                    yield T["ffn"] + T["d_ffn"] * m
                    if m == 0:
                        pe.wait_ge(*at("x_lo", b, 1))
                    if m >= 3:
                        pe.wait_ge(*at("h_ff", b, m - 2))
                    for w in range(2):
                        o = ps[:, 4 + m % 3, w * L:w * L + L]
                        for k in range(K2):
                            pe.matmul(o, wgu[:, m, k, w, :], xhi[:, k, :], start=(k == 0), stop=False)
                        for k in range(K2):
                            mm = pe.matmul(o, wgu[:, m, k, w, :], xlo[:, k, :], start=False, stop=(k == K2 - 1))
                    mm.then_inc(sem["gu"], 1)
                    if m >= 2:
                        down(m - 2)
                yield T["down"]
                down(MF - 2)
                down(MF - 1)

                yield T["xT1"]
                pe.wait_ge(*at("dsc", b, 1))
                xh_transposes(b, 1)
                yield T["xT1"] + AFTER
                pe.wait_ge(*at("xT", b, 1))
                for t in range(T2):
                    for k in range(K2):
                        mm = pe.matmul(ps[:, 4, t * D:t * D + D], xT[:, k, t * P:t * P + P], wq[:, k, :], start=(k == 0), stop=(k == K2 - 1))
                mm.then_inc(sem["q_ps"], 1)
                yield T["qT"]
                pe.wait_ge(*at("q_hi2", b, 1))
                pe.wait_ge(*at("qstack", b, 4))
                for t in range(T2):
                    stack_transposes(t, "qT_ps")

                def rows_of(t_, h, n):
                    return t_[64 * (h % 2):64 * (h % 2) + n, h // 2, :]
                for i in range(8):
                    yield T["scores"] + T["d_scores"] * i
                    t, hg = i // 4, i % 4
                    if i == 0:
                        pe.wait_ge(*at("qT", b, 2))
                    if i >= 2:
                        pe.wait_ge(*at("mx", b, 2 * (i - 1)))
                    for h in range(4):
                        hh = 4 * hg + h
                        mm = pe.matmul(ps[:, 4 + 2 * (i % 2) + h % 2, (h // 2) * L:(h // 2) * L + L],
                                       rows_of(qT, hh, 3 * HD)[:, t * P:t * P + P], rows_of(kT, hh, 3 * HD), start=True, stop=True)
                    mm.then_inc(sem["s_ps"], 1)
                yield T["m"] + AFTER / 2
                pe.wait_ge(*at("mstack", b, 2))
                for t in range(T2):
                    stack_transposes(t, "qT_ps")
                for h in range(H + 3):
                    yield T["heads"] + T["d_heads"] * h
                    if h == 0:
                        pe.wait_ge(*at("qT", b, 4))
                    if h < H:
                        if h >= 2:
                            pe.wait_ge(*at("prob", b, h - 1))
                        for kt in range(T2):
                            mm = pe.matmul(ps[:, 4 + h % 2, kt * L:kt * L + L], rows_of(kT, h, 3 * HD + 4)[:, kt * P:kt * P + P],
                                           rows_of(qT, h, 3 * HD + 4), start=True, stop=True)
                        mm.then_inc(sem["st_ps"], 1)
                    if 2 <= h < H + 2:
                        g = h - 2
                        pe.wait_ge(*at("prob", b, g + 1))
                        if g >= 4 and g % 2 == 0:
                            pe.wait_ge(*at("o_step", b, g - 2))
                        for kt in range(T2):
                            mm = pe.matmul(ps[64 * (g % 2):64 * (g % 2) + 64, 6 + g // 2 % 2, 0:L], vst[:, kt, VW * g:VW * g + 64],
                                           work[:, 2 * (g % 4) + kt, :], start=(kt == 0), stop=(kt == 1))
                        mm.then_inc(sem["pv"], 1)
                    if h >= 4 and h % 2 == 0:
                        j = (h - 4) // 2
                        pe.wait_ge(*at("o_sb", b, j + 1))
                        for t in range(T2):
                            mm = pe.transpose(ps[:, 6 + j % 2, L + t * P:L + t * P + P], work[:, 8 + j % 2, t * P:t * P + P], ident)
                        mm.then_inc(sem["oT_ps"], 1)
                yield T["wo"]
                if b == 0:
                    pe.wait_ge(once["last"], 16 * len(LAST))
                pe.wait_ge(*at("ctok", b, HP))
                for t in range(T2):
                    for k in range(K2):
                        mm = pe.transpose(ps[:, 4, k * L + t * P:k * L + t * P + P], ctok[:, t, 8 * k:8 * k + 8, :].rearrange("p h c -> p (h c)"), ident)
                mm.then_inc(sem["cT_ps"], 1)
                yield T["wo"] + 1.5 * AFTER
                pe.wait_ge(*at("cT", b, 1))
                for t in range(T2):
                    for k in range(K2):
                        mm = pe.matmul(ps[:, 5, t * D:t * D + D], xT[:, k, t * P:t * P + P], wo[:, k, :], start=(k == 0), stop=(k == K2 - 1))
                mm.then_inc(sem["wo_ps"], 1)

            def mixture(b):
                yield T["bxT"]
                pe.wait_ge(*at("xo", b, 0))
                pe.wait_ge(*at("bxh", b, 2))
                for t in range(T2):
                    for k in range(K2):
                        mm = pe.transpose(b3x[:, k, t * P:t * P + P], bxh[:, t, k * P:k * P + P], ident)
                mm.then_inc(sem["bT_ps"], 1)
                yield T["bxT"] + 1.5 * AFTER
                pe.wait_ge(*at("bT", b, 1))
                for t in range(T2):
                    for k in range(K2):
                        mm = pe.matmul(ps[:, 2, t * E:t * E + E], bT[:, k, t * P:t * P + P], wgate[:, k, :], start=(k == 0), stop=(k == K2 - 1))
                mm.then_inc(sem["lg"], 1)
                yield T["gT"]
                pe.wait_ge(*at("lg_tanh", b, 1))
                pe.wait_ge(*at("gates", b, 2))
                for t in range(T2):
                    mm = pe.transpose(psR[0:2 * E, 2, t * P:t * P + P], gst[:, t, :], identR[:, :])
                mm.then_inc(sem["gT_ps"], 1)
                yield T["moe"] - AFTER / 4
                pe.wait_ge(*at("gT", b, 1))
                pe.wait_ge(*at("b_lo", b, 1))
                if b == 0:
                    pe.wait_ge(once["raw_lo"], MM)
                hidden_banks, gate_bank, temps = place(b)
                if b == B - 2:
                    pe.wait_ge(*at("x1", B - 1, 1))

                def second(m):
                    pe.wait_ge(*at("hg", b, m + 1))
                    for t in range(T2):
                        mm = pe.matmul(ps[:, 3, t * D:t * D + D], bw[:, 3 + m % 2, t * P:t * P + P], w2s[:, m, :],
                                       start=(m == 0 and t == 0), stop=(m == MM - 1), skip_group_check=True)
                    mm.then_inc(sem["y2" if m == MM - 1 else "y2_part"], 1)
                for m in range(MM):
                    yield T["moe"] + T["d_moe"] * m
                    hidden_bank = hidden_banks[m % len(hidden_banks)]
                    if m >= len(hidden_banks):
                        pe.wait_ge(*at("hg", b, m - len(hidden_banks) + 1))
                    for w in range(2):
                        o = ps[:, hidden_bank, w * L:w * L + L]
                        for k in range(K2):
                            pe.matmul(o, w13_hi[:, m, k, w, :], bhi[:, k, :], start=(k == 0), stop=False)
                            pe.matmul(o, w13_hi[:, m, k, w, :], blo[:, k, :], start=False, stop=False)
                            mm = pe.matmul(o, w13_lo[:, m, k, w, :], bhi[:, k, :], start=False, stop=(k == K2 - 1))
                    mm.then_inc(sem["h13"], 1)
                    if m >= 2:
                        second(m - 2)
                    if m < MG:
                        yield T["moe"] + T["d_moe"] * m + T["l_gate"]
                        if gate_bank == hidden_bank:
                            pe.wait_ge(*at("m_b", b, m + 1))
                        elif m:
                            pe.wait_ge(*at("hg", b, m))
                        pe.matmul(ps[:, gate_bank, 0:L], gselR[:, m, :], gT[:, :], start=True, stop=True).then_inc(sem["gate"], 1)
                yield T["out"]
                second(MM - 2)
                second(MM - 1)

            start_at_one(pe, 3)
            pe.wait_ge(once["early"], 16 * len(EARLY))
            pe.wait_ge(once["ident_r"], 3)
            schedule(mamba, keys, attention, mixture)


def by_k(w):
    k, n = w.shape
    return w.reshape(k // P, P, n).transpose(1, 0, 2)


def kernel(**inputs):
    import numpy as np
    import concourse.bacc as bacc
    from concourse.bass_utils import run_bass_kernel_spmd

    a = {k: np.asarray(v) for k, v in inputs.items()}
    m = {k[len("L0_xattn_"):]: v for k, v in a.items() if k.startswith("L0_xattn_")}
    f = {k[len("L0_ffn_"):]: v for k, v in a.items() if k.startswith("L0_ffn_")}
    q = {k[len("L1_xattn_"):]: v for k, v in a.items() if k.startswith("L1_xattn_")}
    e = {k[len("L1_ffn_"):]: v for k, v in a.items() if k.startswith("L1_ffn_")}
    z = lambda *s: np.zeros(s, np.float32)

    xp = m["x_proj_w"].T
    wxp = z(D, XR)
    wxp[:, 0:BCR] = wxp[:, BCR:2 * BCR] = xp[:, DTR:]
    wxp[:, 64:64 + DTR] = wxp[:, 96:96 + DTR] = xp[:, :DTR]
    wdt = z(P, D)
    wdt[64:64 + DTR] = wdt[96:96 + DTR] = m["dt_proj_w"].T

    gu = np.stack([by_k(f["gate_w"]), by_k(f["up_w"])], 2)
    gu = gu.reshape(P, K2, 2, MF, P).transpose(0, 3, 1, 2, 4).reshape(P, MF, 512)
    w1, w3, w2 = z(D, MM * P), z(D, MM * P), z(MM * P, D)
    w1[:, :HID] = np.concatenate([e["W1"].transpose(1, 0, 2).reshape(D, E * INTER), e["sw1"].T], 1)
    w3[:, :HID] = np.concatenate([e["W3"].transpose(1, 0, 2).reshape(D, E * INTER), e["sw3"].T], 1)
    w2[:HID] = np.concatenate([e["W2"].reshape(E * INTER, D), e["sw2"].T], 0)
    w13 = np.stack([by_k(w1), by_k(w3)], 2).reshape(P, K2, 2, MM, P).transpose(0, 3, 1, 2, 4).reshape(P, MM, 512)

    def heads(k, v):
        return np.stack([k.reshape(-1, H, HD), v.reshape(-1, H, HD)], 2).reshape(-1, 2 * D)

    def heads_apart(c):
        return c.reshape(H, 2, HD).transpose(1, 0, 2).reshape(2, D)
    wkv = np.concatenate([q["Wk"], q["Wv"]], 1)
    wkvd = heads(q["Wkv_dca"][:, :D], q["Wkv_dca"][:, D:])
    kvb = z(P, 5, D)
    hb = heads_apart(np.concatenate([q["bk"], q["bv"]]))
    kvb[:, 0:2], kvb[:, 2:4] = hb[0], hb[1]
    kvb[MAIN - P:, 1], kvb[MAIN - P:, 3], kvb[MAIN - P:, 4] = q["bkv_dca"][:D], 0.0, q["bkv_dca"][D:]

    vecs = z(P, V_N)
    for i in range(2):
        s = slice(i * P, i * P + P)
        vecs[:, V_CW + 4 * i:V_CW + 4 * i + 4] = m["conv_w"][s, 0]
        vecs[:, V_CB + i] = m["conv_b"][s]
        vecs[:, V_DTB + i] = m["dt_proj_b"][s]
        vecs[:, V_AL + NS * i:V_AL + NS * i + NS] = m["A_log"][s]
        vecs[:, V_D + i] = m["D"][s]
    vecs[:, V_GS:V_GS + MF] = f["gate_scale"].reshape(MF, P).T
    vecs[:, V_US:V_US + MF] = f["up_scale"].reshape(MF, P).T
    vecs[:MAIN - P, V_MM] = 1.0
    vecs[MAIN - P:, V_MM + 1] = 1.0
    rows = z(P, R_N)
    rows[:, R_DS:R_DS + D] = f["down_scale"]
    rows[:, R_BQ:R_BQ + D] = q["bq"]
    rows[:, R_BO:R_BO + D] = q["bo"]
    rows[:, R_QW:R_QW + HD] = q["qn_w"]
    rows[:, R_QB:R_QB + HD] = q["qn_b"]
    rows[:, R_RB:R_RB + E] = e["router_bias"]
    for c, w, wd in ((R_KW, "kn_w", "kn_dca_w"), (R_KB, "kn_b", "kn_dca_b")):
        rows[:, c:c + HD] = rows[:, c + HD:c + 2 * HD] = q[w]
        rows[MAIN - P:, c + HD:c + 2 * HD] = q[wd]
    rows[:, R_G] = a["g_xattn"][0]
    rows[:, R_G + 1] = a["g_xattn"][1]
    rows[:, R_G + 2] = a["g_ffn"][0]
    rows[:, R_G + 3] = a["g_ffn"][1]
    rows[:, R_KM:R_KM + 8] = [-1, -1, 0, 0] * 2
    rows[MAIN - P:, R_KM + 4:R_KM + 8] = [0, 0, -1, -1]
    rows[:, R_TR:R_TR + E * E] = np.tril(np.ones((E, E), np.float32), -1).ravel()
    gsel = z(2 * E, MG * P)
    for i in range(E):
        gsel[i, i * INTER:(i + 1) * INTER] = gsel[E + i, i * INTER:(i + 1) * INTER] = 1.0
    cst = z(P, P + BCR)
    cst[:, :P] = np.eye(P)
    for i in range(2 * BCR):
        cst[i, P + i % BCR] = 1.0

    arrays = dict(
        x=a["x"], ctxT=a["ctx_1024"].transpose(0, 2, 1), w_in=m["in_proj_w"].T, w_xp=by_k(wxp), w_dt=wdt,
        w_gu=gu, w_dn=by_k(f["down_w"]).reshape(P, MF * D), w_q=by_k(q["Wq"]), w_kv=wkv, w_kvd=wkvd,
        w_o=by_k(q["Wo"]), w_gate=by_k(e["gate_w"].T), w13=w13, w2=by_k(w2), kvb=kvb, vecs=vecs, rows=rows,
        gsel=gsel, cst=cst,
    )
    nc = bacc.Bacc("TRN2", target_bir_lowering=False, num_devices=1)
    aps = {}
    for name, arr in arrays.items():
        arrays[name] = arr = np.ascontiguousarray(arr)
        aps[name] = nc.dram_tensor(f"in_{name}", arr.shape, F32, kind="ExternalInput").ap()
    out = nc.dram_tensor("out", (B, L, D), F32, kind="ExternalOutput").ap()
    build(nc, out=out, **aps)
    r = run_bass_kernel_spmd(nc, [{f"in_{k}": v for k, v in arrays.items()}], core_ids=[0])
    return r.results[0]["out"]
```
